# Optimizing a Trainium2 kernel written in Bass

```python
import numpy as np
import jax
import jax.numpy as jnp

def _softmax(x, axis=-1):
    return jax.nn.softmax(x, axis=axis)

def _gelu(x):
    return jax.nn.gelu(x, approximate=True)

def _silu(x):
    return jax.nn.silu(x)

def _sigmoid(x):
    return jax.nn.sigmoid(x)

def _layernorm(x, axis=-1, eps=1e-05):
    m = jnp.mean(x, axis=axis, keepdims=True)
    v = jnp.var(x, axis=axis, keepdims=True)
    return (x - m) / jnp.sqrt(v + eps)

def _scatter_add(tgt, idx, src, axis=0):
    return tgt.at[idx].add(src)

def _segment_sum(src, seg, n):
    return jax.ops.segment_sum(src, seg, n)
kernel_name = 'mk_gnn_preln_d4_gnn_r64_33214a'

def setup_inputs(seed: int=0):
    np.random.seed(seed)
    _w = jnp.asarray

    def _rec_inputs():
        import jax
        import jax.numpy as jnp
        _gk = jax.random.key(seed)
        x = -0.0003713 + 1 * jax.random.normal(jax.random.fold_in(_gk, 1), (100000, 128), jnp.float32)
        src = jax.random.randint(jax.random.fold_in(_gk, 2), (25000,), 0, 100000, jnp.int32)
        dst = jnp.minimum((100000 * jax.random.uniform(jax.random.fold_in(_gk, 3), (25000,)) ** 2.0).astype(jnp.int32), 99999)
        _o = jnp.argsort(dst, stable=True)
        src = src[_o]
        dst = dst[_o]
        edge_attr_4 = -0.00166765 + 0.999426 * jax.random.normal(jax.random.fold_in(_gk, 12), (25000, 4), jnp.float32)
        edge_attr_8 = -0.00016606 + 0.999594 * jax.random.normal(jax.random.fold_in(_gk, 13), (25000, 8), jnp.float32)
        edge_type_8 = jax.random.randint(jax.random.fold_in(_gk, 15), (25000,), 0, 8, jnp.int32)
        edge_weight = jax.random.uniform(jax.random.fold_in(_gk, 16), (25000,), jnp.float32, 0.0, 1)
        node_vec1 = 0.00192408 + 1.00201 * jax.random.normal(jax.random.fold_in(_gk, 17), (100000, 1), jnp.float32)
        node_vec1_n2 = 0.00192408 + 1.00201 * jax.random.normal(jax.random.fold_in(_gk, 18), (100000, 1), jnp.float32)
        return (x, src, dst, edge_attr_4, edge_attr_8, edge_type_8, edge_weight, node_vec1, node_vec1_n2)
    x, src, dst, edge_attr_4, edge_attr_8, edge_type_8, edge_weight, node_vec1, node_vec1_n2 = _rec_inputs()

    def _L0_gnn_setup():
        import jax, jax.numpy as jnp
        import numpy as np
        N_NODES = 100000
        N_EDGES = 50000
        D_IN = 128
        D_OUT = 128
        key = jax.random.key(seed)
        k1, k2, k3, k4, k5, k6 = jax.random.split(key, 6)
        inputs = jax.random.normal(k1, (N_NODES, D_IN), dtype=jnp.float32)
        edge_row = jax.random.randint(k2, (N_EDGES,), 0, N_NODES, dtype=jnp.int32)
        edge_col = jax.random.randint(k3, (N_EDGES,), 0, N_NODES, dtype=jnp.int32)
        edge_weight = jax.random.uniform(k4, (N_EDGES,), dtype=jnp.float32)
        limit = float(np.sqrt(6.0 / (D_IN + D_OUT)))
        weight = jax.random.uniform(k5, (D_IN, D_OUT), minval=-limit, maxval=limit, dtype=jnp.float32)
        bias = jnp.zeros((D_OUT,), dtype=jnp.float32)
        return {'inputs': inputs, 'edge_row': edge_row, 'edge_col': edge_col, 'edge_weight': edge_weight, 'weight': weight, 'bias': bias}
    _L0_gnn_all = _L0_gnn_setup()
    _L0_gnn_in = {k: v for k, v in _L0_gnn_all.items() if k in ('weight', 'bias')}
    del _L0_gnn_all

    def _L1_gnn_setup():
        import jax, jax.numpy as jnp
        import numpy as np
        N = 100000
        E = 25000
        D = 128
        H = 4
        C = D // H

        def leaky(x, slope):
            return jnp.where(x >= 0, x, slope * x)
        key = jax.random.key(seed)
        ks = jax.random.split(key, 12)
        s = 1.0 / np.sqrt(D)
        return {'x': jax.random.normal(ks[0], (N, D), jnp.float32), 'edge_index': jax.random.randint(ks[1], (2, E), 0, N, jnp.int32), 'edge_type': jax.random.randint(ks[2], (E,), 0, 8, jnp.int32), 'W1': jax.random.normal(ks[3], (D, D), jnp.float32) * s, 'b1': jnp.zeros((D,), jnp.float32), 'Wg': jax.random.normal(ks[4], (D, D), jnp.float32) * s, 'att_src': jax.random.normal(ks[5], (1, H, C), jnp.float32) * s, 'att_dst': jax.random.normal(ks[6], (1, H, C), jnp.float32) * s, 'bias_g': jnp.zeros((D,), jnp.float32), 'W2': jax.random.normal(ks[7], (D, D), jnp.float32) * s, 'b2': jnp.zeros((D,), jnp.float32)}
    _L1_gnn_all = _L1_gnn_setup()
    _L1_gnn_in = {k: v for k, v in _L1_gnn_all.items() if k in ('W1', 'b1', 'Wg', 'att_src', 'att_dst', 'bias_g', 'W2', 'b2')}
    del _L1_gnn_all

    def _L2_gnn_setup():
        import jax, jax.numpy as jnp
        import numpy as np
        from jax.ops import segment_sum
        N = 100000
        M = 20000
        E = 25000
        D_IN = 128
        D_OUT = 128
        key = jax.random.key(seed)
        k1, k2, k3, k4, k5, k6 = jax.random.split(key, 6)
        x = jax.random.normal(k1, (N, D_IN), dtype=jnp.float32)
        node_idx = jax.random.randint(k2, (E,), 0, N)
        he_idx = jax.random.randint(k3, (E,), 0, M)
        hyperedge_index = jnp.stack([node_idx, he_idx], axis=0)
        hyperedge_weight = jax.random.uniform(k4, (M,), dtype=jnp.float32)
        W = jax.random.normal(k5, (D_OUT, D_IN), dtype=jnp.float32) / np.sqrt(D_IN)
        b = jax.random.normal(k6, (D_OUT,), dtype=jnp.float32) * 0.01
        return {'x': x, 'hyperedge_index': hyperedge_index, 'hyperedge_weight': hyperedge_weight, 'W': W, 'b': b}
    _L2_gnn_all = _L2_gnn_setup()
    _L2_gnn_in = {k: v for k, v in _L2_gnn_all.items() if k in ('hyperedge_weight', 'W', 'b')}
    del _L2_gnn_all

    def _L3_gnn_setup():
        import jax, jax.numpy as jnp
        import numpy as np
        N = 25000
        E = 6250
        MUL = 32
        NSC = 8
        HID = 64
        WNUM = 4 * MUL
        NUM_NEIGH = 16.0
        INV_SQRT3 = 1.0 / np.sqrt(3.0)
        key = jax.random.key(seed)
        ks = jax.random.split(key, 13)
        return {'node_input': jax.random.normal(ks[0], (N, 4 * MUL), jnp.float32), 'node_attr_input': jax.random.normal(ks[1], (N, 1), jnp.float32), 'node_attr_output': jax.random.normal(ks[2], (N, 1), jnp.float32), 'edge_src': jax.random.randint(ks[3], (E,), 0, N), 'edge_dst': jax.random.randint(ks[4], (E,), 0, N), 'edge_attr': jax.random.normal(ks[5], (E, 4), jnp.float32), 'edge_scalar_attr': jax.random.normal(ks[6], (E, NSC), jnp.float32), 'w1_s': jax.random.normal(ks[7], (MUL, MUL), jnp.float32), 'w1_v': jax.random.normal(ks[8], (MUL, MUL), jnp.float32), 'Wfc1': jax.random.normal(ks[9], (NSC, HID), jnp.float32), 'Wfc2': jax.random.normal(ks[10], (HID, WNUM), jnp.float32), 'w2_s': jax.random.normal(ks[11], (2, MUL, MUL), jnp.float32), 'w2_v': jax.random.normal(ks[12], (2, MUL, MUL), jnp.float32)}
    _L3_gnn_all = _L3_gnn_setup()
    _L3_gnn_in = {k: v for k, v in _L3_gnn_all.items() if k in ('w1_s', 'w1_v', 'Wfc1', 'Wfc2', 'w2_s', 'w2_v')}
    del _L3_gnn_all
    return {'x': x, 'src': src, 'dst': dst, 'edge_attr_4': edge_attr_4, 'edge_attr_8': edge_attr_8, 'edge_type_8': edge_type_8, 'edge_weight': edge_weight, 'node_vec1': node_vec1, 'node_vec1_n2': node_vec1_n2, 'L0_gnn_weight': _L0_gnn_in['weight'], 'L0_gnn_bias': _L0_gnn_in['bias'], 'L1_gnn_W1': _L1_gnn_in['W1'], 'L1_gnn_b1': _L1_gnn_in['b1'], 'L1_gnn_Wg': _L1_gnn_in['Wg'], 'L1_gnn_att_src': _L1_gnn_in['att_src'], 'L1_gnn_att_dst': _L1_gnn_in['att_dst'], 'L1_gnn_bias_g': _L1_gnn_in['bias_g'], 'L1_gnn_W2': _L1_gnn_in['W2'], 'L1_gnn_b2': _L1_gnn_in['b2'], 'L2_gnn_hyperedge_weight': _L2_gnn_in['hyperedge_weight'], 'L2_gnn_W': _L2_gnn_in['W'], 'L2_gnn_b': _L2_gnn_in['b'], 'L3_gnn_w1_s': _L3_gnn_in['w1_s'], 'L3_gnn_w1_v': _L3_gnn_in['w1_v'], 'L3_gnn_Wfc1': _L3_gnn_in['Wfc1'], 'L3_gnn_Wfc2': _L3_gnn_in['Wfc2'], 'L3_gnn_w2_s': _L3_gnn_in['w2_s'], 'L3_gnn_w2_v': _L3_gnn_in['w2_v']}

def reference(x, src, dst, edge_attr_4, edge_attr_8, edge_type_8, edge_weight, node_vec1, node_vec1_n2, L0_gnn_weight, L0_gnn_bias, L1_gnn_W1, L1_gnn_b1, L1_gnn_Wg, L1_gnn_att_src, L1_gnn_att_dst, L1_gnn_bias_g, L1_gnn_W2, L1_gnn_b2, L2_gnn_hyperedge_weight, L2_gnn_W, L2_gnn_b, L3_gnn_w1_s, L3_gnn_w1_v, L3_gnn_Wfc1, L3_gnn_Wfc2, L3_gnn_w2_s, L3_gnn_w2_v):
    import jax
    import jax.numpy as jnp

    def _L0_gnn_ref(inputs, edge_row, edge_col, edge_weight, weight, bias):
        import jax, jax.numpy as jnp
        import numpy as np
        N_NODES = 100000
        N_EDGES = 50000
        D_IN = 128
        D_OUT = 128
        support = inputs @ weight
        messages = edge_weight[:, None] * support[edge_col]
        out = jax.ops.segment_sum(messages, edge_row, num_segments=N_NODES)
        return out + bias

    def _L1_gnn_ref(x, edge_index, edge_type, W1, b1, Wg, att_src, att_dst, bias_g, W2, b2):
        import jax, jax.numpy as jnp
        import numpy as np
        N = 100000
        E = 25000
        D = 128
        H = 4
        C = D // H

        def leaky(x, slope):
            return jnp.where(x >= 0, x, slope * x)
        x = leaky(x, 0.01) @ W1.T + b1
        h = (x @ Wg.T).reshape(N, H, C)
        a_src = jnp.sum(h * att_src, axis=-1)
        a_dst = jnp.sum(h * att_dst, axis=-1)
        src, dst = (edge_index[0], edge_index[1])
        alpha = leaky(a_src[src] + a_dst[dst], 0.2)
        amax = jax.ops.segment_max(alpha, dst, num_segments=N)
        amax = jnp.where(jnp.isfinite(amax), amax, 0.0)
        ex = jnp.exp(alpha - amax[dst])
        denom = jax.ops.segment_sum(ex, dst, num_segments=N)
        coeff = ex / (denom[dst] + 1e-16)
        msg = h[src] * coeff[:, :, None]
        out = jax.ops.segment_sum(msg, dst, num_segments=N)
        out = out.reshape(N, H * C) + bias_g
        out = leaky(out, 0.01) @ W2.T + b2
        return out

    def _L2_gnn_ref(x, hyperedge_index, hyperedge_weight, W, b):
        import jax, jax.numpy as jnp
        import numpy as np
        from jax.ops import segment_sum
        N = 100000
        M = 20000
        E = 25000
        D_IN = 128
        D_OUT = 128
        node_idx = hyperedge_index[0]
        he_idx = hyperedge_index[1]
        num_nodes = x.shape[0]
        num_he = hyperedge_weight.shape[0]
        d_e = segment_sum(jnp.ones_like(he_idx, dtype=x.dtype), he_idx, num_segments=num_he)
        d_e = jnp.clip(d_e, 1.0, None)
        d_v = segment_sum(hyperedge_weight[he_idx], node_idx, num_segments=num_nodes)
        d_v = jnp.clip(d_v, 1.0, None)
        d_v_inv_sqrt = d_v ** (-0.5)
        x_prime = x * d_v_inv_sqrt[:, None]
        he_feat = segment_sum(x_prime[node_idx], he_idx, num_segments=num_he)
        he_feat = he_feat * (hyperedge_weight / d_e)[:, None]
        out = segment_sum(he_feat[he_idx], node_idx, num_segments=num_nodes)
        out = out * d_v_inv_sqrt[:, None]
        return out @ W.T + b

    def _L3_gnn_ref(node_input, node_attr_input, node_attr_output, edge_src, edge_dst, edge_attr, edge_scalar_attr, w1_s, w1_v, Wfc1, Wfc2, w2_s, w2_v):
        import jax, jax.numpy as jnp
        import numpy as np
        N = 25000
        E = 6250
        MUL = 32
        NSC = 8
        HID = 64
        WNUM = 4 * MUL
        NUM_NEIGH = 16.0
        INV_SQRT3 = 1.0 / np.sqrt(3.0)
        n = node_input.shape[0]
        xs = node_input[:, :MUL]
        xv = node_input[:, MUL:].reshape(n, MUL, 3)
        a = node_attr_input[:, 0]
        inv1 = 1.0 / np.sqrt(MUL * 1.0)
        xs1 = jnp.einsum('nu,n,uw->nw', xs, a, w1_s) * inv1
        xv1 = jnp.einsum('nui,n,uw->nwi', xv, a, w1_v) * inv1
        h = jax.nn.silu(edge_scalar_attr @ Wfc1 * (1.0 / np.sqrt(NSC)))
        w = (h @ Wfc2 * (1.0 / np.sqrt(HID))).reshape(-1, 4, MUL)
        es = xs1[edge_src]
        ev = xv1[edge_src]
        ys = edge_attr[:, 0]
        yv = edge_attr[:, 1:4]
        m0 = w[:, 0] * es * ys[:, None]
        m3 = w[:, 3] * jnp.einsum('eui,ei->eu', ev, yv) * INV_SQRT3
        m1 = w[:, 1][:, :, None] * es[:, :, None] * yv[:, None, :]
        m2 = w[:, 2][:, :, None] * ev * ys[:, None, None]
        ne = m0.shape[0]
        edge_features = jnp.concatenate([m0, m3, m1.reshape(ne, 3 * MUL), m2.reshape(ne, 3 * MUL)], axis=1)
        mid = jax.ops.segment_sum(edge_features, edge_dst, num_segments=n)
        mid = mid / np.sqrt(NUM_NEIGH)
        b = node_attr_output[:, 0]
        inv2 = 1.0 / np.sqrt(2.0 * MUL)
        s0 = mid[:, :MUL]
        s1 = mid[:, MUL:2 * MUL]
        v1 = mid[:, 2 * MUL:2 * MUL + 3 * MUL].reshape(n, MUL, 3)
        v2 = mid[:, 2 * MUL + 3 * MUL:].reshape(n, MUL, 3)
        out_s = (jnp.einsum('nu,n,uw->nw', s0, b, w2_s[0]) + jnp.einsum('nu,n,uw->nw', s1, b, w2_s[1])) * inv2
        out_v = (jnp.einsum('nui,n,uw->nwi', v1, b, w2_v[0]) + jnp.einsum('nui,n,uw->nwi', v2, b, w2_v[1])) * inv2
        return jnp.concatenate([out_s, out_v.reshape(n, 3 * MUL)], axis=1)
    edge_index = jnp.stack([src, dst])
    h = jnp.maximum(_layernorm(x, axis=-1), 0.0)
    x = x + _L0_gnn_ref(h, src, dst, edge_weight, L0_gnn_weight, L0_gnn_bias)
    h = jnp.maximum(_layernorm(x, axis=-1), 0.0)
    x = x + _L1_gnn_ref(h, edge_index, edge_type_8, L1_gnn_W1, L1_gnn_b1, L1_gnn_Wg, L1_gnn_att_src, L1_gnn_att_dst, L1_gnn_bias_g, L1_gnn_W2, L1_gnn_b2)
    h = jnp.maximum(_layernorm(x, axis=-1), 0.0)
    x = x + _L2_gnn_ref(h, edge_index, L2_gnn_hyperedge_weight, L2_gnn_W, L2_gnn_b)
    h = jnp.maximum(_layernorm(x, axis=-1), 0.0)
    x = x + _L3_gnn_ref(h, node_vec1, node_vec1_n2, src, dst, edge_attr_4, edge_attr_8, L3_gnn_w1_s, L3_gnn_w1_v, L3_gnn_Wfc1, L3_gnn_Wfc2, L3_gnn_w2_s, L3_gnn_w2_v)
    return x

_drawn_inputs = setup_inputs


def setup_inputs(seed=0):
    import zlib

    import numpy as np

    out = dict(_drawn_inputs(seed))
    spreads = {'L0_gnn_bias': (0.0, 0.1),
     'L1_gnn_b1': (0.0, 0.282),
     'L1_gnn_bias_g': (0.0, 0.1),
     'L1_gnn_b2': (0.0, 0.1)}
    factors = {'L1_gnn_att_src': 7.991, 'L1_gnn_att_dst': 8.0, 'L2_gnn_b': 5.152}
    for name, (base, spread) in spreads.items():
        noise = np.random.default_rng([zlib.crc32(name.encode()), seed]).standard_normal(out[name].shape)
        drawn = base * np.exp(spread * noise) if base else spread * noise
        out[name] = jnp.asarray(drawn.astype(out[name].dtype))
    for name, factor in factors.items():
        out[name] = (out[name] * factor).astype(out[name].dtype)
    return out
```

```python
import math
from contextlib import ExitStack

import concourse.bass as bass
from concourse import mybir

N, E, D = 100000, 25000, 128
M = 20000
H, C = 4, 32
MUL, NSC, HID = 32, 8, 64
P = 128
TILES = math.ceil(E / P)
EP = TILES * P
F = 256
LANES = EP // F
GROUP = 4
NG = TILES // GROUP
GE = GROUP * P
ROW = 132
COL_A, COL_B, COL_HW, COL_DV = 128, 129, 130, 131
SPARE = 2 * GROUP * P
TABLE = N + 1 + SPARE
REC = 16
R_SRC, R_DST, R_W, R_LAST, R_A4, R_A8 = 0, 1, 2, 3, 4, 8
LOG = 15
MID = N // 2
LEAST = 256
BIG_NUM = 1.0e30
EPS = 1e-5
PER_LANE = N // P
CHUNK = 11
NCHUNK = PER_LANE // CHUNK
LEFT = N - PER_LANE * P
DBUF = 3
SIGN = -2147483648

fp32 = mybir.dt.float32
i32 = mybir.dt.int32


class Group:

    def __init__(self, g, use, slot):
        self.g, self.use, self.slot = g, use, slot

    def before(self, n=1):
        out = self
        for _ in range(n):
            out = Group(out.g - 1, out.use - (1 if out.slot == 0 else 0), 1 - out.slot)
        return out

    def from_(self, n):
        return not isinstance(self.g, int) or self.g >= n


def counted(G, again):
    if not again:
        return G
    return Group(G.g + NG, G.use + len(range(G.slot, NG, 2)), G.slot)


class Order:

    def __init__(self, eng, sem):
        self.eng, self.sem, self.base, self.off = eng, sem, 0, 0

    def done(self, ins):
        self.off += 1
        ins.then_inc(self.sem, 1)
        return self.off

    def need(self, at):
        self.eng.wait_ge(self.sem, self.base + at)

    def link(self, ins):
        self.need(self.done(ins))


def for_groups(eng, body, order=None, peel=2):
    steady = 0
    for g in range(peel):
        start = order.off if order else 0
        body(Group(g, g // 2, g % 2))
        steady = order.off - start if order else 0
    first = order.off if order else 0
    with eng.Fori(peel // 2, NG // 2) as i:
        if order:
            order.base = i * (2 * steady) - (peel // 2) * 2 * steady
            order.off = first
        for s in range(2):
            body(Group(i * 2 + s, i, s))
        if order:
            assert order.off == first + 2 * steady, (order.off, first, steady)
    if order:
        order.base, order.off = 0, first + (NG // 2 - peel // 2) * 2 * steady
    body(Group(NG - 1, (NG - 1) // 2, 0))


def build_gnn(nc, x, src, dst, edge_attr_4, edge_attr_8, edge_weight, node_vec1, node_vec1_n2,
              L0_W, L0_b, W1, b1, Wg, att_src, att_dst, bias_g, W2, b2, hw, L2_W, L2_b,
              w1_s, w1_v, Wfc1, Wfc2, w2_s, w2_v, table):
    ALU = mybir.AluOpType
    ACT = mybir.ActivationFunctionType
    AX = mybir.AxisListType

    rec_raw = nc.dram_tensor("rec_raw", (EP, REC), fp32).ap()
    rec_d = nc.dram_tensor("rec_d", (EP, REC), fp32).ap()
    keys_dram = {k: nc.dram_tensor(f"keys_{k}", (EP + 2,), fp32).ap() for k in ("dst", "clip", "src")}
    he_dram = nc.dram_tensor("he", (EP, D), fp32).ap()
    w_dram = nc.dram_tensor("edge_w", (P, TILES * D), fp32).ap()

    ctx = ExitStack()
    with ctx:
        def sb(name, shape, dt=fp32):
            return ctx.enter_context(nc.sbuf_tensor(name, shape, dt))

        def sem(name):
            return ctx.enter_context(nc.semaphore(name))

        bank = [ctx.enter_context(nc.psum_tensor(f"bank{k}", [P, 512], fp32)) for k in range(8)]

        big = sb("big", [P, TILES * ROW])
        work = sb("work", [P, 14000])
        rec = sb("rec", [P, TILES * REC])
        rec_s = sb("rec_s", [P, TILES * 4])
        sc_s = sb("sc_s", [P, TILES * 4])
        sc_d = sb("sc_d", [P, TILES * 4])
        al = sb("al", [P, TILES * H])
        key_col = {k: sb(f"key_{k}", [P, TILES]) for k in ("dst", "clip", "src")}
        cnt_col = sb("cnt_col", [P, TILES])
        wt_col = sb("wt_col", [P, TILES])
        hsc_col = sb("hsc_col", [P, TILES])
        dvis_s = sb("dvis_s", [P, TILES])
        idx = {k: sb(f"idx_{k}", [P, TILES], i32)
               for k in ("e_d", "e_s", "src_d", "dst_d", "add_d", "dst_s", "last_s", "add_s")}
        ident = sb("ident", [P, P])
        pos = sb("pos", [P, F], i32)
        one = sb("one", [1, P])
        zero_col = sb("zero_col", [P, 1])
        eps_col = sb("eps_col", [P, 1])
        edge_mark = sb("edge_mark", [1, 2])
        wts = {k: sb(f"w_{k}", [P, P]) for k in
               ("W0", "W1", "W1T", "Wg", "WgT", "W2", "W2T", "L2", "L2T", "B1", "B2a", "B2b",
                "C", "K1", "K2", "lbgB")}
        att = sb("att", [P, 8])
        attw = sb("attw", [P, 8])
        cols = sb("cols", [P, 4])
        negc1 = sb("negc1", [1, P])
        fc1 = sb("fc1", [NSC, HID])
        fc2 = sb("fc2", [HID, 4 * MUL])
        wv_st = sb("wv_st", [P, 3 * 32])

        def carve(tile, start, size, shape=None, dt=fp32):
            ap = tile[:, start:start + size]
            if dt != fp32:
                ap = ap.bitcast(dt)
            return ap

        rec_st = big[:, 0:4096]
        src_i, dst_i = big[:, 4096:4352].bitcast(i32), big[:, 4352:4608].bitcast(i32)
        w_in, at4_in, at8_in = big[:, 4608:4864], big[:, 4864:5888], big[:, 5888:7936]
        lane_bufs = [big[:, 8192 + k * F:8192 + (k + 1) * F] for k in range(8)]
        sort_b, sort_a = lane_bufs[0:2], lane_bufs[2:4]
        gray, flip = lane_bufs[4].bitcast(i32), lane_bufs[5].bitcast(i32)
        key_f, tmp_f = lane_bufs[6], lane_bufs[7]
        tmp_g = big[:, 10240:10496]
        DB = 10496
        dense = [big[:, DB + k * CHUNK * ROW:DB + (k + 1) * CHUNK * ROW].rearrange("p (r c) -> p r c", c=ROW)
                 for k in range(DBUF)]
        NV = DB + DBUF * CHUNK * ROW
        nv1, nv2, nvh = (big[:, NV + k * PER_LANE:NV + (k + 1) * PER_LANE] for k in range(3))
        LB = NV + 3 * PER_LANE
        left_rows = big[0:LEFT, LB:LB + ROW]
        zeros = big[:, LB + ROW:LB + ROW + 8 * ROW]
        assert LB + 9 * ROW <= TILES * ROW
        hw_last = wv_st[:, 95:96]

        SC = 2400
        wk = [work[0:LANES, SC + k * F:SC + (k + 1) * F] for k in range(15)]
        keyl, prevl, nextl, sprev, snext, eqp, eqn, isl = wk[0:8]
        fa, fb, posf, trash = wk[8:12]
        clipl, clprev, clnext = wk[12:15]
        SC += 15 * F
        ends, endz, carry = (work[0:LANES, SC + 4 * k:SC + 4 * k + 4] for k in range(3))
        rows, run = work[0:4, SC + 16:SC + 272], work[0:4, SC + 272:SC + 372]
        SC += 384
        alb, fw, bw, tt4 = (work[0:LANES, SC + k * H * F:SC + (k + 1) * H * F] for k in range(4))

        weights_in = sem("weights_in")
        consts_ready = sem("consts_ready")
        vec = sem("vec_order")
        asked, answered = sem("pe_asked"), sem("pe_answered")
        pads_ready, raw_in, rec_ready, raw_stored = sem("pads_ready"), sem("raw_in"), sem("rec_ready"), sem("raw_stored")
        dvec_in, dense_ready = sem("dense_vectors_in"), sem("dense_consts")
        dense_in = [sem(f"dense_in{k}") for k in range(DBUF)]
        dense_out = [sem(f"dense_out{k}") for k in range(DBUF)]
        dense_sum = sem("dense_sum")
        left_in, left_sum, left_out = sem("left_in"), sem("left_sum"), sem("left_out")
        keys_ready, keys_stored, keys_in = sem("keys_ready"), sem("keys_stored"), sem("keys_in")
        e_ready = sem("sorted_edges_ready")
        recs_ready, recs_stored = sem("recs_ready"), sem("recs_stored")
        exp_asked, exp_done = sem("exp_asked"), sem("exp_done")
        stage = sem("stage_done")
        roots = sem("roots_ready")

        def stage_end(eng, n):
            eng.sem_inc(stage, 1)
            eng.wait_ge(stage, 5 * n)

        paced = sem("paced")

        def plain(eng):
            eng.sem_inc(paced, 1)

        def loop_sems(name, words):
            out = {}
            for w in words.split():
                out[w] = [sem(f"{name}_{w}{k}") for k in range(2)] if w.endswith("_") else sem(f"{name}_{w}")
            return out

        R = loop_sems("rec", "idx_ rows_ taken")
        S0 = loop_sems("gcn", "var dev idx_ rows_ keys_ taken norm h sel sums chained delta kept")
        A = loop_sems("add", "idx_ delta added_")
        S1 = loop_sems("gat", "var dev idx_ rows_ taken norm h hT hTs xx xxs hh kept logit logits")
        S1b = loop_sems("gatsum", "idx_ keys_ sel sums chained biased z delta kept added_")
        S2 = loop_sems("hyp", "var dev idx_ rows_ keys_ taken norm h sel sums chained he hes stored_")
        S3 = loop_sems("hypsum", "idx_ idxa_ rows_ keys_ sel sums chained delta kept added_ at atT atTs fc fcs w ws wst_")
        S4 = loop_sems("tp", "var dev idx_ rows_ keys_ w_ norm h hT hTs e feat sel sums chained delta kept")

        def ring(start, size, n=2, dt=fp32):
            out = [work[:, start + k * size:start + (k + 1) * size] for k in range(n)]
            return [o.bitcast(dt) for o in out] if dt != fp32 else out

        W8 = 2 * GROUP
        rows_r = ring(0, W8 * ROW)
        idx_r = ring(2112, 8, dt=i32)
        idxa_r = ring(2128, 8, dt=i32)
        small = ring(2144, 128)
        v_r = ring(2400, 512)
        h_r = ring(3424, 512)
        keys_r = ring(4448, GE + 8)
        sel_r = ring(5488, 512)
        ind_r = ring(6512, 512)
        uT_r = ring(7536, 512)
        selw_r = ring(8560, 512)
        dl_r = ring(9584, GROUP * ROW)
        z_r = ring(10640, 512)
        t1_r = ring(11664, 512)
        row_r = ring(12688, 512)
        v8 = ring(2400, 1024)
        h8 = ring(4448, 1024)
        hT8 = work[:, 6496:7520]
        xxT8 = work[:, 7520:8544]
        uT2_r = ring(7536, 1024)
        feat_r = ring(9584, 1024)
        q_t = work[:, 11632:12144]
        t_t = work[:, 12144:12528]
        m3_t = work[:, 12528:12656]
        w_r = ring(12656, 512)
        hT_s = work[:, 2400:2912]

        def t4(ap, c=128):
            return ap.rearrange("p (t c) -> p t c", c=c)

        def wide(ap, n=128):
            return ap.unsqueeze(2).broadcast_to([ap.shape[0], ap.shape[1], n])

        def over(ap, n):
            return ap.unsqueeze(1).broadcast_to([ap.shape[0], n, ap.shape[1]])

        def cols4(tile, G, width=4):
            return tile[:, bass.ds(G.g * width, width)] if not isinstance(G.g, int) else tile[:, G.g * width:(G.g + 1) * width]

        def at(ap, G, n):
            return cols4(ap, G, n)

        block = ctx.enter_context(nc.Block())

        SMALL_LOADS = [
            (wts["W0"][:, :], L0_W), (wts["W1"][:, :], W1), (wts["Wg"][:, :], Wg), (wts["W2"][:, :], W2),
            (wts["L2"][:, :], L2_W),
            (wts["C"][:, :], L0_b.partition_broadcast(P)), (wts["K1"][:, :], b2.partition_broadcast(P)),
            (wts["K2"][:, :], L2_b.partition_broadcast(P)),
            (cols[:, 0:1], b1.unsqueeze(1)), (cols[:, 1:2], bias_g.unsqueeze(1)),
            (fc1[:, :], Wfc1), (fc2[:, :], Wfc2),
        ]

        def rows_of(dram, G):
            part = dram[bass.ds(G.g * GE, GE), :] if not isinstance(G.g, int) else dram[G.g * GE:(G.g + 1) * GE, :]
            return part.rearrange("(t p) c -> p t c", p=P)

        def load_keys(sp, G, which, S):
            if G.from_(2):
                sp.wait_ge(S["sel"], G.g - 1)
            k = keys_dram[which]
            part = k[bass.ds(G.g * GE, GE + 1)] if not isinstance(G.g, int) else k[G.g * GE:G.g * GE + GE + 1]
            sp.dma_start(keys_r[G.slot][:, 0:GE + 1], part.partition_broadcast(P)).then_inc(S["keys_"][G.slot], 16)

        def sp_indices(sp, S, of, again):
            def body(G):
                if G.from_(2):
                    sp.wait_ge(S["rows_"][G.slot], 64 * counted(G, again).use)
                sp.dma_start(idx_r[G.slot][:, 0:4], cols4(of, G)).then_inc(S["idx_"][G.slot], 16)
            for_groups(sp, body)

        def add_indices(sp, S, of, again):
            def body(G):
                if G.from_(2):
                    sp.wait_ge(S["added_"][G.slot], 64 * counted(G, again).use)
                sp.dma_start(idxa_r[G.slot][:, 0:4], cols4(of, G)).then_inc(S["idx_"][G.slot], 16)
            for_groups(sp, body)

        @block.sync
        def _(sp):
            for to, of in SMALL_LOADS:
                sp.dma_start(to, of).then_inc(weights_in, 16)
            sp.wait_ge(consts_ready, 1)
            n = len(SMALL_LOADS)
            with nc.allow_non_contiguous_dma(reason="small weights"):
                for h in range(H):
                    sp.dma_start(att[C * h:C * h + C, h:h + 1], att_src[0, h, :].unsqueeze(1)).then_inc(weights_in, 16)
                    sp.dma_start(att[C * h:C * h + C, 4 + h:5 + h], att_dst[0, h, :].unsqueeze(1)).then_inc(weights_in, 16)
                    n += 2
                sp.dma_start(wts["B1"][0:32, 0:32], w1_s).then_inc(weights_in, 16)
                n += 1
                for a in range(3):
                    sp.dma_start(wts["B1"][32 + a:P:3, 32 + 32 * a:64 + 32 * a], w1_v).then_inc(weights_in, 16)
                    n += 1
                for k, b in enumerate(("B2a", "B2b")):
                    sp.dma_start(wts[b][0:32, 0:32], w2_s[k]).then_inc(weights_in, 16)
                    n += 1
                    for a in range(3):
                        sp.dma_start(wv_st[32 + 32 * a:64 + 32 * a, 32 * k:32 * k + 32], w2_v[k]).then_inc(weights_in, 16)
                        n += 1
            assert n == N_WEIGHTS

            lane_rows = x[0:P * PER_LANE, :].rearrange("(p r) c -> p r c", r=PER_LANE)
            lane_out = table[0:P * PER_LANE, :].rearrange("(p r) c -> p r c", r=PER_LANE)
            sp.dma_start(nv1, node_vec1[0:P * PER_LANE, 0].rearrange("(p r) -> p r", r=PER_LANE)).then_inc(dvec_in, 16)
            sp.dma_start(nv2, node_vec1_n2[0:P * PER_LANE, 0].rearrange("(p r) -> p r", r=PER_LANE)).then_inc(dvec_in, 16)
            sp.dma_start(hw_last, hw[M - 1:M].partition_broadcast(P)).then_inc(dvec_in, 16)
            full, rest = M // PER_LANE, M % PER_LANE
            sp.wait_ge(dense_ready, 1)
            sp.dma_start(nvh[0:full, :], hw[0:full * PER_LANE].rearrange("(p r) -> p r", r=PER_LANE)).then_inc(dvec_in, 16)
            sp.dma_start(nvh[full:full + 1, 0:rest], hw[full * PER_LANE:M].unsqueeze(0)).then_inc(dvec_in, 16)
            for k in range(NCHUNK + 1):
                if k < NCHUNK:
                    if k >= DBUF:
                        sp.wait_ge(dense_out[k % DBUF], 16 * (k // DBUF))
                    sp.dma_start(dense[k % DBUF][:, :, 0:D], lane_rows[:, k * CHUNK:(k + 1) * CHUNK, :]
                                 ).then_inc(dense_in[k % DBUF], 16)
                if k >= 1:
                    j = k - 1
                    sp.wait_ge(dense_sum, j + 1)
                    sp.dma_start(lane_out[:, j * CHUNK:(j + 1) * CHUNK, :], dense[j % DBUF]
                                 ).then_inc(dense_out[j % DBUF], 16)
            sp.dma_start(left_rows[:, 0:D], x[P * PER_LANE:N, :]).then_inc(left_in, 16)
            sp.dma_start(left_rows[:, COL_A:COL_A + 1], node_vec1[P * PER_LANE:N, :]).then_inc(left_in, 16)
            sp.dma_start(left_rows[:, COL_B:COL_B + 1], node_vec1_n2[P * PER_LANE:N, :]).then_inc(left_in, 16)
            sp.wait_ge(left_sum, 1)
            sp.dma_start(table[P * PER_LANE:N, :], left_rows).then_inc(left_out, 16)
            sp.dma_start(table[N:N + 1, :], zeros[0:1, 0:ROW]).then_inc(left_out, 16)
            sp.dma_start(table[N + 1:TABLE, :].rearrange("(p r) c -> p (r c)", p=P), zeros[:, 0:SPARE // P * ROW]
                         ).then_inc(left_out, 16)
            sp.wait_ge(left_out, 48)
            for k in range(DBUF):
                sp.wait_ge(dense_out[k], 16 * len(range(k, NCHUNK, DBUF)))

            sp.wait_ge(e_ready, 1)
            sp_indices(sp, R, idx["e_d"], False)
            sp.wait_ge(e_ready, 2)
            sp_indices(sp, R, idx["e_s"], True)
            stage_end(sp, 1)

            def body(G):
                if G.from_(2):
                    sp.wait_ge(S0["rows_"][G.slot], 64 * G.use)
                sp.dma_start(idx_r[G.slot][:, 0:4], cols4(idx["dst_s"], G)).then_inc(S0["idx_"][G.slot], 16)
                load_keys(sp, G, "src", S0)
            for_groups(sp, body)
            stage_end(sp, 2)
            add_indices(sp, A, idx["add_s"], False)
            stage_end(sp, 3)

            def body(G):
                if G.from_(2):
                    sp.wait_ge(S1["rows_"][G.slot], 128 * G.use)
                sp.dma_start(idx_r[G.slot][:, 0:4], cols4(idx["src_d"], G)).then_inc(S1["idx_"][G.slot], 16)
                sp.dma_start(idx_r[G.slot][:, 4:8], cols4(idx["dst_d"], G)).then_inc(S1["idx_"][G.slot], 16)
            for_groups(sp, body)
            stage_end(sp, 4)
            stage_end(sp, 5)

            def body(G):
                load_keys(sp, G, "dst", S1b)
                if G.from_(2):
                    sp.wait_ge(S1b["added_"][G.slot], 64 * G.use)
                sp.dma_start(idxa_r[G.slot][:, 0:4], cols4(idx["add_d"], G)).then_inc(S1b["idx_"][G.slot], 16)
            for_groups(sp, body)
            stage_end(sp, 6)

            def store(G):
                sp.wait_ge(S2["hes"], G.g + 1)
                sp.dma_start(rows_of(he_dram, G), t4(dl_r[G.slot][:, 0:512])).then_inc(S2["stored_"][G.slot], 16)

            def body(G):
                if G.from_(2):
                    sp.wait_ge(S2["rows_"][G.slot], 64 * G.use)
                sp.dma_start(idx_r[G.slot][:, 0:4], cols4(idx["src_d"], G)).then_inc(S2["idx_"][G.slot], 16)
                load_keys(sp, G, "clip", S2)
                if G.from_(2):
                    store(G.before(2))
            for_groups(sp, body)
            for g in (NG - 2, NG - 1):
                store(Group(g, g // 2, g % 2))
            sp.wait_ge(S2["stored_"][0], 16 * ((NG + 1) // 2))
            sp.wait_ge(S2["stored_"][1], 16 * (NG // 2))
            stage_end(sp, 7)

            def store(G):
                sp.wait_ge(S3["ws"], G.g + 1)
                sp.dma_start(at(w_dram, G, 512), t1_r[G.slot]).then_inc(S3["wst_"][G.slot], 16)

            def body(G):
                if G.from_(2):
                    sp.wait_ge(S3["rows_"][G.slot], 64 * G.use)
                sp.dma_start(idx_r[G.slot][:, 0:4], cols4(idx["last_s"], G)).then_inc(S3["idx_"][G.slot], 16)
                load_keys(sp, G, "src", S3)
                if G.from_(2):
                    sp.wait_ge(S3["added_"][G.slot], 64 * G.use)
                    plain(sp)
                sp.dma_start(idxa_r[G.slot][:, 0:4], cols4(idx["add_s"], G)).then_inc(S3["idxa_"][G.slot], 16)
                if G.from_(2):
                    store(G.before(2))
            for_groups(sp, body)
            for g in (NG - 2, NG - 1):
                store(Group(g, g // 2, g % 2))
            sp.wait_ge(S3["wst_"][0], 16 * ((NG + 1) // 2))
            sp.wait_ge(S3["wst_"][1], 16 * (NG // 2))
            stage_end(sp, 8)

            def body(G):
                if G.from_(2):
                    sp.wait_ge(S4["rows_"][G.slot], 64 * G.use)
                sp.dma_start(idx_r[G.slot][:, 0:4], cols4(idx["src_d"], G)).then_inc(S4["idx_"][G.slot], 16)
                load_keys(sp, G, "dst", S4)
                if G.from_(2):
                    sp.wait_ge(S4["feat"], G.g - 1)
                sp.dma_start(w_r[G.slot], at(w_dram, G, 512)).then_inc(S4["w_"][G.slot], 16)
            for_groups(sp, body)
            stage_end(sp, 9)
            add_indices(sp, A, idx["add_d"], True)
            stage_end(sp, 10)

        @block.gpsimd
        def _(pool):
            g_ = nc.gpsimd
            for b in ("B1", "B2a", "B2b"):
                g_.memset(wts[b][:, :], 0.0)
            g_.memset(att[:, :], 0.0)
            g_.memset(wv_st[:, :], 0.0)
            g_.memset(ident[:, :], 0.0).then_inc(consts_ready, 1)
            g_.iota(pos[:, :], pattern=[[1, F]], base=0, channel_multiplier=F)
            g_.memset(one[:, :], 1.0)
            g_.memset(zero_col[:, :], 0.0)
            g_.memset(eps_col[:, :], EPS)
            g_.memset(edge_mark[:, :], -1.0)
            pool.wait_ge(consts_ready, 1)
            g_.affine_select(out=ident[:, :], in_=ident[:, :], compare_op=ALU.not_equal, fill=1.0, base=0,
                             pattern=[[-1, P]], channel_multiplier=1).then_inc(consts_ready, 1)

            def gather(G, table_ap, S, slot_ap, idx_ap, per=4):
                plain(pool)
                for k in range(per):
                    g_.indirect_dma_start(slot_ap(G, k), None, table_ap,
                                          bass.IndirectOffsetOnAxis(ap=idx_ap[G.slot][:, k:k + 1], axis=0)
                                          ).then_inc(S["rows_"][G.slot], 16)

            def rec_slot(G, k):
                return rows_r[G.slot][:, k * REC:(k + 1) * REC]

            def row_slot(G, k):
                return rows_r[G.slot][:, k * ROW:(k + 1) * ROW]

            def he_slot(G, k):
                return rows_r[G.slot][:, k * D:(k + 1) * D]

            def gathers(S, table_ap, slot, per=4, free="taken", again=False):
                def body(G):
                    n = counted(G, again)
                    pool.wait_ge(S["idx_"][G.slot], 16 * (per // 4) * (n.use + 1))
                    if G.from_(2):
                        pool.wait_ge(S[free], n.g - 1)
                    gather(G, table_ap, S, slot, idx_r, per)
                return body

            def adds(G, S, of):
                plain(pool)
                for k in range(GROUP):
                    g_.indirect_dma_start(table[:, :], bass.IndirectOffsetOnAxis(ap=idxa_r[G.slot][:, k:k + 1], axis=0),
                                          of[G.slot][:, k * ROW:(k + 1) * ROW], None, compute_op=ALU.add
                                          ).then_inc(S["added_"][G.slot], 16)

            def adding(S, ready, again=False):
                def body(G):
                    n = counted(G, again)
                    pool.wait_ge(S["idx_"][G.slot], 16 * (n.use + 1))
                    pool.wait_ge(S[ready], n.g + 1)
                    adds(G, S, dl_r)
                return body

            def added_all(S, loops=1):
                pool.wait_ge(S["added_"][0], 64 * loops * ((NG + 1) // 2))
                pool.wait_ge(S["added_"][1], 64 * loops * (NG // 2))

            pool.wait_ge(raw_stored, 16)
            for_groups(pool, gathers(R, rec_raw, rec_slot))
            pool.wait_ge(recs_stored, 16)
            for_groups(pool, gathers(R, rec_d, rec_slot, again=True))
            stage_end(pool, 1)
            for_groups(pool, gathers(S0, table, row_slot))
            stage_end(pool, 2)
            for_groups(pool, adding(A, "delta"))
            added_all(A)
            stage_end(pool, 3)
            for_groups(pool, gathers(S1, table, row_slot, per=8))
            stage_end(pool, 4)
            stage_end(pool, 5)
            for_groups(pool, adding(S1b, "kept"))
            added_all(S1b)
            stage_end(pool, 6)
            for_groups(pool, gathers(S2, table, row_slot))
            stage_end(pool, 7)

            def add_he(G):
                pool.wait_ge(S3["idxa_"][G.slot], 16 * (G.use + 1))
                pool.wait_ge(S3["kept"], G.g + 1)
                adds(G, S3, dl_r)

            take = gathers(S3, he_dram, he_slot, free="sums")

            def body(G):
                take(G)
                if G.from_(2):
                    add_he(G.before(2))
            def body(G):
                if G.from_(2):
                    add_he(G.before(2))
                take(G)
            for_groups(pool, body)
            for g in (NG - 2, NG - 1):
                add_he(Group(g, g // 2, g % 2))
            added_all(S3)
            stage_end(pool, 8)
            for_groups(pool, gathers(S4, table, row_slot, free="h"))
            stage_end(pool, 9)
            for_groups(pool, adding(A, "delta", again=True))
            added_all(A, 2)
            stage_end(pool, 10)

        @block.tensor
        def _(pe):
            T = nc.tensor
            count = [0]

            def asked_next():
                count[0] += 1
                pe.wait_ge(asked, count[0])

            def flip_blocks(of, cols_of, n_in, width):
                for b in range(2):
                    last = T.transpose(bank[0][0:width, b * n_in:(b + 1) * n_in], cols_of(of, b), ident[0:n_in, 0:n_in])
                last.then_inc(answered, 1)

            lane_blocks = lambda ap, b: ap[:, b * P:(b + 1) * P]
            col_blocks = lambda ap, b: ap[:, b::2]

            def carries(n, row):
                asked_next()
                T.transpose(bank[1][0:n, 0:LANES], ends[:, 0:n], ident[0:LANES, 0:LANES])
                T.transpose(bank[1][0:n, LANES:2 * LANES], endz[:, 0:n], ident[0:LANES, 0:LANES]).then_inc(answered, 1)
                asked_next()
                T.transpose(bank[1][0:LANES, 256:256 + n], row[0:n, :], ident[0:n, 0:n]).then_inc(answered, 1)

            fwd_row, bwd_row = run[:, 0:LANES], run[:, 1:LANES + 1]

            pe.wait_ge(consts_ready, 2)
            pe.wait_ge(weights_in, 16 * N_WEIGHTS)
            asked_next()
            for k, w in enumerate(("W1", "Wg", "W2", "L2")):
                T.transpose(bank[0][:, k * P:(k + 1) * P], wts[w][:, :], ident[:, :])
            T.matmul(bank[1][:, 0:8], wts["Wg"][:, :], att[:, :], start=True, stop=True).then_inc(answered, 1)
            asked_next()
            T.matmul(bank[1][:, 128:256], wts["lbgB"][:, :], wts["W2T"][:, :], start=True, stop=True).then_inc(answered, 1)

            def sort_transposes():
                for k in range(9, LOG + 1):
                    asked_next()
                    flip_blocks(sort_b[0], lane_blocks, P, P)
                    asked_next()
                    flip_blocks(sort_a[(k - 8) % 2], col_blocks, P, P)
                asked_next()
                flip_blocks(sort_b[0], lane_blocks, P, P)

            def to_cols(ap):
                asked_next()
                for b in range(2):
                    last = T.transpose(bank[0][:, b * LANES:(b + 1) * LANES], ap[:, b * P:(b + 1) * P], ident[0:LANES, 0:LANES])
                last.then_inc(answered, 1)

            sort_transposes()
            to_cols(keyl)
            to_cols(fa)
            to_cols(clipl)
            carries(1, bwd_row)
            to_cols(fb)
            carries(1, fwd_row)
            to_cols(fa)
            asked_next()
            for b in range(2):
                last = T.transpose(bank[0][0:LANES, b * P:(b + 1) * P],
                                   rec[:, :].rearrange("p (t c) -> p t c", c=REC)[:, b::2, R_SRC], ident[:, :])
            last.then_inc(answered, 1)
            sort_transposes()
            to_cols(keyl)
            to_cols(fa)
            stage_end(pe, 1)

            def sum_tiles(G, S, rhs, lhs, out, ready):
                pe.wait_ge(S["sel"], G.g + 1)
                if ready:
                    pe.wait_ge(S[ready], G.g + 1)
                if G.from_(2):
                    pe.wait_ge(S["chained"], G.g - 1)
                for t in range(GROUP):
                    last = T.matmul(out[:, t * P:(t + 1) * P], lhs[:, t * P:(t + 1) * P], rhs[:, t * P:(t + 1) * P],
                                    start=True, stop=True)
                return last

            def sums(G):
                sum_tiles(G, S0, selw_r[G.slot], h_r[G.slot], bank[G.slot], "h")
                for t in range(GROUP):
                    last = T.matmul(bank[2 + G.slot][0:1, t * P:(t + 1) * P], small[G.slot][:, 64 + t:65 + t],
                                    sel_r[G.slot][:, t * P:(t + 1) * P], start=True, stop=True)
                last.then_inc(S0["sums"], 1)

            def delta(G):
                pe.wait_ge(S0["chained"], G.g + 1)
                if G.from_(2):
                    pe.wait_ge(S0["kept"], G.g - 1)
                for t in range(GROUP):
                    T.matmul(bank[4 + G.slot][:, t * P:(t + 1) * P], uT_r[G.slot][:, t * P:(t + 1) * P],
                             wts["W0"][:, :], start=True, stop=True)
                for t in range(GROUP):
                    last = T.matmul(bank[6 + G.slot][:, t:t + 1], row_r[G.slot][0:1, t * P:(t + 1) * P], one[0:1, 0:1],
                                    start=True, stop=True)
                last.then_inc(S0["delta"], 1)

            def body(G):
                sums(G)
                if G.from_(1):
                    delta(G.before())
            for_groups(pe, body)
            delta(Group(NG - 1, NG // 2, 0))
            stage_end(pe, 2)
            stage_end(pe, 3)

            def turn(G):
                pe.wait_ge(S1["h"], G.g + 1)
                if G.from_(1):
                    pe.wait_ge(S1["hTs"], G.g)
                for t in range(W8):
                    last = T.transpose(bank[t // 4][:, t % 4 * P:(t % 4 + 1) * P], h8[G.slot][:, t * P:(t + 1) * P], ident[:, :])
                last.then_inc(S1["hT"], 1)

            def first(G):
                pe.wait_ge(S1["hTs"], G.g + 1)
                if G.from_(1):
                    pe.wait_ge(S1["xxs"], G.g)
                for k in range(2):
                    last = T.matmul(bank[2 + k][:, :], wts["W1T"][:, :], hT8[:, k * 512:(k + 1) * 512], start=True, stop=True)
                last.then_inc(S1["xx"], 1)

            def second(G):
                pe.wait_ge(S1["xxs"], G.g + 1)
                if G.from_(1):
                    pe.wait_ge(S1["kept"], G.g)
                    pe.wait_ge(S1["logits"], G.g)
                for t in range(GROUP):
                    T.matmul(bank[4][:, t * P:(t + 1) * P], xxT8[:, t * P:(t + 1) * P], wts["WgT"][:, :], start=True, stop=True)
                for t in range(GROUP):
                    o = bank[5][:, t * H:(t + 1) * H]
                    T.matmul(o, xxT8[:, t * P:(t + 1) * P], attw[:, 0:4], start=True, stop=False)
                    last = T.matmul(o, xxT8[:, 512 + t * P:512 + (t + 1) * P], attw[:, 4:8], start=False, stop=True)
                last.then_inc(S1["hh"], 1)

            def body(G):
                turn(G)
                if G.from_(1):
                    second(G.before())
                first(G)
            for_groups(pe, body)
            second(Group(NG - 1, NG // 2, 0))
            stage_end(pe, 4)

            asked_next()
            alc = al[:, :].rearrange("p (t h) -> p t h", h=H)
            for h in range(H):
                for b in range(2):
                    c0 = (h % 2) * F + b * P
                    last = T.transpose(bank[2 + h // 2][0:LANES, c0:c0 + P], alc[:, b::2, h], ident[:, :])
            last.then_inc(answered, 1)
            carries(H, fwd_row)
            carries(H, bwd_row)
            carries(H, fwd_row)
            carries(H, bwd_row)
            asked_next()
            for h in range(H):
                for b in range(2):
                    c0 = (h % 2) * TILES + b * LANES
                    last = T.transpose(bank[2 + h // 2][:, c0:c0 + LANES], tt4[:, h * F + b * P:h * F + (b + 1) * P],
                                       ident[0:LANES, 0:LANES])
            last.then_inc(answered, 1)
            stage_end(pe, 5)

            def sums(G):
                sum_tiles(G, S1b, sel_r[G.slot], h_r[G.slot], bank[G.slot], None).then_inc(S1b["sums"], 1)

            def delta(G):
                pe.wait_ge(S1b["z"], G.g + 1)
                if G.from_(2):
                    pe.wait_ge(S1b["kept"], G.g - 1)
                for t in range(GROUP):
                    o = bank[4 + G.slot][:, t * P:(t + 1) * P]
                    T.matmul(o, one[0:1, :], negc1[0:1, :], start=True, stop=False)
                    last = T.matmul(o, z_r[G.slot][:, t * P:(t + 1) * P], wts["W2T"][:, :], start=False, stop=True)
                last.then_inc(S1b["delta"], 1)

            def body(G):
                sums(G)
                if G.from_(2):
                    delta(G.before(2))
            for_groups(pe, body, peel=4)
            delta(Group(NG - 2, NG // 2 - 1, 1))
            delta(Group(NG - 1, NG // 2, 0))
            stage_end(pe, 6)

            def sums(G):
                sum_tiles(G, S2, sel_r[G.slot], h_r[G.slot], bank[G.slot], "h").then_inc(S2["sums"], 1)

            def turn(G):
                pe.wait_ge(S2["chained"], G.g + 1)
                if G.from_(2):
                    pe.wait_ge(S2["hes"], G.g - 1)
                for t in range(GROUP):
                    last = T.transpose(bank[4 + G.slot][:, t * P:(t + 1) * P], uT_r[G.slot][:, t * P:(t + 1) * P], ident[:, :])
                last.then_inc(S2["he"], 1)

            def body(G):
                sums(G)
                if G.from_(1):
                    turn(G.before())
            for_groups(pe, body)
            turn(Group(NG - 1, NG // 2, 0))
            stage_end(pe, 7)

            def sums(G):
                pe.wait_ge(S3["rows_"][G.slot], 64 * (G.use + 1))
                sum_tiles(G, S3, sel_r[G.slot], rows_r[G.slot], bank[G.slot], None).then_inc(S3["sums"], 1)

            def delta(G):
                pe.wait_ge(S3["chained"], G.g + 1)
                if G.from_(1):
                    pe.wait_ge(S3["kept"], G.g)
                for t in range(GROUP):
                    last = T.matmul(bank[2][:, t * P:(t + 1) * P], uT_r[G.slot][:, t * P:(t + 1) * P],
                                    wts["L2T"][:, :], start=True, stop=True)
                last.then_inc(S3["delta"], 1)

            def net_in(G):
                pe.wait_ge(S3["at"], G.g + 1)
                for t in range(GROUP):
                    last = T.transpose(bank[3][0:NSC, t * P:(t + 1) * P], small[G.slot][:, t * NSC:(t + 1) * NSC], ident[:, :])
                last.then_inc(S3["atT"], 1)

            def net_mid(G):
                pe.wait_ge(S3["atTs"], G.g + 1)
                T.matmul(bank[5][0:HID, :], fc1[:, :], row_r[0][0:NSC, :], start=True, stop=True).then_inc(S3["fc"], 1)

            def net_out(G):
                pe.wait_ge(S3["fcs"], G.g + 1)
                if G.from_(1):
                    pe.wait_ge(S3["ws"], G.g)
                for t in range(GROUP):
                    last = T.matmul(bank[6][:, t * P:(t + 1) * P], z_r[0][0:HID, t * P:(t + 1) * P], fc2[:, :],
                                    start=True, stop=True)
                last.then_inc(S3["w"], 1)

            def body(G):
                net_in(G)
                sums(G)
                net_mid(G)
                if G.from_(1):
                    delta(G.before())
                net_out(G)
            for_groups(pe, body)
            delta(Group(NG - 1, NG // 2, 0))
            stage_end(pe, 8)

            def turn(G):
                pe.wait_ge(S4["h"], G.g + 1)
                if G.from_(1):
                    pe.wait_ge(S4["hTs"], G.g)
                for t in range(GROUP):
                    last = T.transpose(bank[0][:, t * P:(t + 1) * P], h_r[G.slot][:, t * P:(t + 1) * P], ident[:, :])
                last.then_inc(S4["hT"], 1)

            def linear(G):
                pe.wait_ge(S4["hTs"], G.g + 1)
                if G.from_(2):
                    pe.wait_ge(S4["feat"], G.g - 1)
                for t in range(GROUP):
                    last = T.matmul(bank[1 + G.slot][:, t * P:(t + 1) * P], hT_s[:, t * P:(t + 1) * P], wts["B1"][:, :],
                                    start=True, stop=True)
                last.then_inc(S4["e"], 1)

            def sums(G):
                pe.wait_ge(S4["feat"], G.g + 1)
                pe.wait_ge(S4["sel"], G.g + 1)
                if G.from_(2):
                    pe.wait_ge(S4["chained"], G.g - 1)
                f = feat_r[G.slot].rearrange("p (t k c) -> p t k c", t=GROUP, k=2)
                for k in range(2):
                    for t in range(GROUP):
                        last = T.matmul(bank[3 + 2 * G.slot + k][:, t * P:(t + 1) * P], f[:, t, k, :],
                                        sel_r[G.slot][:, t * P:(t + 1) * P], start=True, stop=True)
                last.then_inc(S4["sums"], 1)

            def delta(G):
                pe.wait_ge(S4["chained"], G.g + 1)
                if G.from_(1):
                    pe.wait_ge(S4["kept"], G.g)
                for t in range(GROUP):
                    o = bank[7][:, t * P:(t + 1) * P]
                    T.matmul(o, uT2_r[G.slot][:, t * P:(t + 1) * P], wts["B2a"][:, :], start=True, stop=False)
                    last = T.matmul(o, uT2_r[G.slot][:, 512 + t * P:512 + (t + 1) * P], wts["B2b"][:, :], start=False, stop=True)
                last.then_inc(S4["delta"], 1)

            def body(G):
                turn(G)
                if G.from_(1):
                    sums(G.before())
                linear(G)
                if G.from_(2):
                    delta(G.before(2))
            for_groups(pe, body, peel=4)
            sums(Group(NG - 1, NG // 2, 0))
            delta(Group(NG - 2, NG // 2 - 1, 1))
            delta(Group(NG - 1, NG // 2, 0))
            stage_end(pe, 9)
            stage_end(pe, 10)

        @block.scalar
        def _(act):
            S_ = nc.scalar

            act.wait_ge(pads_ready, 1)
            full, rest = E // F, E % F
            for to, of, c in ((src_i, src, 1), (dst_i, dst, 1), (w_in, edge_weight, 1)):
                act.dma_start(to[0:full, :], of[0:full * F].rearrange("(q f) -> q f", f=F)).then_inc(raw_in, 16)
                act.dma_start(to[full:full + 1, 0:rest], of[full * F:E].unsqueeze(0)).then_inc(raw_in, 16)
            for to, of, c in ((at4_in, edge_attr_4, 4), (at8_in, edge_attr_8, 8)):
                act.dma_start(to[0:full, :], of[0:full * F, :].rearrange("(q f) c -> q (f c)", f=F)).then_inc(raw_in, 16)
                act.dma_start(to[full:full + 1, 0:rest * c], of[full * F:E, :].rearrange("(q f) c -> q (f c)", q=1)
                              ).then_inc(raw_in, 16)
            act.wait_ge(rec_ready, 1)
            act.dma_start(rec_raw.rearrange("(q f) c -> q (f c)", f=F), rec_st[0:LANES, :]).then_inc(raw_stored, 16)
            act.wait_ge(raw_stored, 16)

            def keep_records(S, to, n, again):
                def body(G):
                    act.wait_ge(S["rows_"][G.slot], 64 * (counted(G, again).use + 1))
                    S_.copy(cols4(to, G, 4 * n).rearrange("p (t c) -> p t c", c=n),
                           rows_r[G.slot][:, 0:4 * REC].rearrange("p (t c) -> p t c", c=REC)[:, :, 0:n]
                           ).then_inc(S["taken"], 1)
                for_groups(act, body)

            keep_records(R, rec, REC, False)

            def exchange_keys(which, n_keys, n_done):
                act.wait_ge(keys_ready, n_keys)
                k = keys_dram[which]
                of = clipl if which == "clip" else keyl
                act.dma_start(k[1:EP + 1].rearrange("(q f) -> q f", f=F), of).then_inc(keys_stored, 16)
                act.dma_start(k[0:1].unsqueeze(0), edge_mark[0:1, 0:1]).then_inc(keys_stored, 16)
                act.dma_start(k[EP + 1:EP + 2].unsqueeze(0), edge_mark[0:1, 1:2]).then_inc(keys_stored, 16)
                act.wait_ge(keys_stored, 48 * n_done)

            def neighbours(which, n):
                k = keys_dram[which]
                act.dma_start(prevl, k[0:EP].rearrange("(q f) -> q f", f=F)).then_inc(keys_in, 16)
                act.dma_start(nextl, k[2:EP + 2].rearrange("(q f) -> q f", f=F)).then_inc(keys_in, 16)
                act.wait_ge(keys_in, 32 * n)

            exchange_keys("dst", 1, 1)
            neighbours("dst", 1)
            exchange_keys("clip", 2, 2)
            act.wait_ge(recs_ready, 1)
            act.dma_start(rec_d.rearrange("(t p) c -> p t c", p=P), rec[:, :].rearrange("p (t c) -> p t c", c=REC)
                          ).then_inc(recs_stored, 16)
            act.wait_ge(recs_stored, 16)
            exchange_keys("src", 3, 3)
            neighbours("src", 2)
            keep_records(R, rec_s, 4, True)
            act.wait_ge(R["taken"], 2 * NG)
            stage_end(act, 1)

            def deviations(G, S, tiles):
                act.wait_ge(S["var"], G.g + 1)
                s = small[G.slot]
                S_.activation(s[:, 104:104 + tiles], s[:, 81:81 + 2 * tiles:2], ACT.Sqrt, bias=eps_col[:, :]
                             ).then_inc(S["dev"], 1)

            def norm(G, S, v, h, tiles, stat):
                act.wait_ge(S["norm"], G.g + 1)
                for t in range(tiles):
                    last = S_.activation(h[:, t * P:(t + 1) * P], v(t), ACT.Relu, bias=stat[:, 8 + t:9 + t],
                                        scale=stat[:, t:t + 1])
                last.then_inc(S["h"], 1)

            def keep(G):
                act.wait_ge(S0["delta"], G.g + 1)
                to = cols4(big, G, GROUP * ROW).rearrange("p (t c) -> p t c", c=ROW)
                S_.copy(to[:, :, 0:D], t4(bank[4 + G.slot][:, :]))
                S_.copy(to[:, :, COL_DV], bank[6 + G.slot][:, 0:GROUP]).then_inc(S0["kept"], 1)

            def body(G):
                deviations(G, S0, GROUP)
                if G.from_(2):
                    act.wait_ge(S0["sums"], G.g - 1)
                norm(G, S0, lambda t: v_r[G.slot][:, t * P:(t + 1) * P], h_r[G.slot], GROUP, small[G.slot])
                if G.from_(1):
                    keep(G.before())
            for_groups(act, body)
            keep(Group(NG - 1, NG // 2, 0))
            act.wait_ge(roots, 1)
            S_.activation(dvis_s[:, :], dvis_s[:, :], ACT.Sqrt).then_inc(roots, 1)
            stage_end(act, 2)

            def feed(S, again):
                def body(G):
                    if G.from_(2):
                        act.wait_ge(S["added_"][G.slot], 64 * counted(G, again).use)
                    S_.copy(dl_r[G.slot], cols4(big, G, GROUP * ROW)).then_inc(S["delta"], 1)
                for_groups(act, body)
            feed(A, False)
            stage_end(act, 3)

            def keep(G):
                act.wait_ge(S1["hh"], G.g + 1)
                S_.copy(cols4(big, G, 512), bank[4][:, :]).then_inc(S1["kept"], 1)

            def body(G):
                deviations(G, S1, W8)
                if G.from_(2):
                    act.wait_ge(S1["hT"], G.g - 1)
                norm(G, S1, lambda t: v8[G.slot][:, t * P:(t + 1) * P], h8[G.slot], W8, small[G.slot])
                act.wait_ge(S1["hT"], G.g + 1)
                if G.from_(1):
                    act.wait_ge(S1["xx"], G.g)
                for k in range(2):
                    last = S_.copy(hT8[:, k * 512:(k + 1) * 512], bank[k][:, :])
                last.then_inc(S1["hTs"], 1)
                if G.from_(1):
                    keep(G.before())
                act.wait_ge(S1["xx"], G.g + 1)
                for k in range(2):
                    last = S_.activation(xxT8[:, k * 512:(k + 1) * 512], bank[2 + k][:, :], ACT.Identity, bias=cols[:, 0:1])
                last.then_inc(S1["xxs"], 1)
            for_groups(act, body)
            keep(Group(NG - 1, NG // 2, 0))
            act.wait_ge(roots, 3)
            S_.activation(wt_col[:, :], wt_col[:, :], ACT.Sqrt).then_inc(roots, 1)
            act.wait_ge(S1["kept"], NG)
            stage_end(act, 4)

            act.dma_start(keyl, keys_dram["dst"][1:EP + 1].rearrange("(q f) -> q f", f=F)).then_inc(keys_in, 16)
            neighbours_again = keys_dram["dst"]
            act.dma_start(prevl, neighbours_again[0:EP].rearrange("(q f) -> q f", f=F)).then_inc(keys_in, 16)
            act.dma_start(nextl, neighbours_again[2:EP + 2].rearrange("(q f) -> q f", f=F)).then_inc(keys_in, 16)
            act.wait_ge(keys_in, 32 * 2 + 48)
            act.wait_ge(exp_asked, 1)
            S_.activation(alb, alb, ACT.Exp).then_inc(exp_done, 1)
            act.wait_ge(exp_done, 1)
            stage_end(act, 5)

            def biased(G):
                act.wait_ge(S1b["chained"], G.g + 1)
                if G.from_(2):
                    act.wait_ge(S1b["z"], G.g - 1)
                S_.activation(t1_r[G.slot], uT_r[G.slot], ACT.Identity, bias=cols[:, 1:2]).then_inc(S1b["biased"], 1)

            def keep(G):
                act.wait_ge(S1b["delta"], G.g + 1)
                if G.from_(2):
                    act.wait_ge(S1b["added_"][G.slot], 64 * G.use)
                S_.copy(dl_r[G.slot].rearrange("p (t c) -> p t c", c=ROW)[:, :, 0:D], t4(bank[4 + G.slot][:, :])
                       ).then_inc(S1b["kept"], 1)

            def body(G):
                if G.from_(1):
                    biased(G.before())
                if G.from_(2):
                    keep(G.before(2))
            for_groups(act, body, peel=4)
            biased(Group(NG - 1, NG // 2, 0))
            keep(Group(NG - 2, NG // 2 - 1, 1))
            keep(Group(NG - 1, NG // 2, 0))
            stage_end(act, 6)

            def keep(G):
                act.wait_ge(S2["he"], G.g + 1)
                if G.from_(2):
                    act.wait_ge(S2["stored_"][G.slot], 16 * G.use)
                s4 = cols4(hsc_col, G)
                for t in range(GROUP):
                    last = S_.mul(dl_r[G.slot][:, t * P:(t + 1) * P], bank[4 + G.slot][:, t * P:(t + 1) * P], s4[:, t:t + 1])
                last.then_inc(S2["hes"], 1)

            def body(G):
                deviations(G, S2, GROUP)
                if G.from_(2):
                    act.wait_ge(S2["sums"], G.g - 1)
                norm(G, S2, lambda t: v_r[G.slot][:, t * P:(t + 1) * P], h_r[G.slot], GROUP, small[G.slot])
                if G.from_(1):
                    keep(G.before())
            for_groups(act, body)
            keep(Group(NG - 1, NG // 2, 0))
            stage_end(act, 7)

            def keep(G):
                act.wait_ge(S3["delta"], G.g + 1)
                if G.from_(2):
                    act.wait_ge(S3["added_"][G.slot], 64 * G.use)
                s4 = cols4(dvis_s, G)
                for t in range(GROUP):
                    last = S_.mul(dl_r[G.slot][:, t * ROW:t * ROW + D], bank[2][:, t * P:(t + 1) * P], s4[:, t:t + 1])
                last.then_inc(S3["kept"], 1)

            def attrs(G):
                if G.from_(2):
                    act.wait_ge(S3["atT"], G.g - 1)
                S_.copy(small[G.slot][:, 0:GROUP * NSC].rearrange("p (t c) -> p t c", c=NSC),
                       cols4(rec, G, GROUP * REC).rearrange("p (t c) -> p t c", c=REC)[:, :, R_A8:R_A8 + NSC]
                       ).then_inc(S3["at"], 1)

            def body(G):
                attrs(G)
                act.wait_ge(S3["atT"], G.g + 1)
                if G.from_(1):
                    act.wait_ge(S3["fc"], G.g)
                S_.copy(row_r[0][0:NSC, :], bank[3][0:NSC, :]).then_inc(S3["atTs"], 1)
                act.wait_ge(S3["fc"], G.g + 1)
                if G.from_(1):
                    act.wait_ge(S3["w"], G.g)
                S_.activation(z_r[0][0:HID, :], bank[5][0:HID, :], ACT.Silu, scale=1.0 / math.sqrt(NSC)
                             ).then_inc(S3["fcs"], 1)
                if G.from_(1):
                    keep(G.before())
                act.wait_ge(S3["w"], G.g + 1)
                if G.from_(2):
                    act.wait_ge(S3["wst_"][G.slot], 16 * G.use)
                S_.copy(t1_r[G.slot], bank[6][:, :]).then_inc(S3["ws"], 1)
            for_groups(act, body)
            keep(Group(NG - 1, NG // 2, 0))
            stage_end(act, 8)

            def keep(G):
                act.wait_ge(S4["delta"], G.g + 1)
                b4 = cols4(sc_d, G, 16)
                to = cols4(big, G, GROUP * ROW)
                for t in range(GROUP):
                    last = S_.mul(to[:, t * ROW:t * ROW + D], bank[7][:, t * P:(t + 1) * P], b4[:, 4 * t + 1:4 * t + 2])
                last.then_inc(S4["kept"], 1)

            def body(G):
                deviations(G, S4, GROUP)
                if G.from_(2):
                    act.wait_ge(S4["hT"], G.g - 1)
                norm(G, S4, lambda t: rows_r[G.slot][:, t * ROW:t * ROW + D], h_r[G.slot], GROUP, small[G.slot])
                act.wait_ge(S4["hT"], G.g + 1)
                if G.from_(1):
                    act.wait_ge(S4["e"], G.g)
                S_.copy(hT_s, bank[0][:, :]).then_inc(S4["hTs"], 1)
                if G.from_(2):
                    keep(G.before(2))
            for_groups(act, body, peel=4)
            keep(Group(NG - 2, NG // 2 - 1, 1))
            keep(Group(NG - 1, NG // 2, 0))
            act.wait_ge(S4["kept"], NG)
            stage_end(act, 9)
            feed(A, True)
            stage_end(act, 10)

        @block.vector
        def _(dve):
            V = nc.vector
            order = Order(dve, vec)
            link, done, need = order.link, order.done, order.need
            count = [0]

            def ask(ins):
                count[0] += 1
                ins.then_inc(asked, 1)
                dve.wait_ge(answered, count[0])

            link(V.memset(src_i, N))
            link(V.memset(dst_i, N))
            link(V.memset(w_in, 0.0))
            link(V.memset(at4_in, 0.0))
            link(V.memset(at8_in, 0.0))
            V.memset(zeros, 0.0).then_inc(pads_ready, 1)

            dve.wait_ge(consts_ready, 2)
            dve.wait_ge(weights_in, 16 * N_WEIGHTS)
            bg, lbg = cols[:, 1:2], cols[:, 2:3]
            link(V.scalar_tensor_tensor(lbg, bg, 0.01, bg, ALU.mult, ALU.max))
            ask(V.tensor_copy(wts["lbgB"][:, :], lbg.broadcast_to([P, P])))
            link(V.tensor_copy(attw[:, :], bank[1][:, 0:8]))
            for k, w in enumerate(("W1T", "WgT", "L2T")):
                b = {"W1T": 0, "WgT": 1, "L2T": 3}[w]
                link(V.tensor_copy(wts[w][:, :], bank[0][:, b * P:(b + 1) * P]))
            ask(V.tensor_copy(wts["W2T"][:, :], bank[0][:, 2 * P:3 * P]))
            link(V.tensor_scalar(negc1[:, :], bank[1][0:1, 128:256], -1.0, None, ALU.mult))
            link(V.tensor_tensor(wts["K1"][:, :], wts["K1"][:, :], bank[1][:, 128:256], ALU.add))
            link(V.tensor_tensor(wts["K1"][:, :], wts["K1"][:, :], wts["K2"][:, :], ALU.add))
            link(V.tensor_tensor(wts["C"][:, :], wts["C"][:, :], wts["K1"][:, :], ALU.add))
            link(V.tensor_scalar(wts["B1"][:, :], wts["B1"][:, :], 1.0 / math.sqrt(MUL), None, ALU.mult))
            out_scale = 1.0 / math.sqrt(2.0 * MUL) / math.sqrt(16.0)
            for k, b in enumerate(("B2a", "B2b")):
                link(V.tensor_scalar(wts[b][0:32, 0:32], wts[b][0:32, 0:32],
                                     out_scale if k == 0 else out_scale / math.sqrt(3.0), None, ALU.mult))
                for a in range(3):
                    r = slice(32 + 32 * a, 64 + 32 * a)
                    link(V.tensor_scalar(wts[b][r, 32 + a:P:3], wv_st[r, 32 * k:32 * k + 32], out_scale, None, ALU.mult))
            link(V.tensor_scalar(fc2[:, :], fc2[:, :], 1.0 / math.sqrt(HID), None, ALU.mult))

            dve.wait_ge(raw_in, 16 * 10)
            r16 = rec_st.rearrange("p (f c) -> p f c", c=REC)
            link(V.tensor_copy(r16[:, :, R_SRC], src_i))
            link(V.tensor_copy(r16[:, :, R_DST], dst_i))
            link(V.tensor_copy(r16[:, :, R_W], w_in))
            link(V.memset(r16[:, :, R_LAST], 0.0))
            link(V.tensor_copy(r16[:, :, R_A4:R_A4 + 4], at4_in.rearrange("p (f c) -> p f c", c=4)))
            V.tensor_copy(r16[:, :, R_A8:R_A8 + 8], at8_in.rearrange("p (f c) -> p f c", c=8)).then_inc(rec_ready, 1)
            link(V.tensor_copy(key_f, dst_i))

            dve.wait_ge(dvec_in, 48)
            V.tensor_copy(nvh, hw_last.broadcast_to([P, PER_LANE])).then_inc(dense_ready, 1)
            link(V.tensor_scalar(gray, pos[:, :], 1, None, ALU.logical_shift_right))
            link(V.tensor_tensor(gray, gray, pos[:, :], ALU.bitwise_xor))

            def to_int(ap):
                return ap.bitcast(i32)

            def turn_signs(k):
                of, by = (pos[:, :], 30) if k == 0 else (gray, 31 - k)
                link(V.tensor_scalar(flip, of, by, SIGN, ALU.logical_shift_left, ALU.bitwise_and))
                link(V.tensor_tensor(to_int(sort_b[0]), to_int(sort_b[0]), flip, ALU.bitwise_xor))

            def step(bufs, b, dist, ask_pe=False):
                x_ = bufs[b].rearrange("p (n two d) -> p n two d", two=2, d=dist)
                y_ = bufs[1 - b].rearrange("p (n two d) -> p n two d", two=2, d=dist)
                done(V.tensor_tensor(y_[:, :, 0, :], x_[:, :, 0, :], x_[:, :, 1, :], ALU.min))
                ins = V.tensor_tensor(y_[:, :, 1, :], x_[:, :, 0, :], x_[:, :, 1, :], ALU.max)
                if ask_pe:
                    ask(ins)
                else:
                    link(ins)

            def sort(kf):
                m_i = to_int(tmp_g)
                link(V.tensor_scalar(tmp_f, kf, float(-MID), None, ALU.add))
                link(V.scalar_tensor_tensor(tmp_f, tmp_f, -1.0, tmp_f, ALU.mult, ALU.max))
                link(V.tensor_scalar(m_i, tmp_f, float(LEAST), None, ALU.add))
                link(V.scalar_tensor_tensor(to_int(sort_b[0]), m_i, LOG, pos[:, :], ALU.logical_shift_left, ALU.bitwise_or))
                link(V.tensor_scalar(m_i, kf, float(MID), None, ALU.is_lt))
                link(V.scalar_tensor_tensor(to_int(sort_b[0]), m_i, 31, to_int(sort_b[0]), ALU.logical_shift_left, ALU.bitwise_or))
                turn_signs(0)
                for k in range(1, LOG + 1):
                    b = 0
                    if k <= 8:
                        dists = [1 << j for j in range(k - 1, -1, -1)]
                        for d_ in dists:
                            step(sort_b, b, d_)
                            b = 1 - b
                        if b:
                            link(V.tensor_copy(sort_b[0], sort_b[1]))
                    else:
                        for_ask = V.tensor_copy(sort_a[1][:, 0:1], sort_b[0][:, 0:1])
                        ask(for_ask)
                        link(V.tensor_copy(sort_a[0].rearrange("p (q b) -> p b q", b=2),
                                           bank[0][:, 0:F].rearrange("p (b q) -> p b q", b=2)))
                        a = 0
                        for j in range(k - 1, 7, -1):
                            step(sort_a, a, (1 << j) // P, ask_pe=(j == 8))
                            a = 1 - a
                        link(V.tensor_copy(sort_b[0], bank[0][:, 0:F]))
                        for j in range(7, -1, -1):
                            step(sort_b, b, 1 << j)
                            b = 1 - b
                    if k < LOG:
                        turn_signs(k)
                ask(V.tensor_copy(sort_a[1][:, 0:1], sort_b[0][:, 0:1]))
                link(V.tensor_copy(sort_a[0].rearrange("p (q b) -> p b q", b=2),
                                   bank[0][:, 0:F].rearrange("p (b q) -> p b q", b=2)))

            def unpack(edge_idx, n):
                link(V.tensor_scalar(to_int(tmp_g)[:, 0:TILES], to_int(sort_a[0])[:, 0:TILES], (1 << LOG) - 1, None,
                                     ALU.bitwise_and))
                V.tensor_scalar(edge_idx[:, :], to_int(tmp_g)[:, 0:TILES], float(EP - 1), None, ALU.min).then_inc(e_ready, 1)
                s_i = to_int(sort_b[0])[0:LANES, :]
                link(V.tensor_scalar(to_int(tmp_f)[0:LANES, :], s_i, LOG, 0xffff, ALU.logical_shift_right, ALU.bitwise_and))
                link(V.tensor_scalar(fa, to_int(tmp_f)[0:LANES, :], float(-LEAST), None, ALU.add))
                link(V.tensor_scalar(to_int(tmp_f)[0:LANES, :], s_i, 31, None, ALU.logical_shift_right))
                link(V.tensor_scalar(fb, to_int(tmp_f)[0:LANES, :], -2.0, 1.0, ALU.mult, ALU.add))
                link(V.tensor_tensor(fa, fa, fb, ALU.mult))
                V.tensor_scalar(keyl, fa, float(MID), None, ALU.add).then_inc(keys_ready, 1)
                dve.wait_ge(keys_ready, n)

            def to_cols(ins, out, dt_copy=True):
                ask(ins)
                link(V.tensor_copy(out.rearrange("p (q b) -> p b q", b=2),
                                   bank[0][:, 0:TILES].rearrange("p (b q) -> p b q", b=2)))

            def run_flags(k_, p_, n_):
                done(V.tensor_tensor(sprev, k_, p_, ALU.is_equal))
                done(V.tensor_tensor(snext, k_, n_, ALU.is_equal))
                done(V.tensor_scalar(eqp, k_, p_[:, 0:1], None, ALU.is_equal))
                done(V.tensor_scalar(eqn, k_, n_[:, F - 1:F], None, ALU.is_equal))
                link(V.tensor_tensor(isl, k_, n_, ALU.not_equal))

            def carries(n, first, ends_of, z_of, op1, op0, initial, forward):
                link(V.tensor_copy(ends[:, 0:n], ends_of))
                ask(V.tensor_copy(endz[:, 0:n], z_of.broadcast_to([LANES, n])))
                done(V.memset(run[0:n, :], initial))
                link(V.tensor_copy(rows[0:n, 0:2 * LANES], bank[1][0:n, 0:2 * LANES]))
                if forward:
                    ask(V.tensor_tensor_scan(run[0:n, 1:LANES + 1], rows[0:n, LANES:2 * LANES], rows[0:n, 0:LANES],
                                             initial, op0, op1))
                else:
                    ask(V.tensor_tensor_scan(run[0:n, LANES - 1::-1], rows[0:n, 2 * LANES - 1:LANES - 1:-1],
                                             rows[0:n, LANES - 1::-1], initial, op0, op1))
                link(V.tensor_copy(carry[:, 0:n], bank[1][0:LANES, 256:256 + n]))

            def head(ap, h):
                return ap[:, h * F:(h + 1) * F]

            def ends_of(ap, n, c):
                return ap[:, c:n * F:F]

            def run_sums(v, out, n):
                for h in range(n):
                    last = V.tensor_tensor_scan(head(out, h), sprev, head(v, h), 0.0, ALU.mult, ALU.add)
                    done(last)
                need(order.off)
                carries(n, 0, ends_of(out, n, F - 1), eqp[:, F - 1:F], ALU.add, ALU.mult, 0.0, True)
                for h in range(n):
                    done(V.scalar_tensor_tensor(head(out, h), eqp, carry[:, h:h + 1], head(out, h), ALU.mult, ALU.add))
                need(order.off)

            def spread_last(v, out, n):
                for h in range(n):
                    done(V.tensor_tensor_scan(head(out, h)[:, ::-1], snext[:, ::-1], head(v, h)[:, ::-1], 0.0,
                                              ALU.mult, ALU.add))
                need(order.off)
                carries(n, 0, ends_of(out, n, 0), eqn[:, 0:1], ALU.add, ALU.mult, 0.0, False)
                for h in range(n):
                    done(V.scalar_tensor_tensor(head(out, h), eqn, carry[:, h:h + 1], head(out, h), ALU.mult, ALU.add))
                need(order.off)

            def targets(add_idx):
                link(V.tensor_tensor(fa, keyl, trash, ALU.subtract))
                link(V.tensor_tensor(fa, fa, isl, ALU.mult))
                to_cols(V.tensor_tensor(fa, fa, trash, ALU.add), add_idx[:, :])

            sort(key_f)
            unpack(idx["e_d"], 1)
            to_cols(V.tensor_copy(fb, keyl), key_col["dst"][:, :])

            dve.wait_ge(dvec_in, 80)
            for k in range(DBUF):
                done(V.memset(dense[k][:, :, COL_DV], 0.0))
            need(order.off)
            for k in range(NCHUNK):
                d_ = dense[k % DBUF]
                r = slice(k * CHUNK, (k + 1) * CHUNK)
                dve.wait_ge(dense_in[k % DBUF], 16 * (k // DBUF + 1))
                V.tensor_copy(d_[:, :, COL_A], nv1[:, r])
                V.tensor_copy(d_[:, :, COL_B], nv2[:, r])
                V.tensor_copy(d_[:, :, COL_HW], nvh[:, r])
                V.tensor_tensor(d_[:, :, 0:D], d_[:, :, 0:D], over(wts["C"][:, :], CHUNK), ALU.add).then_inc(dense_sum, 1)
            dve.wait_ge(left_in, 48)
            done(V.tensor_copy(left_rows[:, COL_HW:COL_HW + 1], hw_last[0:LEFT, :]))
            done(V.memset(left_rows[:, COL_DV:COL_DV + 1], 0.0))
            done(V.tensor_copy(zeros[0:1, COL_HW:COL_HW + 1], hw_last[0:1, :]))
            V.tensor_tensor(left_rows[:, 0:D], left_rows[:, 0:D], wts["C"][0:LEFT, :], ALU.add).then_inc(left_sum, 1)

            dve.wait_ge(keys_in, 32)
            run_flags(keyl, prevl, nextl)
            link(V.tensor_scalar(to_int(posf), pos[0:LANES, :], SPARE - 1, None, ALU.bitwise_and))
            link(V.tensor_scalar(trash, to_int(posf), float(N + 1), None, ALU.add))
            link(V.tensor_copy(posf, pos[0:LANES, :]))
            targets(idx["add_d"])
            link(V.tensor_scalar(clprev, prevl, float(M - 1), None, ALU.min))
            link(V.tensor_scalar(clnext, nextl, float(M - 1), None, ALU.min))
            V.tensor_scalar(clipl, keyl, float(M - 1), None, ALU.min).then_inc(keys_ready, 1)
            dve.wait_ge(keys_ready, 2)
            to_cols(V.tensor_copy(fb, clipl), key_col["clip"][:, :])
            run_flags(clipl, clprev, clnext)
            link(V.tensor_tensor(fa, posf, isl, ALU.mult))
            spread_last(fa, fb, 1)
            rec3 = rec[:, :].rearrange("p (t c) -> p t c", c=REC)
            dve.wait_ge(R["taken"], NG)
            ask(V.tensor_copy(fa, fb))
            V.tensor_copy(rec3[:, :, R_LAST].rearrange("p (q b) -> p b q", b=2),
                          bank[0][:, 0:TILES].rearrange("p (b q) -> p b q", b=2)).then_inc(recs_ready, 1)
            dve.wait_ge(recs_ready, 1)
            link(V.tensor_scalar(fb, keyl, float(M), None, ALU.is_lt))
            run_sums(fb, fa, 1)
            to_cols(V.tensor_copy(clnext, fa), cnt_col[:, :])
            link(V.tensor_copy(idx["src_d"][:, :], rec3[:, :, R_SRC]))
            link(V.tensor_copy(idx["dst_d"][:, :], rec3[:, :, R_DST]))

            done(V.memset(key_f, float(N)))
            ask(V.memset(tmp_g[:, 0:1], 0.0))
            link(V.tensor_copy(key_f[0:LANES, :], bank[0][0:LANES, 0:F]))
            dve.wait_ge(keys_stored, 96)
            sort(key_f)
            unpack(idx["e_s"], 3)
            to_cols(V.tensor_copy(fb, keyl), key_col["src"][:, :])
            dve.wait_ge(keys_in, 64)
            run_flags(keyl, prevl, nextl)
            targets(idx["add_s"])
            dve.wait_ge(R["taken"], 2 * NG)
            rs = rec_s[:, :].rearrange("p (t c) -> p t c", c=4)
            link(V.tensor_copy(idx["dst_s"][:, :], rs[:, :, R_DST]))
            link(V.tensor_copy(idx["last_s"][:, :], rs[:, :, R_LAST]))
            link(V.memset(big[:, :].rearrange("p (t c) -> p t c", c=ROW)[:, :, D:ROW], 0.0))
            stage_end(dve, 1)

            def statistics(G, S, v, tiles):
                s = small[G.slot]
                for t in range(tiles):
                    done(V.bn_stats(s[:, 16 + 6 * t:22 + 6 * t], v(t)))
                need(order.off)
                plain(dve)
                for t in range(tiles):
                    ins = V.bn_aggr(s[:, 80 + 2 * t:82 + 2 * t], s[:, 16 + 6 * t:22 + 6 * t])
                    if t < tiles - 1:
                        done(ins)
                ins.then_inc(S["var"], 1)

            def scales(G, S, tiles, weight=None):
                s = small[G.slot]
                dve.wait_ge(S["dev"], G.g + 1)
                link(V.reciprocal(s[:, 0:tiles], s[:, 104:104 + tiles]))
                if weight is not None:
                    link(V.tensor_tensor(s[:, 0:tiles], s[:, 0:tiles], weight, ALU.mult))
                V.scalar_tensor_tensor(s[:, 8:8 + tiles], s[:, 80:80 + 2 * tiles:2], -1.0, s[:, 0:tiles],
                                       ALU.mult, ALU.mult).then_inc(S["norm"], 1)

            def matrices(G, S, which):
                dve.wait_ge(S["keys_"][G.slot], 16 * (G.use + 1))
                k = keys_r[G.slot]
                here = t4(k[:, 1:GE + 1])
                done(V.tensor_tensor(t4(sel_r[G.slot]), here, wide(cols4(key_col[which], G)), ALU.is_equal))
                V.tensor_tensor(t4(ind_r[G.slot]), here, wide(k[:, 0:GE:P]), ALU.is_equal).then_inc(S["sel"], 1)

            def chain(G, S, banks, ring_, free, first=(), lag=2):
                dve.wait_ge(S["sums"], G.g + 1)
                if G.from_(2) and free:
                    dve.wait_ge(S[free], G.g - 1)
                for t in range(GROUP):
                    for k, b in enumerate(banks):
                        o = 512 * k
                        if t:
                            before = ring_[G.slot][:, o + t * P - 1:o + t * P]
                        elif G.from_(1):
                            before = ring_[1 - G.slot][:, o + 511:o + 512]
                        else:
                            before = zero_col[:, :]
                        ins = V.scalar_tensor_tensor(ring_[G.slot][:, o + t * P:o + (t + 1) * P],
                                                     ind_r[G.slot][:, t * P:(t + 1) * P], before,
                                                     b[:, t * P:(t + 1) * P], ALU.mult, ALU.add)
                        if t < GROUP - 1 or k < len(banks) - 1:
                            done(ins)
                    if t < GROUP - 1:
                        need(order.off)
                ins.then_inc(S["chained"], 1)
                dve.wait_ge(S["chained"], G.g + 1)

            def front(G):
                dve.wait_ge(S0["rows_"][G.slot], 64 * (G.use + 1))
                r = rows_r[G.slot][:, 0:GROUP * ROW].rearrange("p (t c) -> p t c", c=ROW)
                if G.from_(2):
                    dve.wait_ge(S0["sums"], G.g - 1)
                done(V.tensor_tensor(t4(v_r[G.slot]), r[:, :, 0:D], over(wts["C"][:, :], GROUP), ALU.subtract))
                V.tensor_copy(small[G.slot][:, 64:68], r[:, :, COL_HW]).then_inc(S0["taken"], 1)
                need(order.off)
                statistics(G, S0, lambda t: v_r[G.slot][:, t * P:(t + 1) * P], GROUP)
                dve.wait_ge(S0["keys_"][G.slot], 16 * (G.use + 1))
                k = keys_r[G.slot]
                here = t4(k[:, 1:GE + 1])
                done(V.tensor_tensor(t4(ind_r[G.slot]), here, wide(k[:, 0:GE:P]), ALU.is_equal))
                link(V.tensor_tensor(t4(sel_r[G.slot]), here, wide(cols4(key_col["src"], G)), ALU.is_equal))
                w4 = cols4(rec_s, G, 16).rearrange("p (t c) -> p t c", c=4)[:, :, R_W]
                V.tensor_tensor(t4(selw_r[G.slot]), t4(sel_r[G.slot]), wide(w4), ALU.mult).then_inc(S0["sel"], 1)
                scales(G, S0, GROUP)

            def chains(G):
                dve.wait_ge(S0["sums"], G.g + 1)
                if G.from_(2):
                    dve.wait_ge(S0["delta"], G.g - 1)
                for t in range(GROUP):
                    c = slice(t * P, (t + 1) * P)
                    if t:
                        u0, d0 = uT_r[G.slot][:, t * P - 1:t * P], row_r[G.slot][0:1, t * P - 1:t * P]
                    elif G.from_(1):
                        u0, d0 = uT_r[1 - G.slot][:, 511:512], row_r[1 - G.slot][0:1, 511:512]
                    else:
                        u0, d0 = zero_col[:, :], zero_col[0:1, :]
                    done(V.scalar_tensor_tensor(row_r[G.slot][0:1, c], ind_r[G.slot][0:1, c], d0,
                                                bank[2 + G.slot][0:1, c], ALU.mult, ALU.add))
                    ins = V.scalar_tensor_tensor(uT_r[G.slot][:, c], ind_r[G.slot][:, c], u0, bank[G.slot][:, c],
                                                 ALU.mult, ALU.add)
                    if t < GROUP - 1:
                        link(ins)
                ins.then_inc(S0["chained"], 1)
                dve.wait_ge(S0["chained"], G.g + 1)

            def body(G):
                front(G)
                if G.from_(1):
                    chains(G.before())
            for_groups(dve, body, order)
            chains(Group(NG - 1, NG // 2, 0))
            dve.wait_ge(S0["kept"], NG)
            V.tensor_scalar(dvis_s[:, :], big[:, :].rearrange("p (t c) -> p t c", c=ROW)[:, :, COL_DV],
                            1.0, None, ALU.max).then_inc(roots, 1)
            dve.wait_ge(roots, 2)
            link(V.reciprocal(dvis_s[:, :], dvis_s[:, :]))
            stage_end(dve, 2)
            stage_end(dve, 3)

            def logits(G):
                dve.wait_ge(S1["hh"], G.g + 1)
                done(V.tensor_copy(small[G.slot][:, 112:128], bank[5][:, 0:16]))
                need(order.off)
                V.scalar_tensor_tensor(cols4(al, G, 16), small[G.slot][:, 112:128], 0.2, small[G.slot][:, 112:128],
                                       ALU.mult, ALU.max).then_inc(S1["logits"], 1)

            def body(G):
                dve.wait_ge(S1["rows_"][G.slot], 128 * (G.use + 1))
                if G.from_(2):
                    dve.wait_ge(S1["h"], G.g - 1)
                r = rows_r[G.slot].rearrange("p (t c) -> p t c", c=ROW)
                done(V.tensor_tensor(t4(v8[G.slot]), r[:, :, 0:D], over(wts["K1"][:, :], W8), ALU.subtract))
                done(V.tensor_copy(cols4(sc_s, G, 16).rearrange("p (t c) -> p t c", c=4), r[:, 0:GROUP, D:ROW]))
                V.tensor_copy(cols4(sc_d, G, 16).rearrange("p (t c) -> p t c", c=4), r[:, GROUP:W8, D:ROW]
                              ).then_inc(S1["taken"], 1)
                need(order.off)
                statistics(G, S1, lambda t: v8[G.slot][:, t * P:(t + 1) * P], W8)
                scales(G, S1, W8)
                if G.from_(1):
                    logits(G.before())
            for_groups(dve, body, order)
            logits(Group(NG - 1, NG // 2, 0))
            dve.wait_ge(S1["logits"], NG)
            s4 = sc_s[:, :].rearrange("p (t c) -> p t c", c=4)
            d4 = sc_d[:, :].rearrange("p (t c) -> p t c", c=4)
            V.tensor_scalar(wt_col[:, :], s4[:, :, 3], 1.0, None, ALU.max).then_inc(roots, 1)
            dve.wait_ge(roots, 4)
            link(V.reciprocal(wt_col[:, :], wt_col[:, :]))
            link(V.tensor_scalar(hsc_col[:, :], key_col["dst"][:, :], float(M), None, ALU.is_lt))
            link(V.tensor_tensor(wt_col[:, :], wt_col[:, :], hsc_col[:, :], ALU.mult))
            link(V.tensor_scalar(hsc_col[:, :], cnt_col[:, :], 1.0, None, ALU.max))
            link(V.reciprocal(hsc_col[:, :], hsc_col[:, :]))
            link(V.tensor_tensor(hsc_col[:, :], hsc_col[:, :], d4[:, :, 2], ALU.mult))
            link(V.tensor_tensor(rec3[:, :, R_A4:R_A4 + 4], rec3[:, :, R_A4:R_A4 + 4], wide(s4[:, :, 0], 4), ALU.mult))
            stage_end(dve, 4)

            dve.wait_ge(keys_in, 64 + 48)
            run_flags(keyl, prevl, nextl)
            ask(V.tensor_copy(fb, keyl))
            for k in range(2):
                done(V.tensor_copy(alb[:, 512 * k:512 * (k + 1)], bank[2 + k][0:LANES, :]))
            need(order.off)
            link(V.tensor_scalar(fa, sprev, 1.0, BIG_NUM, ALU.subtract, ALU.mult))
            link(V.tensor_scalar(fb, eqp, 1.0, BIG_NUM, ALU.subtract, ALU.mult))
            for h in range(H):
                done(V.tensor_tensor_scan(head(fw, h), fa, head(alb, h), -BIG_NUM, ALU.add, ALU.max))
            need(order.off)
            carries(H, 0, ends_of(fw, H, F - 1), fb[:, F - 1:F], ALU.max, ALU.add, -BIG_NUM, True)
            for h in range(H):
                done(V.scalar_tensor_tensor(head(fw, h), fb, carry[:, h:h + 1], head(fw, h), ALU.add, ALU.max))
            need(order.off)
            h4 = lambda ap: ap.rearrange("p (h f) -> p h f", h=H)
            link(V.tensor_tensor(h4(fw), h4(fw), over(isl, H), ALU.mult))
            spread_last(fw, bw, H)
            V.tensor_tensor(alb, alb, bw, ALU.subtract).then_inc(exp_asked, 1)
            dve.wait_ge(exp_done, 1)
            run_sums(alb, fw, H)
            link(V.tensor_tensor(h4(fw), h4(fw), over(isl, H), ALU.mult))
            spread_last(fw, bw, H)
            link(V.tensor_scalar(bw, bw, 1e-16, None, ALU.add))
            link(V.reciprocal(bw, bw))
            ask(V.tensor_tensor(tt4, alb, bw, ALU.mult))
            alc = al[:, :].rearrange("p (q b h) -> p h b q", b=2, h=H)
            for h in range(H):
                c0 = (h % 2) * TILES
                link(V.tensor_copy(alc[:, h], bank[2 + h // 2][:, c0:c0 + TILES].rearrange("p (b q) -> p b q", b=2)))
            for s in range(2):
                link(V.memset(dl_r[s].rearrange("p (t c) -> p t c", c=ROW)[:, :, D:ROW], 0.0))
            stage_end(dve, 5)

            def front(G):
                if G.from_(2):
                    dve.wait_ge(S1b["sums"], G.g - 1)
                c = cols4(al, G, 16)
                done(V.tensor_tensor(h_r[G.slot].rearrange("p (a c) -> p a c", c=C),
                                     cols4(big, G, 512).rearrange("p (a c) -> p a c", c=C), wide(c, C), ALU.mult))
                matrices(G, S1b, "dst")

            def leaky(G):
                dve.wait_ge(S1b["biased"], G.g + 1)
                if G.from_(2):
                    dve.wait_ge(S1b["delta"], G.g - 1)
                V.scalar_tensor_tensor(z_r[G.slot], t1_r[G.slot], 0.01, t1_r[G.slot], ALU.mult, ALU.max
                                       ).then_inc(S1b["z"], 1)

            def body(G):
                front(G)
                if G.from_(2):
                    leaky(G.before(2))
                if G.from_(1):
                    chain(G.before(), S1b, [bank[1 - G.slot]], uT_r, "biased")
            for_groups(dve, body, order, peel=4)
            leaky(Group(NG - 2, NG // 2 - 1, 1))
            chain(Group(NG - 1, NG // 2, 0), S1b, [bank[0]], uT_r, "biased")
            leaky(Group(NG - 1, NG // 2, 0))
            dve.wait_ge(S1b["z"], NG)
            stage_end(dve, 6)

            def front(G):
                dve.wait_ge(S2["rows_"][G.slot], 64 * (G.use + 1))
                if G.from_(2):
                    dve.wait_ge(S2["sums"], G.g - 1)
                r = rows_r[G.slot][:, 0:GROUP * ROW].rearrange("p (t c) -> p t c", c=ROW)
                V.tensor_tensor(t4(v_r[G.slot]), r[:, :, 0:D], over(wts["K2"][:, :], GROUP), ALU.subtract
                                ).then_inc(S2["taken"], 1)
                dve.wait_ge(S2["taken"], G.g + 1)
                statistics(G, S2, lambda t: v_r[G.slot][:, t * P:(t + 1) * P], GROUP)
                matrices(G, S2, "clip")
                scales(G, S2, GROUP, cols4(wt_col, G))

            def body(G):
                front(G)
                if G.from_(1):
                    chain(G.before(), S2, [bank[1 - G.slot]], uT_r, "he")
            for_groups(dve, body, order)
            chain(Group(NG - 1, NG // 2, 0), S2, [bank[0]], uT_r, "he")
            stage_end(dve, 7)
            for s in range(2):
                link(V.memset(dl_r[s].rearrange("p (t c) -> p t c", c=ROW)[:, :, D:ROW], 0.0))

            def body(G):
                if G.from_(2):
                    dve.wait_ge(S3["sums"], G.g - 1)
                matrices(G, S3, "src")
                if G.from_(1):
                    chain(G.before(), S3, [bank[1 - G.slot]], uT_r, "delta")
            for_groups(dve, body, order)
            chain(Group(NG - 1, NG // 2, 0), S3, [bank[0]], uT_r, "delta")
            link(V.memset(big[:, :].rearrange("p (t c) -> p t c", c=ROW)[:, :, D:ROW], 0.0))
            stage_end(dve, 8)

            def front(G):
                dve.wait_ge(S4["rows_"][G.slot], 64 * (G.use + 1))
                if G.from_(2):
                    dve.wait_ge(S4["sums"], G.g - 1)
                    dve.wait_ge(S4["h"], G.g - 1)
                statistics(G, S4, lambda t: rows_r[G.slot][:, t * ROW:t * ROW + D], GROUP)
                if G.from_(2):
                    chain2(G.before(2))
                matrices(G, S4, "dst")
                scales(G, S4, GROUP)

            def features(G):
                dve.wait_ge(S4["e"], G.g + 1)
                dve.wait_ge(S4["w_"][G.slot], 16 * (G.use + 1))
                e_ = t4(bank[1 + G.slot][:, :])
                ev = e_[:, :, 32:128].rearrange("p t (i c) -> p t i c", c=MUL)
                y = cols4(rec, G, GROUP * REC).rearrange("p (t c) -> p t c", c=REC)
                w = t4(w_r[G.slot])
                f = feat_r[G.slot].rearrange("p (t k c) -> p t k c", t=GROUP, k=2)
                q = q_t.rearrange("p (t k c) -> p t k c", t=GROUP, k=4)
                tv = t_t.rearrange("p (t i c) -> p t i c", t=GROUP, i=3)
                m3 = m3_t.rearrange("p (t c) -> p t c", c=MUL)

                def many(ap, n):
                    return ap.unsqueeze(2).broadcast_to([P, GROUP, n, MUL])

                def per(ap, n):
                    return ap.unsqueeze(3).broadcast_to([P, GROUP, n, MUL])
                done(V.tensor_tensor(q, many(e_[:, :, 0:32], 4), per(y[:, :, R_A4:R_A4 + 4], 4), ALU.mult))
                done(V.tensor_tensor(tv, ev, per(y[:, :, R_A4 + 1:R_A4 + 4], 3), ALU.mult))
                need(order.off - 1)
                done(V.tensor_tensor(f[:, :, 0, 0:32], q[:, :, 0, :], w[:, :, 0:32], ALU.mult))
                done(V.tensor_tensor(f[:, :, 0, 32:128].rearrange("p t (i c) -> p t i c", c=MUL), q[:, :, 1:4, :],
                                     many(w[:, :, 32:64], 3), ALU.mult))
                need(order.off - 2)
                done(V.tensor_reduce(m3, tv.rearrange("p t i c -> p t c i"), AX.X, ALU.add))
                need(order.off - 1)
                ys = y[:, :, R_A4:R_A4 + 1].unsqueeze(3).broadcast_to([P, GROUP, 3, MUL])
                done(V.tensor_tensor(q[:, :, 0:3, :], ev, ys, ALU.mult))
                need(order.off - 1)
                done(V.tensor_tensor(f[:, :, 1, 0:32], m3, w[:, :, 96:128], ALU.mult))
                need(order.off - 1)
                V.tensor_tensor(f[:, :, 1, 32:128].rearrange("p t (i c) -> p t i c", c=MUL), q[:, :, 0:3, :],
                                many(w[:, :, 64:96], 3), ALU.mult).then_inc(S4["feat"], 1)
                dve.wait_ge(S4["feat"], G.g + 1)

            def chain2(G):
                chain(G, S4, [bank[3 + 2 * G.slot], bank[4 + 2 * G.slot]], uT2_r, "delta")

            def body(G):
                front(G)
                if G.from_(1):
                    features(G.before())
            for_groups(dve, body, order, peel=4)
            features(Group(NG - 1, NG // 2, 0))
            chain2(Group(NG - 2, NG // 2 - 1, 1))
            chain2(Group(NG - 1, NG // 2, 0))
            stage_end(dve, 9)
            stage_end(dve, 10)


N_WEIGHTS = 12 + 2 * H + 1 + 3 + 2 * 4

_INS = ["x", "src", "dst", "edge_attr_4", "edge_attr_8", "edge_weight", "node_vec1", "node_vec1_n2",
        "L0_gnn_weight", "L0_gnn_bias", "L1_gnn_W1", "L1_gnn_b1", "L1_gnn_Wg", "L1_gnn_att_src",
        "L1_gnn_att_dst", "L1_gnn_bias_g", "L1_gnn_W2", "L1_gnn_b2", "L2_gnn_hyperedge_weight",
        "L2_gnn_W", "L2_gnn_b", "L3_gnn_w1_s", "L3_gnn_w1_v", "L3_gnn_Wfc1", "L3_gnn_Wfc2",
        "L3_gnn_w2_s", "L3_gnn_w2_v"]


def kernel(**inputs):
    import numpy as _np
    import concourse.bacc as _bacc
    from concourse import mybir as _mybir
    from concourse.bass_utils import run_bass_kernel_spmd as _run

    nc = _bacc.Bacc("TRN2", target_bir_lowering=False, num_devices=1)
    arrays, args = {}, []
    for name in _INS:
        a = _np.ascontiguousarray(inputs[name])
        arrays[f"in_{name}_dram"] = a
        args.append(nc.dram_tensor(f"in_{name}_dram", a.shape, _mybir.dt.from_np(a.dtype), kind="ExternalInput").ap())
    args.append(nc.dram_tensor("out_0_dram", (TABLE, ROW), _mybir.dt.float32, kind="ExternalOutput").ap())
    build_gnn(nc, *args)
    r = _run(nc, [arrays], core_ids=[0])
    return _np.ascontiguousarray(r.results[0]["out_0_dram"][:N, :D])
```

```python
import math
from contextlib import ExitStack

import concourse.bass as bass
from concourse import mybir

N, E, D = 100000, 25000, 128
M = 20000
H, C = 4, 32
MUL, NSC, HID = 32, 8, 64
P = 128
TILES = math.ceil(E / P)
EP = TILES * P
F = 256
LANES = EP // F
GROUP = 4
NG = TILES // GROUP
GE = GROUP * P
UNROLL = 4
ROW = 132
COL_A, COL_B, COL_HW, COL_DV = 128, 129, 130, 131
SPARE = UNROLL * GROUP * P
TABLE = N + 1 + SPARE
REC = 16
R_SRC, R_DST, R_W, R_LAST, R_A4, R_A8 = 0, 1, 2, 3, 4, 8
LOG = 15
MID = N // 2
LEAST = 256
BIG_NUM = 1.0e30
EPS = 1e-5
PER_LANE = N // P
CHUNK = 11
NCHUNK = PER_LANE // CHUNK
LEFT = N - PER_LANE * P
DBUF = 3
SIGN = -2147483648

fp32 = mybir.dt.float32
i32 = mybir.dt.int32


class Group:

    def __init__(self, step, place):
        self.step, self.place = step, place
        self.g = step * UNROLL + place
        self.slot = place % 2

    def use(self, slots=2):
        return self.step * (UNROLL // slots) + self.place // slots

    def before(self, n=1):
        carry = -((self.place - n) // UNROLL)
        return Group(self.step - carry if carry else self.step, (self.place - n) % UNROLL)

    def after(self):
        return Group(self.step + 1, 0) if self.place == UNROLL - 1 else Group(self.step, self.place + 1)

    def from_(self, n):
        return not isinstance(self.g, int) or self.g >= n


def group(g):
    return Group(g // UNROLL, g % UNROLL)


class Slots:

    def __init__(self, sems, loops):
        self.sems, self.loops, self.start = sems, dict(loops), {}
        self.n = len(sems)
        total = 0
        for name, amount in loops:
            self.start[name] = total
            total += amount

    def of(self, G):
        return self.sems[G.place % self.n]

    def wait(self, eng, name, G):
        k = G.place % self.n
        base = self.start[name] * len(range(k, NG, self.n))
        eng.wait_ge(self.sems[k], (G.use(self.n) + 1) * self.loops[name] + base)

    def wait_all(self, eng, name):
        for k in range(self.n):
            eng.wait_ge(self.sems[k], (self.start[name] + self.loops[name]) * len(range(k, NG, self.n)))


class Order:

    def __init__(self, eng, sem):
        self.eng, self.sem, self.base, self.off = eng, sem, 0, 0

    def done(self, ins):
        self.off += 1
        ins.then_inc(self.sem, 1)
        return self.off

    def need(self, at):
        self.eng.wait_ge(self.sem, self.base + at)

    def link(self, ins):
        self.need(self.done(ins))


def for_groups(eng, body, order=None):
    for g in range(UNROLL):
        start = order.off if order else 0
        body(group(g))
        steady = order.off - start if order else 0
    first = order.off if order else 0
    with eng.Fori(1, NG // UNROLL) as i:
        if order:
            order.base = i * (UNROLL * steady) - UNROLL * steady
            order.off = first
        for place in range(UNROLL):
            body(Group(i, place))
        if order:
            assert order.off == first + UNROLL * steady, (order.off, first, steady)
    if order:
        order.base, order.off = 0, first + (NG // UNROLL - 1) * UNROLL * steady
    assert NG % UNROLL == 1
    body(group(NG - 1))


def build_gnn(nc, x, src, dst, edge_attr_4, edge_attr_8, edge_weight, node_vec1, node_vec1_n2,
              L0_W, L0_b, W1, b1, Wg, att_src, att_dst, bias_g, W2, b2, hw, L2_W, L2_b,
              w1_s, w1_v, Wfc1, Wfc2, w2_s, w2_v, table):
    ALU = mybir.AluOpType
    ACT = mybir.ActivationFunctionType
    AX = mybir.AxisListType

    rec_raw = nc.dram_tensor("rec_raw", (EP, REC), fp32).ap()
    rec_d = nc.dram_tensor("rec_d", (EP, REC), fp32).ap()
    keys_dram = {k: nc.dram_tensor(f"keys_{k}", (EP + 2,), fp32).ap() for k in ("dst", "clip", "src")}
    he_dram = nc.dram_tensor("he", (EP, D), fp32).ap()
    w_dram = nc.dram_tensor("edge_w", (P, TILES * D), fp32).ap()

    ctx = ExitStack()
    with ctx:
        def sb(name, shape, dt=fp32):
            return ctx.enter_context(nc.sbuf_tensor(name, shape, dt))

        def sem(name):
            return ctx.enter_context(nc.semaphore(name))

        bank = [ctx.enter_context(nc.psum_tensor(f"bank{k}", [P, 512], fp32)) for k in range(8)]

        big = sb("big", [P, TILES * ROW])
        work = sb("work", [P, 14000])
        rec = sb("rec", [P, TILES * REC])
        rec_s = sb("rec_s", [P, TILES * 4])
        sc_s = sb("sc_s", [P, TILES * 4])
        sc_d = sb("sc_d", [P, TILES * 4])
        al = sb("al", [P, TILES * H])
        key_col = {k: sb(f"key_{k}", [P, TILES]) for k in ("dst", "clip", "src")}
        cnt_col = sb("cnt_col", [P, TILES])
        wt_col = sb("wt_col", [P, TILES])
        hsc_col = sb("hsc_col", [P, TILES])
        dvis_s = sb("dvis_s", [P, TILES])
        idx = {k: sb(f"idx_{k}", [P, TILES], i32)
               for k in ("e_d", "e_s", "src_d", "dst_d", "add_d", "dst_s", "last_s", "add_s")}
        ident = sb("ident", [P, P])
        pos = sb("pos", [P, F], i32)
        one = sb("one", [1, P])
        zero_col = sb("zero_col", [P, 1])
        eps_col = sb("eps_col", [P, 1])
        edge_mark = sb("edge_mark", [1, 2])
        wts = {k: sb(f"w_{k}", [P, P]) for k in
               ("W0", "W1", "W1T", "Wg", "WgT", "W2", "W2T", "L2", "L2T", "B1", "B2a", "B2b",
                "C", "K1", "K2", "lbgB")}
        att = sb("att", [P, 8])
        attw = sb("attw", [P, 8])
        cols = sb("cols", [P, 4])
        negc1 = sb("negc1", [1, P])
        fc1 = sb("fc1", [NSC, HID])
        fc2 = sb("fc2", [HID, 4 * MUL])
        wv_st = sb("wv_st", [P, 3 * 32])

        def carve(tile, start, size, shape=None, dt=fp32):
            ap = tile[:, start:start + size]
            if dt != fp32:
                ap = ap.bitcast(dt)
            return ap

        rec_st = big[:, 0:4096]
        src_i, dst_i = big[:, 4096:4352].bitcast(i32), big[:, 4352:4608].bitcast(i32)
        wt_in, at4_in, at8_in = big[:, 4608:4864], big[:, 4864:5888], big[:, 5888:7936]
        lane_bufs = [big[:, 8192 + k * F:8192 + (k + 1) * F] for k in range(8)]
        sort_b, sort_a = lane_bufs[0:2], lane_bufs[2:4]
        gray, flip = lane_bufs[4].bitcast(i32), lane_bufs[5].bitcast(i32)
        key_f, tmp_f = lane_bufs[6], lane_bufs[7]
        tmp_g = big[:, 10240:10496]
        DB = 10496
        dense = [big[:, DB + k * CHUNK * ROW:DB + (k + 1) * CHUNK * ROW].rearrange("p (r c) -> p r c", c=ROW)
                 for k in range(DBUF)]
        NV = DB + DBUF * CHUNK * ROW
        nv1, nv2, nvh = (big[:, NV + k * PER_LANE:NV + (k + 1) * PER_LANE] for k in range(3))
        LB = NV + 3 * PER_LANE
        left_rows = big[0:LEFT, LB:LB + ROW]
        zeros = big[:, LB + ROW:LB + ROW + SPARE // P * ROW]
        assert LB + (SPARE // P + 1) * ROW <= TILES * ROW
        hw_last = wv_st[:, 95:96]

        SC = 2400
        wk = [work[0:LANES, SC + k * F:SC + (k + 1) * F] for k in range(15)]
        keyl, prevl, nextl, sprev, snext, eqp, eqn, isl = wk[0:8]
        fa, fb, posf, trash = wk[8:12]
        clipl, clprev, clnext = wk[12:15]
        SC += 15 * F
        ends, endz, carry = (work[0:LANES, SC + 4 * k:SC + 4 * k + 4] for k in range(3))
        rows, run = work[0:4, SC + 16:SC + 272], work[0:4, SC + 272:SC + 372]
        SC += 384
        alb, fw, bw, tt4 = (work[0:LANES, SC + k * H * F:SC + (k + 1) * H * F] for k in range(4))

        weights_in = sem("weights_in")
        consts_ready = sem("consts_ready")
        vec = sem("vec_order")
        asked, answered = sem("pe_asked"), sem("pe_answered")
        pads_ready, raw_in, rec_ready, raw_stored = sem("pads_ready"), sem("raw_in"), sem("rec_ready"), sem("raw_stored")
        dvec_in, dense_ready = sem("dense_vectors_in"), sem("dense_consts")
        dense_in = [sem(f"dense_in{k}") for k in range(DBUF)]
        dense_out = [sem(f"dense_out{k}") for k in range(DBUF)]
        dense_sum = sem("dense_sum")
        left_in, left_sum, left_out = sem("left_in"), sem("left_sum"), sem("left_out")
        keys_ready, keys_stored, keys_in = sem("keys_ready"), sem("keys_stored"), sem("keys_in")
        e_ready = sem("sorted_edges_ready")
        recs_ready, recs_stored = sem("recs_ready"), sem("recs_stored")
        exp_asked, exp_done = sem("exp_asked"), sem("exp_done")
        stage = sem("stage_done")
        roots = sem("roots_ready")

        def stage_end(eng, n):
            eng.sem_inc(stage, 1)
            eng.wait_ge(stage, 5 * n)

        paced = sem("paced")

        def plain(eng):
            eng.sem_inc(paced, 1)

        def loop_sems(name, words):
            out = {}
            for w in words.split():
                out[w] = [sem(f"{name}_{w}{k}") for k in range(2)] if w.endswith("_") else sem(f"{name}_{w}")
            return out

        R = loop_sems("rec", "taken")
        S0 = loop_sems("gcn", "var dev taken norm h sel selw sums chained delta kept")
        A = loop_sems("add", "delta")
        S1 = loop_sems("gat", "var dev taken norm h hT hTs xx xxs hh kept logits")
        S1b = loop_sems("gatsum", "sel sums chained biased z delta kept")
        S2 = loop_sems("hyp", "var dev taken norm h sel sums chained he hes")
        S3 = loop_sems("hypsum", "sel sums chained delta kept at atT atTs fc fcs w ws")
        S4 = loop_sems("tp", "var dev norm h hT hTs e feat sel sums chained delta kept")
        hes_stored = Slots([sem(f"he_stored{k}") for k in range(2)], [("S2", 16)])
        w_stored = Slots([sem(f"w_stored{k}") for k in range(2)], [("S3", 16)])
        w_in = Slots([sem(f"w_in{k}") for k in range(2)], [("S4", 16)])
        rows_in = Slots([sem(f"rows_in{k}") for k in range(UNROLL)],
                        [("P1", 64), ("P2", 64), ("S0", 64), ("S1", 128), ("S2", 64), ("S3", 64), ("S4", 64)])
        added = Slots([sem(f"added{k}") for k in range(UNROLL)], [("A0", 64), ("S1b", 64), ("S3", 64), ("A3", 64)])
        keys_at = Slots([sem(f"keys_at{k}") for k in range(2)],
                        [("S0", 16), ("S1b", 16), ("S2", 16), ("S3", 16), ("S4", 16)])
        idx_taken, idxa_taken = sem("gather_indices_taken"), sem("add_indices_taken")

        def ring(start, size, n=2, dt=fp32):
            out = [work[:, start + k * size:start + (k + 1) * size] for k in range(n)]
            return [o.bitcast(dt) for o in out] if dt != fp32 else out

        W8 = 2 * GROUP
        rows_r = ring(0, GROUP * ROW, UNROLL)
        rows8_r = ring(8544, W8 * ROW, UNROLL)
        idx_r = ring(2112, 8, UNROLL, dt=i32)
        idxa_r = ring(13984, 4, UNROLL, dt=i32)
        small = ring(2144, 128)
        v_r = ring(2400, 512)
        h_r = ring(3424, 512)
        keys_r = ring(4448, GE + 8)
        sel_r = ring(5488, 512)
        ind_r = ring(6512, 512)
        uT_r = ring(7536, 512)
        selw_r = ring(8560, 512)
        dl_r = ring(9584, GROUP * ROW)
        dl4_r = dl_r + ring(0, GROUP * ROW)
        dl4h_r = dl_r + ring(2400, GROUP * ROW)
        z_r = ring(10640, 512)
        t1_r = ring(11664, 512)
        row_r = ring(12688, 512)
        v8 = ring(2400, 1024)
        h8 = ring(4448, 1024)
        hT8 = work[:, 6496:7520]
        xxT8 = work[:, 7520:8544]
        uT2_r = ring(7536, 1024)
        feat_r = ring(9584, 1024)
        q_t = work[:, 11632:12144]
        t_t = work[:, 12144:12528]
        m3_t = work[:, 12528:12656]
        w_r = ring(12656, 512)
        hT_s = work[:, 2400:2912]

        def t4(ap, c=128):
            return ap.rearrange("p (t c) -> p t c", c=c)

        def wide(ap, n=128):
            return ap.unsqueeze(2).broadcast_to([ap.shape[0], ap.shape[1], n])

        def over(ap, n):
            return ap.unsqueeze(1).broadcast_to([ap.shape[0], n, ap.shape[1]])

        def cols4(tile, G, width=4):
            return tile[:, bass.ds(G.g * width, width)] if not isinstance(G.g, int) else tile[:, G.g * width:(G.g + 1) * width]

        def at(ap, G, n):
            return cols4(ap, G, n)

        block = ctx.enter_context(nc.Block())

        SMALL_LOADS = [
            (wts["W0"][:, :], L0_W), (wts["W1"][:, :], W1), (wts["Wg"][:, :], Wg), (wts["W2"][:, :], W2),
            (wts["L2"][:, :], L2_W),
            (wts["C"][:, :], L0_b.partition_broadcast(P)), (wts["K1"][:, :], b2.partition_broadcast(P)),
            (wts["K2"][:, :], L2_b.partition_broadcast(P)),
            (cols[:, 0:1], b1.unsqueeze(1)), (cols[:, 1:2], bias_g.unsqueeze(1)),
            (fc1[:, :], Wfc1), (fc2[:, :], Wfc2),
        ]

        def rows_of(dram, G):
            part = dram[bass.ds(G.g * GE, GE), :] if not isinstance(G.g, int) else dram[G.g * GE:(G.g + 1) * GE, :]
            return part.rearrange("(t p) c -> p t c", p=P)

        def load_keys(sp, G, which, S, name):
            if G.from_(2):
                sp.wait_ge(S["sel"], G.g - 1)
            k = keys_dram[which]
            part = k[bass.ds(G.g * GE, GE + 1)] if not isinstance(G.g, int) else k[G.g * GE:G.g * GE + GE + 1]
            sp.dma_start(keys_r[G.slot][:, 0:GE + 1], part.partition_broadcast(P)).then_inc(keys_at.of(G), 16)

        @block.sync
        def _(sp):
            for to, of in SMALL_LOADS:
                sp.dma_start(to, of).then_inc(weights_in, 16)
            sp.wait_ge(consts_ready, 1)
            n = len(SMALL_LOADS)
            with nc.allow_non_contiguous_dma(reason="small weights"):
                for h in range(H):
                    sp.dma_start(att[C * h:C * h + C, h:h + 1], att_src[0, h, :].unsqueeze(1)).then_inc(weights_in, 16)
                    sp.dma_start(att[C * h:C * h + C, 4 + h:5 + h], att_dst[0, h, :].unsqueeze(1)).then_inc(weights_in, 16)
                    n += 2
                sp.dma_start(wts["B1"][0:32, 0:32], w1_s).then_inc(weights_in, 16)
                n += 1
                for a in range(3):
                    sp.dma_start(wts["B1"][32 + a:P:3, 32 + 32 * a:64 + 32 * a], w1_v).then_inc(weights_in, 16)
                    n += 1
                for k, b in enumerate(("B2a", "B2b")):
                    sp.dma_start(wts[b][0:32, 0:32], w2_s[k]).then_inc(weights_in, 16)
                    n += 1
                    for a in range(3):
                        sp.dma_start(wv_st[32 + 32 * a:64 + 32 * a, 32 * k:32 * k + 32], w2_v[k]).then_inc(weights_in, 16)
                        n += 1
            assert n == N_WEIGHTS

            lane_rows = x[0:P * PER_LANE, :].rearrange("(p r) c -> p r c", r=PER_LANE)
            lane_out = table[0:P * PER_LANE, :].rearrange("(p r) c -> p r c", r=PER_LANE)
            sp.dma_start(nv1, node_vec1[0:P * PER_LANE, 0].rearrange("(p r) -> p r", r=PER_LANE)).then_inc(dvec_in, 16)
            sp.dma_start(nv2, node_vec1_n2[0:P * PER_LANE, 0].rearrange("(p r) -> p r", r=PER_LANE)).then_inc(dvec_in, 16)
            sp.dma_start(hw_last, hw[M - 1:M].partition_broadcast(P)).then_inc(dvec_in, 16)
            full, rest = M // PER_LANE, M % PER_LANE
            sp.wait_ge(dense_ready, 1)
            sp.dma_start(nvh[0:full, :], hw[0:full * PER_LANE].rearrange("(p r) -> p r", r=PER_LANE)).then_inc(dvec_in, 16)
            sp.dma_start(nvh[full:full + 1, 0:rest], hw[full * PER_LANE:M].unsqueeze(0)).then_inc(dvec_in, 16)
            for k in range(NCHUNK + 1):
                if k < NCHUNK:
                    if k >= DBUF:
                        sp.wait_ge(dense_out[k % DBUF], 16 * (k // DBUF))
                    sp.dma_start(dense[k % DBUF][:, :, 0:D], lane_rows[:, k * CHUNK:(k + 1) * CHUNK, :]
                                 ).then_inc(dense_in[k % DBUF], 16)
                if k >= 1:
                    j = k - 1
                    sp.wait_ge(dense_sum, j + 1)
                    sp.dma_start(lane_out[:, j * CHUNK:(j + 1) * CHUNK, :], dense[j % DBUF]
                                 ).then_inc(dense_out[j % DBUF], 16)
            sp.dma_start(left_rows[:, 0:D], x[P * PER_LANE:N, :]).then_inc(left_in, 16)
            sp.dma_start(left_rows[:, COL_A:COL_A + 1], node_vec1[P * PER_LANE:N, :]).then_inc(left_in, 16)
            sp.dma_start(left_rows[:, COL_B:COL_B + 1], node_vec1_n2[P * PER_LANE:N, :]).then_inc(left_in, 16)
            sp.wait_ge(left_sum, 1)
            sp.dma_start(table[P * PER_LANE:N, :], left_rows).then_inc(left_out, 16)
            sp.dma_start(table[N:N + 1, :], zeros[0:1, 0:ROW]).then_inc(left_out, 16)
            sp.dma_start(table[N + 1:TABLE, :].rearrange("(p r) c -> p (r c)", p=P), zeros[:, 0:SPARE // P * ROW]
                         ).then_inc(left_out, 16)
            sp.wait_ge(left_out, 48)
            for k in range(DBUF):
                sp.wait_ge(dense_out[k], 16 * len(range(k, NCHUNK, DBUF)))

            stage_end(sp, 1)

            for_groups(sp, lambda G: load_keys(sp, G, "src", S0, "S0"))
            stage_end(sp, 2)
            stage_end(sp, 3)
            stage_end(sp, 4)
            stage_end(sp, 5)

            for_groups(sp, lambda G: load_keys(sp, G, "dst", S1b, "S1b"))
            stage_end(sp, 6)

            def store(G):
                sp.wait_ge(S2["hes"], G.g + 1)
                sp.dma_start(rows_of(he_dram, G), t4(dl_r[G.slot][:, 0:512])).then_inc(hes_stored.of(G), 16)

            def body(G):
                load_keys(sp, G, "clip", S2, "S2")
                if G.from_(3):
                    store(G.before(3))
            for_groups(sp, body)
            for g in (NG - 3, NG - 2, NG - 1):
                store(group(g))
            hes_stored.wait_all(sp, "S2")
            stage_end(sp, 7)

            def store(G):
                sp.wait_ge(S3["ws"], G.g + 1)
                sp.dma_start(at(w_dram, G, 512), t1_r[G.slot]).then_inc(w_stored.of(G), 16)

            def body(G):
                load_keys(sp, G, "src", S3, "S3")
                if G.from_(1):
                    store(G.before())
            for_groups(sp, body)
            store(group(NG - 1))
            w_stored.wait_all(sp, "S3")
            stage_end(sp, 8)

            def body(G):
                load_keys(sp, G, "dst", S4, "S4")
                if G.from_(2):
                    sp.wait_ge(S4["feat"], G.g - 1)
                sp.dma_start(w_r[G.slot], at(w_dram, G, 512)).then_inc(w_in.of(G), 16)
            for_groups(sp, body)
            stage_end(sp, 9)
            stage_end(sp, 10)

        @block.gpsimd
        def _(pool):
            g_ = nc.gpsimd
            for b in ("B1", "B2a", "B2b"):
                g_.memset(wts[b][:, :], 0.0)
            g_.memset(att[:, :], 0.0)
            g_.memset(wv_st[:, :], 0.0)
            g_.memset(ident[:, :], 0.0).then_inc(consts_ready, 1)
            g_.iota(pos[:, :], pattern=[[1, F]], base=0, channel_multiplier=F)
            g_.memset(one[:, :], 1.0)
            g_.memset(zero_col[:, :], 0.0)
            g_.memset(eps_col[:, :], EPS)
            g_.memset(edge_mark[:, :], -1.0)
            pool.wait_ge(consts_ready, 1)
            g_.affine_select(out=ident[:, :], in_=ident[:, :], compare_op=ALU.not_equal, fill=1.0, base=0,
                             pattern=[[-1, P]], channel_multiplier=1).then_inc(consts_ready, 1)

            taken = {"gather": 0, "add": 0}

            def take_indices(G, kind, of, name, base):
                ring_, done_ = (idx_r, rows_in) if kind == "gather" else (idxa_r, added)
                if G.from_(UNROLL):
                    done_.wait(pool, name, G.before(UNROLL))
                for k, f in enumerate(of):
                    ins = g_.tensor_copy(ring_[G.place][:, 4 * k:4 * k + 4], cols4(f, G))
                ins.then_inc(idx_taken if kind == "gather" else idxa_taken, 1)

            def with_indices(kind, of, name, move):
                base = taken[kind]
                taken[kind] += NG
                counter = idx_taken if kind == "gather" else idxa_taken
                take_indices(group(0), kind, of, name, base)

                def body(G):
                    if not (isinstance(G.g, int) and G.g == NG - 1):
                        take_indices(G.after(), kind, of, name, base)
                    pool.wait_ge(counter, G.g + (1 + base))
                    move(G)
                return body

            def gathers(name, table_ap, of, free, columns=ROW, ring_=rows_r, done_before=0):
                def move(G):
                    if G.from_(UNROLL):
                        pool.wait_ge(free, G.g + (done_before - UNROLL + 1))
                    plain(pool)
                    for k in range(4 * len(of)):
                        g_.indirect_dma_start(ring_[G.place][:, k * columns:(k + 1) * columns], None, table_ap,
                                              bass.IndirectOffsetOnAxis(ap=idx_r[G.place][:, k:k + 1], axis=0)
                                              ).then_inc(rows_in.of(G), 16)
                return with_indices("gather", of, name, move)

            def adds(name, of, ready, ring_=dl4_r, done_before=0):
                def move(G):
                    pool.wait_ge(ready, G.g + (1 + done_before))
                    plain(pool)
                    for k in range(GROUP):
                        g_.indirect_dma_start(table[:, :], bass.IndirectOffsetOnAxis(ap=idxa_r[G.place][:, k:k + 1], axis=0),
                                              ring_[G.place][:, k * ROW:(k + 1) * ROW], None, compute_op=ALU.add
                                              ).then_inc(added.of(G), 16)
                return with_indices("add", of, name, move)

            pool.wait_ge(raw_stored, 16)
            pool.wait_ge(e_ready, 1)
            for_groups(pool, gathers("P1", rec_raw, [idx["e_d"]], R["taken"], REC))
            pool.wait_ge(recs_stored, 16)
            pool.wait_ge(e_ready, 2)
            for_groups(pool, gathers("P2", rec_d, [idx["e_s"]], R["taken"], REC, done_before=NG))
            stage_end(pool, 1)
            for_groups(pool, gathers("S0", table, [idx["dst_s"]], S0["taken"]))
            stage_end(pool, 2)
            for_groups(pool, adds("A0", [idx["add_s"]], A["delta"]))
            added.wait_all(pool, "A0")
            stage_end(pool, 3)
            for_groups(pool, gathers("S1", table, [idx["src_d"], idx["dst_d"]], S1["taken"], ring_=rows8_r))
            stage_end(pool, 4)
            stage_end(pool, 5)
            for_groups(pool, adds("S1b", [idx["add_d"]], S1b["kept"]))
            added.wait_all(pool, "S1b")
            stage_end(pool, 6)
            for_groups(pool, gathers("S2", table, [idx["src_d"]], S2["taken"]))
            stage_end(pool, 7)

            take = gathers("S3", he_dram, [idx["last_s"]], S3["sums"], D)
            add = adds("S3", [idx["add_s"]], S3["kept"], dl4h_r)

            def body(G):
                take(G)
                if G.from_(3):
                    add(G.before(3))
            for_groups(pool, body)
            for g in (NG - 3, NG - 2, NG - 1):
                add(group(g))
            added.wait_all(pool, "S3")
            stage_end(pool, 8)
            for_groups(pool, gathers("S4", table, [idx["src_d"]], S4["h"]))
            stage_end(pool, 9)
            for_groups(pool, adds("A3", [idx["add_d"]], A["delta"], done_before=NG))
            added.wait_all(pool, "A3")
            stage_end(pool, 10)

        @block.tensor
        def _(pe):
            T = nc.tensor
            count = [0]

            def asked_next():
                count[0] += 1
                pe.wait_ge(asked, count[0])

            def flip_blocks(of, cols_of, n_in, width):
                for b in range(2):
                    last = T.transpose(bank[0][0:width, b * n_in:(b + 1) * n_in], cols_of(of, b), ident[0:n_in, 0:n_in])
                last.then_inc(answered, 1)

            lane_blocks = lambda ap, b: ap[:, b * P:(b + 1) * P]
            col_blocks = lambda ap, b: ap[:, b::2]

            def carries(n, row):
                asked_next()
                T.transpose(bank[1][0:n, 0:LANES], ends[:, 0:n], ident[0:LANES, 0:LANES])
                T.transpose(bank[1][0:n, LANES:2 * LANES], endz[:, 0:n], ident[0:LANES, 0:LANES]).then_inc(answered, 1)
                asked_next()
                T.transpose(bank[1][0:LANES, 256:256 + n], row[0:n, :], ident[0:n, 0:n]).then_inc(answered, 1)

            fwd_row, bwd_row = run[:, 0:LANES], run[:, 1:LANES + 1]

            pe.wait_ge(consts_ready, 2)
            pe.wait_ge(weights_in, 16 * N_WEIGHTS)
            asked_next()
            for k, w in enumerate(("W1", "Wg", "W2", "L2")):
                T.transpose(bank[0][:, k * P:(k + 1) * P], wts[w][:, :], ident[:, :])
            T.matmul(bank[1][:, 0:8], wts["Wg"][:, :], att[:, :], start=True, stop=True).then_inc(answered, 1)
            asked_next()
            T.matmul(bank[1][:, 128:256], wts["lbgB"][:, :], wts["W2T"][:, :], start=True, stop=True).then_inc(answered, 1)

            def sort_transposes():
                for k in range(9, LOG + 1):
                    asked_next()
                    flip_blocks(sort_b[0], lane_blocks, P, P)
                    asked_next()
                    flip_blocks(sort_a[(k - 8) % 2], col_blocks, P, P)
                asked_next()
                flip_blocks(sort_b[0], lane_blocks, P, P)

            def to_cols(ap):
                asked_next()
                for b in range(2):
                    last = T.transpose(bank[0][:, b * LANES:(b + 1) * LANES], ap[:, b * P:(b + 1) * P], ident[0:LANES, 0:LANES])
                last.then_inc(answered, 1)

            sort_transposes()
            to_cols(keyl)
            to_cols(fa)
            to_cols(clipl)
            carries(1, bwd_row)
            to_cols(fb)
            carries(1, fwd_row)
            to_cols(fa)
            asked_next()
            for b in range(2):
                last = T.transpose(bank[0][0:LANES, b * P:(b + 1) * P],
                                   rec[:, :].rearrange("p (t c) -> p t c", c=REC)[:, b::2, R_SRC], ident[:, :])
            last.then_inc(answered, 1)
            sort_transposes()
            to_cols(keyl)
            to_cols(fa)
            stage_end(pe, 1)

            def sum_tiles(G, S, rhs, lhs, out, ready):
                pe.wait_ge(S["sel"], G.g + 1)
                if ready:
                    pe.wait_ge(S[ready], G.g + 1)
                if G.from_(2):
                    pe.wait_ge(S["chained"], G.g - 1)
                for t in range(GROUP):
                    last = T.matmul(out[:, t * P:(t + 1) * P], lhs[:, t * P:(t + 1) * P], rhs[:, t * P:(t + 1) * P],
                                    start=True, stop=True)
                return last

            def sums(G):
                pe.wait_ge(S0["selw"], G.g + 1)
                sum_tiles(G, S0, selw_r[G.slot], h_r[G.slot], bank[G.slot], "h")
                for t in range(GROUP):
                    last = T.matmul(bank[2 + G.slot][0:1, t * P:(t + 1) * P], small[G.slot][:, 64 + t:65 + t],
                                    sel_r[G.slot][:, t * P:(t + 1) * P], start=True, stop=True)
                last.then_inc(S0["sums"], 1)

            def delta(G):
                pe.wait_ge(S0["chained"], G.g + 1)
                if G.from_(2):
                    pe.wait_ge(S0["kept"], G.g - 1)
                for t in range(GROUP):
                    T.matmul(bank[4 + G.slot][:, t * P:(t + 1) * P], uT_r[G.slot][:, t * P:(t + 1) * P],
                             wts["W0"][:, :], start=True, stop=True)
                for t in range(GROUP):
                    last = T.matmul(bank[6 + G.slot][:, t:t + 1], row_r[G.slot][0:1, t * P:(t + 1) * P], one[0:1, 0:1],
                                    start=True, stop=True)
                last.then_inc(S0["delta"], 1)

            def body(G):
                sums(G)
                if G.from_(1):
                    delta(G.before())
            for_groups(pe, body)
            delta(group(NG - 1))
            stage_end(pe, 2)
            stage_end(pe, 3)

            def turn(G):
                pe.wait_ge(S1["h"], G.g + 1)
                if G.from_(1):
                    pe.wait_ge(S1["hTs"], G.g)
                for t in range(W8):
                    last = T.transpose(bank[t // 4][:, t % 4 * P:(t % 4 + 1) * P], h8[G.slot][:, t * P:(t + 1) * P], ident[:, :])
                last.then_inc(S1["hT"], 1)

            def first(G):
                pe.wait_ge(S1["hTs"], G.g + 1)
                if G.from_(1):
                    pe.wait_ge(S1["xxs"], G.g)
                for k in range(2):
                    last = T.matmul(bank[2 + k][:, :], wts["W1T"][:, :], hT8[:, k * 512:(k + 1) * 512], start=True, stop=True)
                last.then_inc(S1["xx"], 1)

            def second(G):
                pe.wait_ge(S1["xxs"], G.g + 1)
                if G.from_(1):
                    pe.wait_ge(S1["kept"], G.g)
                    pe.wait_ge(S1["logits"], G.g)
                for t in range(GROUP):
                    T.matmul(bank[4][:, t * P:(t + 1) * P], xxT8[:, t * P:(t + 1) * P], wts["WgT"][:, :], start=True, stop=True)
                for t in range(GROUP):
                    o = bank[5][:, t * H:(t + 1) * H]
                    T.matmul(o, xxT8[:, t * P:(t + 1) * P], attw[:, 0:4], start=True, stop=False)
                    last = T.matmul(o, xxT8[:, 512 + t * P:512 + (t + 1) * P], attw[:, 4:8], start=False, stop=True)
                last.then_inc(S1["hh"], 1)

            def body(G):
                turn(G)
                if G.from_(1):
                    second(G.before())
                first(G)
            for_groups(pe, body)
            second(group(NG - 1))
            stage_end(pe, 4)

            asked_next()
            alc = al[:, :].rearrange("p (t h) -> p t h", h=H)
            for h in range(H):
                for b in range(2):
                    c0 = (h % 2) * F + b * P
                    last = T.transpose(bank[2 + h // 2][0:LANES, c0:c0 + P], alc[:, b::2, h], ident[:, :])
            last.then_inc(answered, 1)
            carries(H, fwd_row)
            carries(H, bwd_row)
            carries(H, fwd_row)
            carries(H, bwd_row)
            asked_next()
            for h in range(H):
                for b in range(2):
                    c0 = (h % 2) * TILES + b * LANES
                    last = T.transpose(bank[2 + h // 2][:, c0:c0 + LANES], tt4[:, h * F + b * P:h * F + (b + 1) * P],
                                       ident[0:LANES, 0:LANES])
            last.then_inc(answered, 1)
            stage_end(pe, 5)

            def sums(G):
                sum_tiles(G, S1b, sel_r[G.slot], h_r[G.slot], bank[G.slot], None).then_inc(S1b["sums"], 1)

            def delta(G):
                pe.wait_ge(S1b["z"], G.g + 1)
                if G.from_(2):
                    pe.wait_ge(S1b["kept"], G.g - 1)
                for t in range(GROUP):
                    o = bank[4 + G.slot][:, t * P:(t + 1) * P]
                    T.matmul(o, one[0:1, :], negc1[0:1, :], start=True, stop=False)
                    last = T.matmul(o, z_r[G.slot][:, t * P:(t + 1) * P], wts["W2T"][:, :], start=False, stop=True)
                last.then_inc(S1b["delta"], 1)

            def body(G):
                sums(G)
                if G.from_(2):
                    delta(G.before(2))
            for_groups(pe, body)
            delta(group(NG - 2))
            delta(group(NG - 1))
            stage_end(pe, 6)

            def sums(G):
                sum_tiles(G, S2, sel_r[G.slot], h_r[G.slot], bank[G.slot], "h").then_inc(S2["sums"], 1)

            def turn(G):
                pe.wait_ge(S2["chained"], G.g + 1)
                if G.from_(2):
                    pe.wait_ge(S2["hes"], G.g - 1)
                for t in range(GROUP):
                    last = T.transpose(bank[4 + G.slot][:, t * P:(t + 1) * P], uT_r[G.slot][:, t * P:(t + 1) * P], ident[:, :])
                last.then_inc(S2["he"], 1)

            def body(G):
                sums(G)
                if G.from_(1):
                    turn(G.before())
            for_groups(pe, body)
            turn(group(NG - 1))
            stage_end(pe, 7)

            def sums(G):
                rows_in.wait(pe, "S3", G)
                sum_tiles(G, S3, sel_r[G.slot], rows_r[G.place], bank[G.slot], None).then_inc(S3["sums"], 1)

            def delta(G):
                pe.wait_ge(S3["chained"], G.g + 1)
                if G.from_(1):
                    pe.wait_ge(S3["kept"], G.g)
                for t in range(GROUP):
                    last = T.matmul(bank[2][:, t * P:(t + 1) * P], uT_r[G.slot][:, t * P:(t + 1) * P],
                                    wts["L2T"][:, :], start=True, stop=True)
                last.then_inc(S3["delta"], 1)

            def net_in(G):
                pe.wait_ge(S3["at"], G.g + 1)
                for t in range(GROUP):
                    last = T.transpose(bank[3][0:NSC, t * P:(t + 1) * P], small[G.slot][:, t * NSC:(t + 1) * NSC], ident[:, :])
                last.then_inc(S3["atT"], 1)

            def net_mid(G):
                pe.wait_ge(S3["atTs"], G.g + 1)
                T.matmul(bank[5][0:HID, :], fc1[:, :], row_r[0][0:NSC, :], start=True, stop=True).then_inc(S3["fc"], 1)

            def net_out(G):
                pe.wait_ge(S3["fcs"], G.g + 1)
                if G.from_(1):
                    pe.wait_ge(S3["ws"], G.g)
                for t in range(GROUP):
                    last = T.matmul(bank[6][:, t * P:(t + 1) * P], z_r[0][0:HID, t * P:(t + 1) * P], fc2[:, :],
                                    start=True, stop=True)
                last.then_inc(S3["w"], 1)

            def body(G):
                net_in(G)
                sums(G)
                net_mid(G)
                if G.from_(1):
                    delta(G.before())
                net_out(G)
            for_groups(pe, body)
            delta(group(NG - 1))
            stage_end(pe, 8)

            def turn(G):
                pe.wait_ge(S4["h"], G.g + 1)
                if G.from_(1):
                    pe.wait_ge(S4["hTs"], G.g)
                for t in range(GROUP):
                    last = T.transpose(bank[0][:, t * P:(t + 1) * P], h_r[G.slot][:, t * P:(t + 1) * P], ident[:, :])
                last.then_inc(S4["hT"], 1)

            def linear(G):
                pe.wait_ge(S4["hTs"], G.g + 1)
                if G.from_(2):
                    pe.wait_ge(S4["feat"], G.g - 1)
                for t in range(GROUP):
                    last = T.matmul(bank[1 + G.slot][:, t * P:(t + 1) * P], hT_s[:, t * P:(t + 1) * P], wts["B1"][:, :],
                                    start=True, stop=True)
                last.then_inc(S4["e"], 1)

            def sums(G):
                pe.wait_ge(S4["feat"], G.g + 1)
                pe.wait_ge(S4["sel"], G.g + 1)
                if G.from_(2):
                    pe.wait_ge(S4["chained"], G.g - 1)
                f = feat_r[G.slot].rearrange("p (t k c) -> p t k c", t=GROUP, k=2)
                for k in range(2):
                    for t in range(GROUP):
                        last = T.matmul(bank[3 + 2 * G.slot + k][:, t * P:(t + 1) * P], f[:, t, k, :],
                                        sel_r[G.slot][:, t * P:(t + 1) * P], start=True, stop=True)
                last.then_inc(S4["sums"], 1)

            def delta(G):
                pe.wait_ge(S4["chained"], G.g + 1)
                if G.from_(1):
                    pe.wait_ge(S4["kept"], G.g)
                for t in range(GROUP):
                    o = bank[7][:, t * P:(t + 1) * P]
                    T.matmul(o, uT2_r[G.slot][:, t * P:(t + 1) * P], wts["B2a"][:, :], start=True, stop=False)
                    last = T.matmul(o, uT2_r[G.slot][:, 512 + t * P:512 + (t + 1) * P], wts["B2b"][:, :], start=False, stop=True)
                last.then_inc(S4["delta"], 1)

            def body(G):
                turn(G)
                if G.from_(1):
                    sums(G.before())
                linear(G)
                if G.from_(2):
                    delta(G.before(2))
            for_groups(pe, body)
            sums(group(NG - 1))
            delta(group(NG - 2))
            delta(group(NG - 1))
            stage_end(pe, 9)
            stage_end(pe, 10)

        @block.scalar
        def _(act):
            S_ = nc.scalar

            act.wait_ge(pads_ready, 1)
            full, rest = E // F, E % F
            for to, of, c in ((src_i, src, 1), (dst_i, dst, 1), (wt_in, edge_weight, 1)):
                act.dma_start(to[0:full, :], of[0:full * F].rearrange("(q f) -> q f", f=F)).then_inc(raw_in, 16)
                act.dma_start(to[full:full + 1, 0:rest], of[full * F:E].unsqueeze(0)).then_inc(raw_in, 16)
            for to, of, c in ((at4_in, edge_attr_4, 4), (at8_in, edge_attr_8, 8)):
                act.dma_start(to[0:full, :], of[0:full * F, :].rearrange("(q f) c -> q (f c)", f=F)).then_inc(raw_in, 16)
                act.dma_start(to[full:full + 1, 0:rest * c], of[full * F:E, :].rearrange("(q f) c -> q (f c)", q=1)
                              ).then_inc(raw_in, 16)
            act.wait_ge(rec_ready, 1)
            act.dma_start(rec_raw.rearrange("(q f) c -> q (f c)", f=F), rec_st[0:LANES, :]).then_inc(raw_stored, 16)
            act.wait_ge(raw_stored, 16)

            def keep_records(name, to, n):
                def body(G):
                    rows_in.wait(act, name, G)
                    S_.copy(cols4(to, G, 4 * n).rearrange("p (t c) -> p t c", c=n),
                           rows_r[G.place][:, 0:4 * REC].rearrange("p (t c) -> p t c", c=REC)[:, :, 0:n]
                           ).then_inc(R["taken"], 1)
                for_groups(act, body)

            keep_records("P1", rec, REC)

            def exchange_keys(which, n_keys, n_done):
                act.wait_ge(keys_ready, n_keys)
                k = keys_dram[which]
                of = clipl if which == "clip" else keyl
                act.dma_start(k[1:EP + 1].rearrange("(q f) -> q f", f=F), of).then_inc(keys_stored, 16)
                act.dma_start(k[0:1].unsqueeze(0), edge_mark[0:1, 0:1]).then_inc(keys_stored, 16)
                act.dma_start(k[EP + 1:EP + 2].unsqueeze(0), edge_mark[0:1, 1:2]).then_inc(keys_stored, 16)
                act.wait_ge(keys_stored, 48 * n_done)

            def neighbours(which, n):
                k = keys_dram[which]
                act.dma_start(prevl, k[0:EP].rearrange("(q f) -> q f", f=F)).then_inc(keys_in, 16)
                act.dma_start(nextl, k[2:EP + 2].rearrange("(q f) -> q f", f=F)).then_inc(keys_in, 16)
                act.wait_ge(keys_in, 32 * n)

            exchange_keys("dst", 1, 1)
            neighbours("dst", 1)
            exchange_keys("clip", 2, 2)
            act.wait_ge(recs_ready, 1)
            act.dma_start(rec_d.rearrange("(t p) c -> p t c", p=P), rec[:, :].rearrange("p (t c) -> p t c", c=REC)
                          ).then_inc(recs_stored, 16)
            act.wait_ge(recs_stored, 16)
            exchange_keys("src", 3, 3)
            neighbours("src", 2)
            keep_records("P2", rec_s, 4)
            act.wait_ge(R["taken"], 2 * NG)
            stage_end(act, 1)

            def deviations(G, S, tiles):
                act.wait_ge(S["var"], G.g + 1)
                s = small[G.slot]
                S_.activation(s[:, 104:104 + tiles], s[:, 81:81 + 2 * tiles:2], ACT.Sqrt, bias=eps_col[:, :]
                             ).then_inc(S["dev"], 1)

            def norm(G, S, v, h, tiles, stat):
                act.wait_ge(S["norm"], G.g + 1)
                for t in range(tiles):
                    last = S_.activation(h[:, t * P:(t + 1) * P], v(t), ACT.Relu, bias=stat[:, 8 + t:9 + t],
                                        scale=stat[:, t:t + 1])
                last.then_inc(S["h"], 1)

            def keep(G):
                act.wait_ge(S0["delta"], G.g + 1)
                to = cols4(big, G, GROUP * ROW).rearrange("p (t c) -> p t c", c=ROW)
                S_.copy(to[:, :, 0:D], t4(bank[4 + G.slot][:, :]))
                S_.copy(to[:, :, COL_DV], bank[6 + G.slot][:, 0:GROUP]).then_inc(S0["kept"], 1)

            def weigh(G):
                act.wait_ge(S0["sel"], G.g + 1)
                w4 = cols4(rec_s, G, 16)
                for t in range(GROUP):
                    c = slice(t * P, (t + 1) * P)
                    last = S_.mul(selw_r[G.slot][:, c], sel_r[G.slot][:, c], w4[:, 4 * t + R_W:4 * t + R_W + 1])
                last.then_inc(S0["selw"], 1)

            def body(G):
                deviations(G, S0, GROUP)
                if G.from_(2):
                    act.wait_ge(S0["sums"], G.g - 1)
                weigh(G)
                norm(G, S0, lambda t: v_r[G.slot][:, t * P:(t + 1) * P], h_r[G.slot], GROUP, small[G.slot])
                if G.from_(2):
                    keep(G.before(2))
            for_groups(act, body)
            keep(group(NG - 2))
            keep(group(NG - 1))
            act.wait_ge(roots, 1)
            S_.activation(dvis_s[:, :], dvis_s[:, :], ACT.Sqrt).then_inc(roots, 1)
            stage_end(act, 2)

            def feed(name):
                def body(G):
                    if G.from_(UNROLL):
                        added.wait(act, name, G.before(UNROLL))
                    S_.copy(dl4_r[G.place], cols4(big, G, GROUP * ROW)).then_inc(A["delta"], 1)
                for_groups(act, body)
            feed("A0")
            stage_end(act, 3)

            def keep(G):
                act.wait_ge(S1["hh"], G.g + 1)
                S_.copy(cols4(big, G, 512), bank[4][:, :]).then_inc(S1["kept"], 1)

            def bias(G):
                act.wait_ge(S1["xx"], G.g + 1)
                for k in range(2):
                    last = S_.activation(xxT8[:, k * 512:(k + 1) * 512], bank[2 + k][:, :], ACT.Identity, bias=cols[:, 0:1])
                last.then_inc(S1["xxs"], 1)

            def body(G):
                deviations(G, S1, W8)
                if G.from_(2):
                    act.wait_ge(S1["hT"], G.g - 1)
                norm(G, S1, lambda t: v8[G.slot][:, t * P:(t + 1) * P], h8[G.slot], W8, small[G.slot])
                if G.from_(2):
                    keep(G.before(2))
                if G.from_(1):
                    bias(G.before())
                act.wait_ge(S1["hT"], G.g + 1)
                for k in range(2):
                    last = S_.copy(hT8[:, k * 512:(k + 1) * 512], bank[k][:, :])
                last.then_inc(S1["hTs"], 1)
            for_groups(act, body)
            keep(group(NG - 2))
            bias(group(NG - 1))
            keep(group(NG - 1))
            act.wait_ge(roots, 3)
            S_.activation(wt_col[:, :], wt_col[:, :], ACT.Sqrt).then_inc(roots, 1)
            act.wait_ge(S1["kept"], NG)
            stage_end(act, 4)

            act.dma_start(keyl, keys_dram["dst"][1:EP + 1].rearrange("(q f) -> q f", f=F)).then_inc(keys_in, 16)
            neighbours_again = keys_dram["dst"]
            act.dma_start(prevl, neighbours_again[0:EP].rearrange("(q f) -> q f", f=F)).then_inc(keys_in, 16)
            act.dma_start(nextl, neighbours_again[2:EP + 2].rearrange("(q f) -> q f", f=F)).then_inc(keys_in, 16)
            act.wait_ge(keys_in, 32 * 2 + 48)
            act.wait_ge(exp_asked, 1)
            S_.activation(alb, alb, ACT.Exp).then_inc(exp_done, 1)
            act.wait_ge(exp_done, 1)
            stage_end(act, 5)

            def biased(G):
                act.wait_ge(S1b["chained"], G.g + 1)
                if G.from_(2):
                    act.wait_ge(S1b["z"], G.g - 1)
                S_.activation(t1_r[G.slot], uT_r[G.slot], ACT.Identity, bias=cols[:, 1:2]).then_inc(S1b["biased"], 1)

            def keep(G):
                act.wait_ge(S1b["delta"], G.g + 1)
                if G.from_(UNROLL):
                    added.wait(act, "S1b", G.before(UNROLL))
                S_.copy(dl4_r[G.place].rearrange("p (t c) -> p t c", c=ROW)[:, :, 0:D], t4(bank[4 + G.slot][:, :])
                       ).then_inc(S1b["kept"], 1)

            def body(G):
                if G.from_(1):
                    biased(G.before())
                if G.from_(2):
                    keep(G.before(2))
            for_groups(act, body)
            biased(group(NG - 1))
            keep(group(NG - 2))
            keep(group(NG - 1))
            stage_end(act, 6)

            def keep(G):
                act.wait_ge(S2["he"], G.g + 1)
                if G.from_(2):
                    hes_stored.wait(act, "S2", G.before(2))
                s4 = cols4(hsc_col, G)
                for t in range(GROUP):
                    last = S_.mul(dl_r[G.slot][:, t * P:(t + 1) * P], bank[4 + G.slot][:, t * P:(t + 1) * P], s4[:, t:t + 1])
                last.then_inc(S2["hes"], 1)

            def body(G):
                deviations(G, S2, GROUP)
                if G.from_(2):
                    act.wait_ge(S2["sums"], G.g - 1)
                norm(G, S2, lambda t: v_r[G.slot][:, t * P:(t + 1) * P], h_r[G.slot], GROUP, small[G.slot])
                if G.from_(2):
                    keep(G.before(2))
            for_groups(act, body)
            keep(group(NG - 2))
            keep(group(NG - 1))
            stage_end(act, 7)

            def keep(G):
                act.wait_ge(S3["delta"], G.g + 1)
                if G.from_(UNROLL):
                    added.wait(act, "S3", G.before(UNROLL))
                s4 = cols4(dvis_s, G)
                for t in range(GROUP):
                    last = S_.mul(dl4h_r[G.place][:, t * ROW:t * ROW + D], bank[2][:, t * P:(t + 1) * P], s4[:, t:t + 1])
                last.then_inc(S3["kept"], 1)

            def attrs(G):
                if G.from_(2):
                    act.wait_ge(S3["atT"], G.g - 1)
                S_.copy(small[G.slot][:, 0:GROUP * NSC].rearrange("p (t c) -> p t c", c=NSC),
                       cols4(rec, G, GROUP * REC).rearrange("p (t c) -> p t c", c=REC)[:, :, R_A8:R_A8 + NSC]
                       ).then_inc(S3["at"], 1)

            def body(G):
                attrs(G)
                act.wait_ge(S3["atT"], G.g + 1)
                if G.from_(1):
                    act.wait_ge(S3["fc"], G.g)
                S_.copy(row_r[0][0:NSC, :], bank[3][0:NSC, :]).then_inc(S3["atTs"], 1)
                act.wait_ge(S3["fc"], G.g + 1)
                if G.from_(1):
                    act.wait_ge(S3["w"], G.g)
                S_.activation(z_r[0][0:HID, :], bank[5][0:HID, :], ACT.Silu, scale=1.0 / math.sqrt(NSC)
                             ).then_inc(S3["fcs"], 1)
                if G.from_(1):
                    keep(G.before())
                act.wait_ge(S3["w"], G.g + 1)
                if G.from_(2):
                    w_stored.wait(act, "S3", G.before(2))
                S_.copy(t1_r[G.slot], bank[6][:, :]).then_inc(S3["ws"], 1)
            for_groups(act, body)
            keep(group(NG - 1))
            stage_end(act, 8)

            def keep(G):
                act.wait_ge(S4["delta"], G.g + 1)
                b4 = cols4(sc_d, G, 16)
                to = cols4(big, G, GROUP * ROW)
                for t in range(GROUP):
                    last = S_.mul(to[:, t * ROW:t * ROW + D], bank[7][:, t * P:(t + 1) * P], b4[:, 4 * t + 1:4 * t + 2])
                last.then_inc(S4["kept"], 1)

            def body(G):
                deviations(G, S4, GROUP)
                if G.from_(2):
                    act.wait_ge(S4["hT"], G.g - 1)
                norm(G, S4, lambda t: rows_r[G.place][:, t * ROW:t * ROW + D], h_r[G.slot], GROUP, small[G.slot])
                act.wait_ge(S4["hT"], G.g + 1)
                if G.from_(1):
                    act.wait_ge(S4["e"], G.g)
                S_.copy(hT_s, bank[0][:, :]).then_inc(S4["hTs"], 1)
                if G.from_(2):
                    keep(G.before(2))
            for_groups(act, body)
            keep(group(NG - 2))
            keep(group(NG - 1))
            act.wait_ge(S4["kept"], NG)
            stage_end(act, 9)
            feed("A3")
            stage_end(act, 10)

        @block.vector
        def _(dve):
            V = nc.vector
            order = Order(dve, vec)
            link, done, need = order.link, order.done, order.need
            count = [0]

            def ask(ins):
                count[0] += 1
                ins.then_inc(asked, 1)
                dve.wait_ge(answered, count[0])

            link(V.memset(src_i, N))
            link(V.memset(dst_i, N))
            link(V.memset(wt_in, 0.0))
            link(V.memset(at4_in, 0.0))
            link(V.memset(at8_in, 0.0))
            V.memset(zeros, 0.0).then_inc(pads_ready, 1)

            dve.wait_ge(consts_ready, 2)
            dve.wait_ge(weights_in, 16 * N_WEIGHTS)
            bg, lbg = cols[:, 1:2], cols[:, 2:3]
            link(V.scalar_tensor_tensor(lbg, bg, 0.01, bg, ALU.mult, ALU.max))
            ask(V.tensor_copy(wts["lbgB"][:, :], lbg.broadcast_to([P, P])))
            link(V.tensor_copy(attw[:, :], bank[1][:, 0:8]))
            for k, w in enumerate(("W1T", "WgT", "L2T")):
                b = {"W1T": 0, "WgT": 1, "L2T": 3}[w]
                link(V.tensor_copy(wts[w][:, :], bank[0][:, b * P:(b + 1) * P]))
            ask(V.tensor_copy(wts["W2T"][:, :], bank[0][:, 2 * P:3 * P]))
            link(V.tensor_scalar(negc1[:, :], bank[1][0:1, 128:256], -1.0, None, ALU.mult))
            link(V.tensor_tensor(wts["K1"][:, :], wts["K1"][:, :], bank[1][:, 128:256], ALU.add))
            link(V.tensor_tensor(wts["K1"][:, :], wts["K1"][:, :], wts["K2"][:, :], ALU.add))
            link(V.tensor_tensor(wts["C"][:, :], wts["C"][:, :], wts["K1"][:, :], ALU.add))
            link(V.tensor_scalar(wts["B1"][:, :], wts["B1"][:, :], 1.0 / math.sqrt(MUL), None, ALU.mult))
            out_scale = 1.0 / math.sqrt(2.0 * MUL) / math.sqrt(16.0)
            for k, b in enumerate(("B2a", "B2b")):
                link(V.tensor_scalar(wts[b][0:32, 0:32], wts[b][0:32, 0:32],
                                     out_scale if k == 0 else out_scale / math.sqrt(3.0), None, ALU.mult))
                for a in range(3):
                    r = slice(32 + 32 * a, 64 + 32 * a)
                    link(V.tensor_scalar(wts[b][r, 32 + a:P:3], wv_st[r, 32 * k:32 * k + 32], out_scale, None, ALU.mult))
            link(V.tensor_scalar(fc2[:, :], fc2[:, :], 1.0 / math.sqrt(HID), None, ALU.mult))

            dve.wait_ge(raw_in, 16 * 10)
            r16 = rec_st.rearrange("p (f c) -> p f c", c=REC)
            link(V.tensor_copy(r16[:, :, R_SRC], src_i))
            link(V.tensor_copy(r16[:, :, R_DST], dst_i))
            link(V.tensor_copy(r16[:, :, R_W], wt_in))
            link(V.memset(r16[:, :, R_LAST], 0.0))
            link(V.tensor_copy(r16[:, :, R_A4:R_A4 + 4], at4_in.rearrange("p (f c) -> p f c", c=4)))
            V.tensor_copy(r16[:, :, R_A8:R_A8 + 8], at8_in.rearrange("p (f c) -> p f c", c=8)).then_inc(rec_ready, 1)
            link(V.tensor_copy(key_f, dst_i))

            dve.wait_ge(dvec_in, 48)
            V.tensor_copy(nvh, hw_last.broadcast_to([P, PER_LANE])).then_inc(dense_ready, 1)
            link(V.tensor_scalar(gray, pos[:, :], 1, None, ALU.logical_shift_right))
            link(V.tensor_tensor(gray, gray, pos[:, :], ALU.bitwise_xor))

            def to_int(ap):
                return ap.bitcast(i32)

            def turn_signs(k):
                of, by = (pos[:, :], 30) if k == 0 else (gray, 31 - k)
                link(V.tensor_scalar(flip, of, by, SIGN, ALU.logical_shift_left, ALU.bitwise_and))
                link(V.tensor_tensor(to_int(sort_b[0]), to_int(sort_b[0]), flip, ALU.bitwise_xor))

            def step(bufs, b, dist, ask_pe=False):
                x_ = bufs[b].rearrange("p (n two d) -> p n two d", two=2, d=dist)
                y_ = bufs[1 - b].rearrange("p (n two d) -> p n two d", two=2, d=dist)
                done(V.tensor_tensor(y_[:, :, 0, :], x_[:, :, 0, :], x_[:, :, 1, :], ALU.min))
                ins = V.tensor_tensor(y_[:, :, 1, :], x_[:, :, 0, :], x_[:, :, 1, :], ALU.max)
                if ask_pe:
                    ask(ins)
                else:
                    link(ins)

            def sort(kf):
                m_i = to_int(tmp_g)
                link(V.tensor_scalar(tmp_f, kf, float(-MID), None, ALU.add))
                link(V.scalar_tensor_tensor(tmp_f, tmp_f, -1.0, tmp_f, ALU.mult, ALU.max))
                link(V.tensor_scalar(m_i, tmp_f, float(LEAST), None, ALU.add))
                link(V.scalar_tensor_tensor(to_int(sort_b[0]), m_i, LOG, pos[:, :], ALU.logical_shift_left, ALU.bitwise_or))
                link(V.tensor_scalar(m_i, kf, float(MID), None, ALU.is_lt))
                link(V.scalar_tensor_tensor(to_int(sort_b[0]), m_i, 31, to_int(sort_b[0]), ALU.logical_shift_left, ALU.bitwise_or))
                turn_signs(0)
                for k in range(1, LOG + 1):
                    b = 0
                    if k <= 8:
                        dists = [1 << j for j in range(k - 1, -1, -1)]
                        for d_ in dists:
                            step(sort_b, b, d_)
                            b = 1 - b
                        if b:
                            link(V.tensor_copy(sort_b[0], sort_b[1]))
                    else:
                        for_ask = V.tensor_copy(sort_a[1][:, 0:1], sort_b[0][:, 0:1])
                        ask(for_ask)
                        link(V.tensor_copy(sort_a[0].rearrange("p (q b) -> p b q", b=2),
                                           bank[0][:, 0:F].rearrange("p (b q) -> p b q", b=2)))
                        a = 0
                        for j in range(k - 1, 7, -1):
                            step(sort_a, a, (1 << j) // P, ask_pe=(j == 8))
                            a = 1 - a
                        link(V.tensor_copy(sort_b[0], bank[0][:, 0:F]))
                        for j in range(7, -1, -1):
                            step(sort_b, b, 1 << j)
                            b = 1 - b
                    if k < LOG:
                        turn_signs(k)
                ask(V.tensor_copy(sort_a[1][:, 0:1], sort_b[0][:, 0:1]))
                link(V.tensor_copy(sort_a[0].rearrange("p (q b) -> p b q", b=2),
                                   bank[0][:, 0:F].rearrange("p (b q) -> p b q", b=2)))

            def unpack(edge_idx, n):
                link(V.tensor_scalar(to_int(tmp_g)[:, 0:TILES], to_int(sort_a[0])[:, 0:TILES], (1 << LOG) - 1, None,
                                     ALU.bitwise_and))
                V.tensor_scalar(edge_idx[:, :], to_int(tmp_g)[:, 0:TILES], float(EP - 1), None, ALU.min).then_inc(e_ready, 1)
                s_i = to_int(sort_b[0])[0:LANES, :]
                link(V.tensor_scalar(to_int(tmp_f)[0:LANES, :], s_i, LOG, 0xffff, ALU.logical_shift_right, ALU.bitwise_and))
                link(V.tensor_scalar(fa, to_int(tmp_f)[0:LANES, :], float(-LEAST), None, ALU.add))
                link(V.tensor_scalar(to_int(tmp_f)[0:LANES, :], s_i, 31, None, ALU.logical_shift_right))
                link(V.tensor_scalar(fb, to_int(tmp_f)[0:LANES, :], -2.0, 1.0, ALU.mult, ALU.add))
                link(V.tensor_tensor(fa, fa, fb, ALU.mult))
                V.tensor_scalar(keyl, fa, float(MID), None, ALU.add).then_inc(keys_ready, 1)
                dve.wait_ge(keys_ready, n)

            def to_cols(ins, out, dt_copy=True):
                ask(ins)
                link(V.tensor_copy(out.rearrange("p (q b) -> p b q", b=2),
                                   bank[0][:, 0:TILES].rearrange("p (b q) -> p b q", b=2)))

            def run_flags(k_, p_, n_):
                done(V.tensor_tensor(sprev, k_, p_, ALU.is_equal))
                done(V.tensor_tensor(snext, k_, n_, ALU.is_equal))
                done(V.tensor_scalar(eqp, k_, p_[:, 0:1], None, ALU.is_equal))
                done(V.tensor_scalar(eqn, k_, n_[:, F - 1:F], None, ALU.is_equal))
                link(V.tensor_tensor(isl, k_, n_, ALU.not_equal))

            def carries(n, first, ends_of, z_of, op1, op0, initial, forward):
                link(V.tensor_copy(ends[:, 0:n], ends_of))
                ask(V.tensor_copy(endz[:, 0:n], z_of.broadcast_to([LANES, n])))
                done(V.memset(run[0:n, :], initial))
                link(V.tensor_copy(rows[0:n, 0:2 * LANES], bank[1][0:n, 0:2 * LANES]))
                if forward:
                    ask(V.tensor_tensor_scan(run[0:n, 1:LANES + 1], rows[0:n, LANES:2 * LANES], rows[0:n, 0:LANES],
                                             initial, op0, op1))
                else:
                    ask(V.tensor_tensor_scan(run[0:n, LANES - 1::-1], rows[0:n, 2 * LANES - 1:LANES - 1:-1],
                                             rows[0:n, LANES - 1::-1], initial, op0, op1))
                link(V.tensor_copy(carry[:, 0:n], bank[1][0:LANES, 256:256 + n]))

            def head(ap, h):
                return ap[:, h * F:(h + 1) * F]

            def ends_of(ap, n, c):
                return ap[:, c:n * F:F]

            def run_sums(v, out, n):
                for h in range(n):
                    last = V.tensor_tensor_scan(head(out, h), sprev, head(v, h), 0.0, ALU.mult, ALU.add)
                    done(last)
                need(order.off)
                carries(n, 0, ends_of(out, n, F - 1), eqp[:, F - 1:F], ALU.add, ALU.mult, 0.0, True)
                for h in range(n):
                    done(V.scalar_tensor_tensor(head(out, h), eqp, carry[:, h:h + 1], head(out, h), ALU.mult, ALU.add))
                need(order.off)

            def spread_last(v, out, n):
                for h in range(n):
                    done(V.tensor_tensor_scan(head(out, h)[:, ::-1], snext[:, ::-1], head(v, h)[:, ::-1], 0.0,
                                              ALU.mult, ALU.add))
                need(order.off)
                carries(n, 0, ends_of(out, n, 0), eqn[:, 0:1], ALU.add, ALU.mult, 0.0, False)
                for h in range(n):
                    done(V.scalar_tensor_tensor(head(out, h), eqn, carry[:, h:h + 1], head(out, h), ALU.mult, ALU.add))
                need(order.off)

            def targets(add_idx):
                link(V.tensor_tensor(fa, keyl, trash, ALU.subtract))
                link(V.tensor_tensor(fa, fa, isl, ALU.mult))
                to_cols(V.tensor_tensor(fa, fa, trash, ALU.add), add_idx[:, :])

            sort(key_f)
            unpack(idx["e_d"], 1)
            to_cols(V.tensor_copy(fb, keyl), key_col["dst"][:, :])

            dve.wait_ge(dvec_in, 80)
            for k in range(DBUF):
                done(V.memset(dense[k][:, :, COL_DV], 0.0))
            need(order.off)
            for k in range(NCHUNK):
                d_ = dense[k % DBUF]
                r = slice(k * CHUNK, (k + 1) * CHUNK)
                dve.wait_ge(dense_in[k % DBUF], 16 * (k // DBUF + 1))
                V.tensor_copy(d_[:, :, COL_A], nv1[:, r])
                V.tensor_copy(d_[:, :, COL_B], nv2[:, r])
                V.tensor_copy(d_[:, :, COL_HW], nvh[:, r])
                V.tensor_tensor(d_[:, :, 0:D], d_[:, :, 0:D], over(wts["C"][:, :], CHUNK), ALU.add).then_inc(dense_sum, 1)
            dve.wait_ge(left_in, 48)
            done(V.tensor_copy(left_rows[:, COL_HW:COL_HW + 1], hw_last[0:LEFT, :]))
            done(V.memset(left_rows[:, COL_DV:COL_DV + 1], 0.0))
            done(V.tensor_copy(zeros[0:1, COL_HW:COL_HW + 1], hw_last[0:1, :]))
            V.tensor_tensor(left_rows[:, 0:D], left_rows[:, 0:D], wts["C"][0:LEFT, :], ALU.add).then_inc(left_sum, 1)

            dve.wait_ge(keys_in, 32)
            run_flags(keyl, prevl, nextl)
            link(V.tensor_scalar(to_int(posf), pos[0:LANES, :], SPARE - 1, None, ALU.bitwise_and))
            link(V.tensor_scalar(trash, to_int(posf), float(N + 1), None, ALU.add))
            link(V.tensor_copy(posf, pos[0:LANES, :]))
            targets(idx["add_d"])
            link(V.tensor_scalar(clprev, prevl, float(M - 1), None, ALU.min))
            link(V.tensor_scalar(clnext, nextl, float(M - 1), None, ALU.min))
            V.tensor_scalar(clipl, keyl, float(M - 1), None, ALU.min).then_inc(keys_ready, 1)
            dve.wait_ge(keys_ready, 2)
            to_cols(V.tensor_copy(fb, clipl), key_col["clip"][:, :])
            run_flags(clipl, clprev, clnext)
            link(V.tensor_tensor(fa, posf, isl, ALU.mult))
            spread_last(fa, fb, 1)
            rec3 = rec[:, :].rearrange("p (t c) -> p t c", c=REC)
            dve.wait_ge(R["taken"], NG)
            ask(V.tensor_copy(fa, fb))
            V.tensor_copy(rec3[:, :, R_LAST].rearrange("p (q b) -> p b q", b=2),
                          bank[0][:, 0:TILES].rearrange("p (b q) -> p b q", b=2)).then_inc(recs_ready, 1)
            dve.wait_ge(recs_ready, 1)
            link(V.tensor_scalar(fb, keyl, float(M), None, ALU.is_lt))
            run_sums(fb, fa, 1)
            to_cols(V.tensor_copy(clnext, fa), cnt_col[:, :])
            link(V.tensor_copy(idx["src_d"][:, :], rec3[:, :, R_SRC]))
            link(V.tensor_copy(idx["dst_d"][:, :], rec3[:, :, R_DST]))

            done(V.memset(key_f, float(N)))
            ask(V.memset(tmp_g[:, 0:1], 0.0))
            link(V.tensor_copy(key_f[0:LANES, :], bank[0][0:LANES, 0:F]))
            dve.wait_ge(keys_stored, 96)
            sort(key_f)
            unpack(idx["e_s"], 3)
            to_cols(V.tensor_copy(fb, keyl), key_col["src"][:, :])
            dve.wait_ge(keys_in, 64)
            run_flags(keyl, prevl, nextl)
            targets(idx["add_s"])
            dve.wait_ge(R["taken"], 2 * NG)
            rs = rec_s[:, :].rearrange("p (t c) -> p t c", c=4)
            link(V.tensor_copy(idx["dst_s"][:, :], rs[:, :, R_DST]))
            link(V.tensor_copy(idx["last_s"][:, :], rs[:, :, R_LAST]))
            stage_end(dve, 1)
            link(V.memset(big[:, :].rearrange("p (t c) -> p t c", c=ROW)[:, :, D:ROW], 0.0))

            def statistics(G, S, v, tiles):
                s = small[G.slot]
                for t in range(tiles):
                    done(V.bn_stats(s[:, 16 + 6 * t:22 + 6 * t], v(t)))
                need(order.off)
                plain(dve)
                for t in range(tiles):
                    ins = V.bn_aggr(s[:, 80 + 2 * t:82 + 2 * t], s[:, 16 + 6 * t:22 + 6 * t])
                    if t < tiles - 1:
                        done(ins)
                ins.then_inc(S["var"], 1)

            def scales(G, S, tiles, weight=None):
                s = small[G.slot]
                dve.wait_ge(S["dev"], G.g + 1)
                link(V.reciprocal(s[:, 0:tiles], s[:, 104:104 + tiles]))
                if weight is not None:
                    link(V.tensor_tensor(s[:, 0:tiles], s[:, 0:tiles], weight, ALU.mult))
                V.scalar_tensor_tensor(s[:, 8:8 + tiles], s[:, 80:80 + 2 * tiles:2], -1.0, s[:, 0:tiles],
                                       ALU.mult, ALU.mult).then_inc(S["norm"], 1)

            def matrices(G, S, which, name):
                keys_at.wait(dve, name, G)
                k = keys_r[G.slot]
                here = t4(k[:, 1:GE + 1])
                done(V.tensor_tensor(t4(sel_r[G.slot]), here, wide(cols4(key_col[which], G)), ALU.is_equal))
                V.tensor_tensor(t4(ind_r[G.slot]), here, wide(k[:, 0:GE:P]), ALU.is_equal).then_inc(S["sel"], 1)

            def chain(G, S, banks, ring_, free, first=(), lag=2):
                dve.wait_ge(S["sums"], G.g + 1)
                if G.from_(2) and free:
                    dve.wait_ge(S[free], G.g - 1)
                for t in range(GROUP):
                    for k, b in enumerate(banks):
                        o = 512 * k
                        if t:
                            before = ring_[G.slot][:, o + t * P - 1:o + t * P]
                        elif G.from_(1):
                            before = ring_[1 - G.slot][:, o + 511:o + 512]
                        else:
                            before = zero_col[:, :]
                        ins = V.scalar_tensor_tensor(ring_[G.slot][:, o + t * P:o + (t + 1) * P],
                                                     ind_r[G.slot][:, t * P:(t + 1) * P], before,
                                                     b[:, t * P:(t + 1) * P], ALU.mult, ALU.add)
                        if t < GROUP - 1 or k < len(banks) - 1:
                            done(ins)
                    if t < GROUP - 1:
                        need(order.off)
                ins.then_inc(S["chained"], 1)
                dve.wait_ge(S["chained"], G.g + 1)

            def front(G):
                rows_in.wait(dve, "S0", G)
                r = rows_r[G.place][:, 0:GROUP * ROW].rearrange("p (t c) -> p t c", c=ROW)
                if G.from_(2):
                    dve.wait_ge(S0["sums"], G.g - 1)
                done(V.tensor_tensor(t4(v_r[G.slot]), r[:, :, 0:D], over(wts["C"][:, :], GROUP), ALU.subtract))
                V.tensor_copy(small[G.slot][:, 64:68], r[:, :, COL_HW]).then_inc(S0["taken"], 1)
                need(order.off)
                statistics(G, S0, lambda t: v_r[G.slot][:, t * P:(t + 1) * P], GROUP)
                matrices(G, S0, "src", "S0")
                scales(G, S0, GROUP)

            def chains(G):
                dve.wait_ge(S0["sums"], G.g + 1)
                if G.from_(2):
                    dve.wait_ge(S0["delta"], G.g - 1)
                for t in range(GROUP):
                    c = slice(t * P, (t + 1) * P)
                    if t:
                        u0, d0 = uT_r[G.slot][:, t * P - 1:t * P], row_r[G.slot][0:1, t * P - 1:t * P]
                    elif G.from_(1):
                        u0, d0 = uT_r[1 - G.slot][:, 511:512], row_r[1 - G.slot][0:1, 511:512]
                    else:
                        u0, d0 = zero_col[:, :], zero_col[0:1, :]
                    done(V.scalar_tensor_tensor(row_r[G.slot][0:1, c], ind_r[G.slot][0:1, c], d0,
                                                bank[2 + G.slot][0:1, c], ALU.mult, ALU.add))
                    ins = V.scalar_tensor_tensor(uT_r[G.slot][:, c], ind_r[G.slot][:, c], u0, bank[G.slot][:, c],
                                                 ALU.mult, ALU.add)
                    if t < GROUP - 1:
                        link(ins)
                ins.then_inc(S0["chained"], 1)
                dve.wait_ge(S0["chained"], G.g + 1)

            def body(G):
                front(G)
                if G.from_(1):
                    chains(G.before())
            for_groups(dve, body, order)
            chains(group(NG - 1))
            dve.wait_ge(S0["kept"], NG)
            V.tensor_scalar(dvis_s[:, :], big[:, :].rearrange("p (t c) -> p t c", c=ROW)[:, :, COL_DV],
                            1.0, None, ALU.max).then_inc(roots, 1)
            dve.wait_ge(roots, 2)
            link(V.reciprocal(dvis_s[:, :], dvis_s[:, :]))
            stage_end(dve, 2)
            stage_end(dve, 3)

            def logits(G):
                dve.wait_ge(S1["hh"], G.g + 1)
                done(V.tensor_copy(small[G.slot][:, 112:128], bank[5][:, 0:16]))
                need(order.off)
                V.scalar_tensor_tensor(cols4(al, G, 16), small[G.slot][:, 112:128], 0.2, small[G.slot][:, 112:128],
                                       ALU.mult, ALU.max).then_inc(S1["logits"], 1)

            def body(G):
                rows_in.wait(dve, "S1", G)
                if G.from_(2):
                    dve.wait_ge(S1["h"], G.g - 1)
                r = rows8_r[G.place].rearrange("p (t c) -> p t c", c=ROW)
                done(V.tensor_tensor(t4(v8[G.slot]), r[:, :, 0:D], over(wts["K1"][:, :], W8), ALU.subtract))
                done(V.tensor_copy(cols4(sc_s, G, 16).rearrange("p (t c) -> p t c", c=4), r[:, 0:GROUP, D:ROW]))
                V.tensor_copy(cols4(sc_d, G, 16).rearrange("p (t c) -> p t c", c=4), r[:, GROUP:W8, D:ROW]
                              ).then_inc(S1["taken"], 1)
                need(order.off)
                statistics(G, S1, lambda t: v8[G.slot][:, t * P:(t + 1) * P], W8)
                scales(G, S1, W8)
                if G.from_(2):
                    logits(G.before(2))
            for_groups(dve, body, order)
            logits(group(NG - 2))
            logits(group(NG - 1))
            dve.wait_ge(S1["logits"], NG)
            s4 = sc_s[:, :].rearrange("p (t c) -> p t c", c=4)
            d4 = sc_d[:, :].rearrange("p (t c) -> p t c", c=4)
            V.tensor_scalar(wt_col[:, :], s4[:, :, 3], 1.0, None, ALU.max).then_inc(roots, 1)
            dve.wait_ge(roots, 4)
            link(V.reciprocal(wt_col[:, :], wt_col[:, :]))
            link(V.tensor_scalar(hsc_col[:, :], key_col["dst"][:, :], float(M), None, ALU.is_lt))
            link(V.tensor_tensor(wt_col[:, :], wt_col[:, :], hsc_col[:, :], ALU.mult))
            link(V.tensor_scalar(hsc_col[:, :], cnt_col[:, :], 1.0, None, ALU.max))
            link(V.reciprocal(hsc_col[:, :], hsc_col[:, :]))
            link(V.tensor_tensor(hsc_col[:, :], hsc_col[:, :], d4[:, :, 2], ALU.mult))
            link(V.tensor_tensor(rec3[:, :, R_A4:R_A4 + 4], rec3[:, :, R_A4:R_A4 + 4], wide(s4[:, :, 0], 4), ALU.mult))
            stage_end(dve, 4)

            dve.wait_ge(keys_in, 64 + 48)
            run_flags(keyl, prevl, nextl)
            ask(V.tensor_copy(fb, keyl))
            for k in range(2):
                done(V.tensor_copy(alb[:, 512 * k:512 * (k + 1)], bank[2 + k][0:LANES, :]))
            need(order.off)
            link(V.tensor_scalar(fa, sprev, 1.0, BIG_NUM, ALU.subtract, ALU.mult))
            link(V.tensor_scalar(fb, eqp, 1.0, BIG_NUM, ALU.subtract, ALU.mult))
            for h in range(H):
                done(V.tensor_tensor_scan(head(fw, h), fa, head(alb, h), -BIG_NUM, ALU.add, ALU.max))
            need(order.off)
            carries(H, 0, ends_of(fw, H, F - 1), fb[:, F - 1:F], ALU.max, ALU.add, -BIG_NUM, True)
            for h in range(H):
                done(V.scalar_tensor_tensor(head(fw, h), fb, carry[:, h:h + 1], head(fw, h), ALU.add, ALU.max))
            need(order.off)
            h4 = lambda ap: ap.rearrange("p (h f) -> p h f", h=H)
            link(V.tensor_tensor(h4(fw), h4(fw), over(isl, H), ALU.mult))
            spread_last(fw, bw, H)
            V.tensor_tensor(alb, alb, bw, ALU.subtract).then_inc(exp_asked, 1)
            dve.wait_ge(exp_done, 1)
            run_sums(alb, fw, H)
            link(V.tensor_tensor(h4(fw), h4(fw), over(isl, H), ALU.mult))
            spread_last(fw, bw, H)
            link(V.tensor_scalar(bw, bw, 1e-16, None, ALU.add))
            link(V.reciprocal(bw, bw))
            ask(V.tensor_tensor(tt4, alb, bw, ALU.mult))
            alc = al[:, :].rearrange("p (q b h) -> p h b q", b=2, h=H)
            for h in range(H):
                c0 = (h % 2) * TILES
                link(V.tensor_copy(alc[:, h], bank[2 + h // 2][:, c0:c0 + TILES].rearrange("p (b q) -> p b q", b=2)))
            for s in range(UNROLL):
                link(V.memset(dl4_r[s].rearrange("p (t c) -> p t c", c=ROW)[:, :, D:ROW], 0.0))
            stage_end(dve, 5)

            def front(G):
                if G.from_(2):
                    dve.wait_ge(S1b["sums"], G.g - 1)
                c = cols4(al, G, 16)
                done(V.tensor_tensor(h_r[G.slot].rearrange("p (a c) -> p a c", c=C),
                                     cols4(big, G, 512).rearrange("p (a c) -> p a c", c=C), wide(c, C), ALU.mult))
                matrices(G, S1b, "dst", "S1b")

            def leaky(G):
                dve.wait_ge(S1b["biased"], G.g + 1)
                if G.from_(2):
                    dve.wait_ge(S1b["delta"], G.g - 1)
                V.scalar_tensor_tensor(z_r[G.slot], t1_r[G.slot], 0.01, t1_r[G.slot], ALU.mult, ALU.max
                                       ).then_inc(S1b["z"], 1)

            def body(G):
                front(G)
                if G.from_(2):
                    leaky(G.before(2))
                if G.from_(1):
                    chain(G.before(), S1b, [bank[1 - G.slot]], uT_r, "biased")
            for_groups(dve, body, order)
            leaky(group(NG - 2))
            chain(group(NG - 1), S1b, [bank[0]], uT_r, "biased")
            leaky(group(NG - 1))
            dve.wait_ge(S1b["z"], NG)
            stage_end(dve, 6)

            def front(G):
                rows_in.wait(dve, "S2", G)
                if G.from_(2):
                    dve.wait_ge(S2["sums"], G.g - 1)
                r = rows_r[G.place].rearrange("p (t c) -> p t c", c=ROW)
                V.tensor_tensor(t4(v_r[G.slot]), r[:, :, 0:D], over(wts["K2"][:, :], GROUP), ALU.subtract
                                ).then_inc(S2["taken"], 1)
                dve.wait_ge(S2["taken"], G.g + 1)
                statistics(G, S2, lambda t: v_r[G.slot][:, t * P:(t + 1) * P], GROUP)
                matrices(G, S2, "clip", "S2")
                scales(G, S2, GROUP, cols4(wt_col, G))

            def body(G):
                front(G)
                if G.from_(1):
                    chain(G.before(), S2, [bank[1 - G.slot]], uT_r, "he")
            for_groups(dve, body, order)
            chain(group(NG - 1), S2, [bank[0]], uT_r, "he")
            stage_end(dve, 7)
            for s in range(UNROLL):
                link(V.memset(dl4h_r[s].rearrange("p (t c) -> p t c", c=ROW)[:, :, D:ROW], 0.0))

            def body(G):
                if G.from_(2):
                    dve.wait_ge(S3["sums"], G.g - 1)
                matrices(G, S3, "src", "S3")
                if G.from_(1):
                    chain(G.before(), S3, [bank[1 - G.slot]], uT_r, "delta")
            for_groups(dve, body, order)
            chain(group(NG - 1), S3, [bank[0]], uT_r, "delta")
            link(V.memset(big[:, :].rearrange("p (t c) -> p t c", c=ROW)[:, :, D:ROW], 0.0))
            stage_end(dve, 8)

            def front(G):
                rows_in.wait(dve, "S4", G)
                if G.from_(2):
                    dve.wait_ge(S4["sums"], G.g - 1)
                    dve.wait_ge(S4["h"], G.g - 1)
                statistics(G, S4, lambda t: rows_r[G.place][:, t * ROW:t * ROW + D], GROUP)
                if G.from_(2):
                    chain2(G.before(2))
                matrices(G, S4, "dst", "S4")
                scales(G, S4, GROUP)

            def features(G):
                dve.wait_ge(S4["e"], G.g + 1)
                w_in.wait(dve, "S4", G)
                e_ = t4(bank[1 + G.slot][:, :])
                ev = e_[:, :, 32:128].rearrange("p t (i c) -> p t i c", c=MUL)
                y = cols4(rec, G, GROUP * REC).rearrange("p (t c) -> p t c", c=REC)
                w = t4(w_r[G.slot])
                f = feat_r[G.slot].rearrange("p (t k c) -> p t k c", t=GROUP, k=2)
                q = q_t.rearrange("p (t k c) -> p t k c", t=GROUP, k=4)
                tv = t_t.rearrange("p (t i c) -> p t i c", t=GROUP, i=3)
                m3 = m3_t.rearrange("p (t c) -> p t c", c=MUL)

                def many(ap, n):
                    return ap.unsqueeze(2).broadcast_to([P, GROUP, n, MUL])

                def per(ap, n):
                    return ap.unsqueeze(3).broadcast_to([P, GROUP, n, MUL])
                done(V.tensor_tensor(q, many(e_[:, :, 0:32], 4), per(y[:, :, R_A4:R_A4 + 4], 4), ALU.mult))
                done(V.tensor_tensor(tv, ev, per(y[:, :, R_A4 + 1:R_A4 + 4], 3), ALU.mult))
                need(order.off - 1)
                done(V.tensor_tensor(f[:, :, 0, 0:32], q[:, :, 0, :], w[:, :, 0:32], ALU.mult))
                done(V.tensor_tensor(f[:, :, 0, 32:128].rearrange("p t (i c) -> p t i c", c=MUL), q[:, :, 1:4, :],
                                     many(w[:, :, 32:64], 3), ALU.mult))
                need(order.off - 2)
                done(V.tensor_reduce(m3, tv.rearrange("p t i c -> p t c i"), AX.X, ALU.add))
                need(order.off - 1)
                ys = y[:, :, R_A4:R_A4 + 1].unsqueeze(3).broadcast_to([P, GROUP, 3, MUL])
                done(V.tensor_tensor(q[:, :, 0:3, :], ev, ys, ALU.mult))
                need(order.off - 1)
                done(V.tensor_tensor(f[:, :, 1, 0:32], m3, w[:, :, 96:128], ALU.mult))
                need(order.off - 1)
                V.tensor_tensor(f[:, :, 1, 32:128].rearrange("p t (i c) -> p t i c", c=MUL), q[:, :, 0:3, :],
                                many(w[:, :, 64:96], 3), ALU.mult).then_inc(S4["feat"], 1)
                dve.wait_ge(S4["feat"], G.g + 1)

            def chain2(G):
                chain(G, S4, [bank[3 + 2 * G.slot], bank[4 + 2 * G.slot]], uT2_r, "delta")

            def body(G):
                front(G)
                if G.from_(1):
                    features(G.before())
            for_groups(dve, body, order)
            features(group(NG - 1))
            chain2(group(NG - 2))
            chain2(group(NG - 1))
            stage_end(dve, 9)
            stage_end(dve, 10)


N_WEIGHTS = 12 + 2 * H + 1 + 3 + 2 * 4

_INS = ["x", "src", "dst", "edge_attr_4", "edge_attr_8", "edge_weight", "node_vec1", "node_vec1_n2",
        "L0_gnn_weight", "L0_gnn_bias", "L1_gnn_W1", "L1_gnn_b1", "L1_gnn_Wg", "L1_gnn_att_src",
        "L1_gnn_att_dst", "L1_gnn_bias_g", "L1_gnn_W2", "L1_gnn_b2", "L2_gnn_hyperedge_weight",
        "L2_gnn_W", "L2_gnn_b", "L3_gnn_w1_s", "L3_gnn_w1_v", "L3_gnn_Wfc1", "L3_gnn_Wfc2",
        "L3_gnn_w2_s", "L3_gnn_w2_v"]


def kernel(**inputs):
    import numpy as _np
    import concourse.bacc as _bacc
    from concourse import mybir as _mybir
    from concourse.bass_utils import run_bass_kernel_spmd as _run

    nc = _bacc.Bacc("TRN2", target_bir_lowering=False, num_devices=1)
    arrays, args = {}, []
    for name in _INS:
        a = _np.ascontiguousarray(inputs[name])
        arrays[f"in_{name}_dram"] = a
        args.append(nc.dram_tensor(f"in_{name}_dram", a.shape, _mybir.dt.from_np(a.dtype), kind="ExternalInput").ap())
    args.append(nc.dram_tensor("out_0_dram", (TABLE, ROW), _mybir.dt.float32, kind="ExternalOutput").ap())
    build_gnn(nc, *args)
    r = _run(nc, [arrays], core_ids=[0])
    return _np.ascontiguousarray(r.results[0]["out_0_dram"][:N, :D])
```

```python
import math
from contextlib import ExitStack

import concourse.bass as bass
from concourse import mybir

N, E, D = 100000, 25000, 128
M = 20000
H, C = 4, 32
MUL, NSC, HID = 32, 8, 64
P = 128
TILES = math.ceil(E / P)
EP = TILES * P
F = 256
LANES = EP // F
GROUP = 4
NG = TILES // GROUP
GE = GROUP * P
UNROLL = 4
ROW = 132
COL_A, COL_B, COL_HW, COL_DV = 128, 129, 130, 131
SPARE = UNROLL * GROUP * P
TABLE = N + 1 + SPARE
REC = 16
R_SRC, R_DST, R_W, R_LAST, R_A4, R_A8 = 0, 1, 2, 3, 4, 8
LOG = 15
MID = N // 2
WEIGHTS_AT = 3
RUNS_AT = 12
LEAST = 256
BIG_NUM = 1.0e30
EPS = 1e-5
PER_LANE = N // P
CHUNK = 11
NCHUNK = PER_LANE // CHUNK
LEFT = N - PER_LANE * P
DBUF = 5
POOL_STEPS = 5
STEPS = NCHUNK // DBUF
AHEAD = 3
SIGN = -2147483648

fp32 = mybir.dt.float32
i32 = mybir.dt.int32


class Group:

    def __init__(self, step, place):
        self.step, self.place = step, place
        self.g = step * UNROLL + place
        self.slot = place % 2

    def use(self, slots=2):
        return self.step * (UNROLL // slots) + self.place // slots

    def before(self, n=1):
        carry = -((self.place - n) // UNROLL)
        return Group(self.step - carry if carry else self.step, (self.place - n) % UNROLL)

    def after(self):
        return Group(self.step + 1, 0) if self.place == UNROLL - 1 else Group(self.step, self.place + 1)

    def from_(self, n):
        return not isinstance(self.g, int) or self.g >= n


def group(g):
    return Group(g // UNROLL, g % UNROLL)


class Slots:

    def __init__(self, sems, loops):
        self.sems, self.loops, self.start = sems, dict(loops), {}
        self.n = len(sems)
        total = 0
        for name, amount in loops:
            self.start[name] = total
            total += amount

    def of(self, G):
        return self.sems[G.place % self.n]

    def wait(self, eng, name, G):
        k = G.place % self.n
        base = self.start[name] * len(range(k, NG, self.n))
        eng.wait_ge(self.sems[k], (G.use(self.n) + 1) * self.loops[name] + base)

    def wait_all(self, eng, name):
        for k in range(self.n):
            eng.wait_ge(self.sems[k], (self.start[name] + self.loops[name]) * len(range(k, NG, self.n)))


class Order:

    def __init__(self, eng, sem):
        self.eng, self.sem, self.base, self.off = eng, sem, 0, 0

    def done(self, ins):
        self.off += 1
        ins.then_inc(self.sem, 1)
        return self.off

    def need(self, at):
        self.eng.wait_ge(self.sem, self.base + at)

    def link(self, ins):
        self.need(self.done(ins))


def for_groups(eng, body, order=None):
    for g in range(UNROLL):
        start = order.off if order else 0
        body(group(g))
        steady = order.off - start if order else 0
    first = order.off if order else 0
    with eng.Fori(1, NG // UNROLL) as i:
        if order:
            order.base = i * (UNROLL * steady) - UNROLL * steady
            order.off = first
        for place in range(UNROLL):
            body(Group(i, place))
        if order:
            assert order.off == first + UNROLL * steady, (order.off, first, steady)
    if order:
        order.base, order.off = 0, first + (NG // UNROLL - 1) * UNROLL * steady
    assert NG % UNROLL == 1
    body(group(NG - 1))


def build_gnn(nc, x, src, dst, edge_attr_4, edge_attr_8, edge_weight, node_vec1, node_vec1_n2,
              L0_W, L0_b, W1, b1, Wg, att_src, att_dst, bias_g, W2, b2, hw, L2_W, L2_b,
              w1_s, w1_v, Wfc1, Wfc2, w2_s, w2_v, table):
    ALU = mybir.AluOpType
    ACT = mybir.ActivationFunctionType
    AX = mybir.AxisListType

    rec_raw = nc.dram_tensor("rec_raw", (EP, REC), fp32).ap()
    rec_d = nc.dram_tensor("rec_d", (EP, REC), fp32).ap()
    keys_dram = {k: nc.dram_tensor(f"keys_{k}", (EP + 2,), fp32).ap() for k in ("dst", "clip", "src")}
    he_dram = nc.dram_tensor("he", (EP, D), fp32).ap()
    w_dram = nc.dram_tensor("edge_w", (P, TILES * 2 * D), fp32).ap()

    ctx = ExitStack()
    with ctx:
        def sb(name, shape, dt=fp32):
            return ctx.enter_context(nc.sbuf_tensor(name, shape, dt))

        def sem(name):
            return ctx.enter_context(nc.semaphore(name))

        bank = [ctx.enter_context(nc.psum_tensor(f"bank{k}", [P, 512], fp32)) for k in range(8)]

        big = sb("big", [P, TILES * ROW])
        work = sb("work", [P, 14000])
        rec = sb("rec", [P, TILES * REC])
        rec_s = sb("rec_s", [P, TILES * 4])
        sc_s = sb("sc_s", [P, TILES * 4])
        sc_d = sb("sc_d", [P, TILES * 4])
        al = sb("al", [P, TILES * H])
        key_col = {k: sb(f"key_{k}", [P, TILES]) for k in ("dst", "clip", "src")}
        cnt_col = sb("cnt_col", [P, TILES])
        steps_down = sb("steps_down", [1, 1], i32)
        wt_col = sb("wt_col", [P, TILES])
        hsc_col = sb("hsc_col", [P, TILES])
        dvis_s = sb("dvis_s", [P, TILES])
        idx = {k: sb(f"idx_{k}", [P, TILES], i32)
               for k in ("e_d", "e_s", "src_d", "dst_d", "add_d", "dst_s", "last_s", "add_s")}
        ident = sb("ident", [P, P])
        pos = sb("pos", [P, F], i32)
        one = sb("one", [1, P])
        zero_col = sb("zero_col", [P, 1])
        exp_warm = sb("exp_warm", [P, 1])
        eps_col = sb("eps_col", [P, 1])
        edge_mark = sb("edge_mark", [1, 2])
        wts = {k: sb(f"w_{k}", [P, P]) for k in
               ("W0", "W1", "W1T", "Wg", "WgT", "W2", "W2T", "L2", "L2T", "B1", "B2a", "B2b",
                "C", "K1", "K2", "lbgB")}
        att = sb("att", [P, 8])
        attw = sb("attw", [P, 8])
        cols = sb("cols", [P, 4])
        negc1 = sb("negc1", [1, P])
        fc1 = sb("fc1", [NSC, HID])
        fc2 = sb("fc2", [HID, 4 * MUL])
        wv_st = sb("wv_st", [P, 3 * 32])

        rec_st = big[:, 0:4096]
        src_i, dst_i = big[:, 4096:4352].bitcast(i32), big[:, 4352:4608].bitcast(i32)
        wt_in, at4_in, at8_in = big[:, 4608:4864], big[:, 4864:5888], big[:, 5888:7936]
        lane_bufs = [big[:, 8192 + k * F:8192 + (k + 1) * F] for k in range(8)]
        sort_b, sort_a = lane_bufs[0:2], lane_bufs[2:4]
        gray, flip = lane_bufs[4].bitcast(i32), lane_bufs[5].bitcast(i32)
        key_f, tmp_f = lane_bufs[6], lane_bufs[7]
        tmp_g = big[:, 10240:10496]
        next_i = tmp_g.bitcast(i32)
        DB = 10496
        dense = [big[:, DB + k * CHUNK * ROW:DB + (k + 1) * CHUNK * ROW].rearrange("p (r c) -> p r c", c=ROW)
                 for k in range(DBUF)]
        NV = DB + DBUF * CHUNK * ROW
        nv1, nv2, nvh = (big[:, NV + k * PER_LANE:NV + (k + 1) * PER_LANE] for k in range(3))
        LB = NV + 3 * PER_LANE
        left_rows = big[0:LEFT, LB:LB + ROW]
        zeros = big[:, LB + ROW:LB + ROW + SPARE // P * ROW]
        assert LB + (SPARE // P + 1) * ROW <= TILES * ROW
        hw_last = wv_st[:, 95:96]
        worst = wv_st[:, 94:95]

        SC = 2400
        wk = [work[0:LANES, SC + k * F:SC + (k + 1) * F] for k in range(15)]
        keyl, prevl, nextl, sprev, snext, eqp, eqn, isl = wk[0:8]
        fa, fb, posf, trash = wk[8:12]
        clipl, clprev, clnext = wk[12:15]
        SC += 15 * F
        ends, endz, carry = (work[0:LANES, SC + 4 * k:SC + 4 * k + 4] for k in range(3))
        rows, run = work[0:4, SC + 16:SC + 272], work[0:4, SC + 272:SC + 372]
        SC += 384
        alb, fw, bw, tt4 = (work[0:LANES, SC + k * H * F:SC + (k + 1) * H * F] for k in range(4))

        weights_in = sem("weights_in")
        consts_ready = sem("consts_ready")
        vec = sem("vec_order")
        asked, answered = sem("pe_asked"), sem("pe_answered")
        pads_ready, raw_in, rec_ready, raw_stored = sem("pads_ready"), sem("raw_in"), sem("rec_ready"), sem("raw_stored")
        dvec_in, dense_ready = sem("dense_vectors_in"), sem("dense_consts")
        dense_in = [sem(f"dense_in{k}") for k in range(DBUF)]
        dense_out = [sem(f"dense_out{k}") for k in range(DBUF)]
        dense_sum = [sem(f"dense_sum{k}") for k in range(DBUF)]
        biases_ready = sem("biases_ready")
        left_in, left_sum, left_out = sem("left_in"), sem("left_sum"), sem("left_out")
        keys_ready, keys_stored, keys_in = sem("keys_ready"), sem("keys_stored"), sem("keys_in")
        e_ready = sem("sorted_edges_ready")
        recs_ready, recs_stored = sem("recs_ready"), sem("recs_stored")
        exp_asked, exp_done = sem("exp_asked"), sem("exp_done")
        stage = sem("stage_done")
        flag_ready = sem("flag_ready")
        ids_in = sem("ids_in")
        roots = sem("roots_ready")

        def stage_end(eng, n):
            eng.sem_inc(stage, 1)
            eng.wait_ge(stage, 5 * n)

        def of_rows(name):
            return recs_in if name == "BY_DST" else rows_in

        def load_unsorted(eng):
            eng.wait_ge(flag_ready, 1)
            return eng.value_load(steps_down[0:1, 0:1], min_val=0, max_val=1)

        paced = sem("paced")

        def plain(eng):
            eng.sem_inc(paced, 1)

        def loop_sems(name, words):
            out = {}
            for w in words.split():
                out[w] = [sem(f"{name}_{w}{k}") for k in range(2)] if w.endswith("_") else sem(f"{name}_{w}")
            return out

        R = loop_sems("rec", "taken")
        GCN = loop_sems("gcn", "var dev norm h sel selw sums chained delta kept")
        GAT = loop_sems("gat", "var dev taken norm h hT hTs xx xxs hh kept logits")
        GATSUM = loop_sems("gatsum", "sel sums chained biased z delta kept")
        HYP = loop_sems("hyp", "var dev taken norm h sel sums chained he hes")
        HYPSUM = loop_sems("hypsum", "sel sums chained delta kept at atT atTs fc fcs w ws wide")
        TP = loop_sems("tp", "var dev norm h hT hTs e feat sel sums chained delta kept")
        hes_stored = Slots([sem(f"he_stored{k}") for k in range(2)], [("HYP", 16)])
        w_stored = Slots([sem(f"w_stored{k}") for k in range(2)], [("HYPSUM", 16)])
        w_in = Slots([sem(f"w_in{k}") for k in range(2)], [("TP", 16)])
        recs_in = Slots([sem(f"recs_in{k}") for k in range(UNROLL)], [("BY_DST", 64)])
        rows_in = Slots([sem(f"rows_in{k}") for k in range(UNROLL)],
                        [("BY_SRC", 64), ("GCN", 64), ("GAT", 128), ("HYP", 64), ("HYPSUM", 64), ("TP", 64)])
        added = Slots([sem(f"added{k}") for k in range(UNROLL)], [("GCN", 64), ("GATSUM", 64), ("HYPSUM", 64), ("TP", 64)])
        keys_at = Slots([sem(f"keys_at{k}") for k in range(2)],
                        [("GCN", 16), ("GATSUM", 16), ("HYP", 16), ("HYPSUM", 16), ("TP", 16)])
        big_in = Slots([sem(f"big_in{k}") for k in range(UNROLL)], [("GCN", 16), ("TP", 16)])
        fed = Slots([sem(f"fed{k}") for k in range(UNROLL)], [("GCN", 16), ("TP", 16)])
        idx_in = Slots([sem(f"gather_indices_in{k}") for k in range(UNROLL)], [("GCN", 16), ("GAT", 32), ("TP", 16)])
        idxa_in = Slots([sem(f"add_indices_in{k}") for k in range(UNROLL)], [("GCN", 16), ("TP", 16)])
        idx_taken, idxa_taken = sem("gather_indices_taken"), sem("add_indices_taken")

        def ring(start, size, n=2, dt=fp32):
            out = [work[:, start + k * size:start + (k + 1) * size] for k in range(n)]
            return [o.bitcast(dt) for o in out] if dt != fp32 else out

        W8 = 2 * GROUP
        rows_r = ring(0, GROUP * ROW, UNROLL)
        rows8_r = ring(8544, W8 * ROW, UNROLL)
        idx_r = ring(2112, 8, UNROLL, dt=i32)
        idxa_r = ring(13984, 4, UNROLL, dt=i32)
        small = ring(2144, 128)
        v_r = ring(2400, 512)
        h_r = ring(3424, 512)
        keys_r = ring(4448, GE + 8)
        sel_r = ring(5488, 512)
        ind_r = ring(6512, 512)
        uT_r = ring(7536, 512)
        selw_r = ring(8560, 512)
        dl_r = ring(9584, GROUP * ROW)
        dl4_r = dl_r + ring(0, GROUP * ROW)
        dl4h_r = dl_r + ring(2400, GROUP * ROW)
        z_r = ring(10640, 512)
        t1_r = ring(11664, 512)
        row_r = ring(12688, 512)
        wide_r = [big[:, k * 1024:(k + 1) * 1024] for k in range(2)]
        v8 = ring(2400, 1024)
        h8 = ring(4448, 1024)
        hT8 = work[:, 6496:7520]
        xxT8 = work[:, 7520:8544]
        uT2_r = ring(7536, 1024)
        feat_r = ring(9584, 1024)
        t_t = work[:, 2912:3296]
        w_r = ring(11632, 1024)
        hT_s = work[:, 2400:2912]

        def t4(ap, c=128):
            return ap.rearrange("p (t c) -> p t c", c=c)

        def wide(ap, n=128):
            return ap.unsqueeze(2).broadcast_to([ap.shape[0], ap.shape[1], n])

        def over(ap, n):
            return ap.unsqueeze(1).broadcast_to([ap.shape[0], n, ap.shape[1]])

        def cols4(tile, G, width=4):
            return tile[:, bass.ds(G.g * width, width)] if not isinstance(G.g, int) else tile[:, G.g * width:(G.g + 1) * width]

        def at(ap, G, n):
            return cols4(ap, G, n)

        block = ctx.enter_context(nc.Block())

        SMALL_LOADS = [
            (wts["W0"][:, :], L0_W), (wts["W1"][:, :], W1), (wts["Wg"][:, :], Wg), (wts["W2"][:, :], W2),
            (wts["L2"][:, :], L2_W),
            (wts["C"][:, :], L0_b.partition_broadcast(P)), (wts["K1"][:, :], b2.partition_broadcast(P)),
            (wts["K2"][:, :], L2_b.partition_broadcast(P)),
            (cols[:, 0:1], b1.unsqueeze(1)), (cols[:, 1:2], bias_g.unsqueeze(1)),
            (fc1[:, :], Wfc1), (fc2[:, :], Wfc2),
        ]

        def rows_at(ap, i, q):
            at_ = (i * DBUF + q) * CHUNK
            return ap[:, at_:at_ + CHUNK] if isinstance(i, int) else ap[:, bass.ds(at_, CHUNK)]

        def dense_chunk(eng, seq, i, q):
            seq.wait_ge(dense_in[q], (i + 1) * 16)
            d_ = dense[q]
            eng.tensor_copy(d_[:, :, COL_A], rows_at(nv1, i, q))
            eng.tensor_copy(d_[:, :, COL_B], rows_at(nv2, i, q))
            eng.tensor_copy(d_[:, :, COL_HW], rows_at(nvh, i, q))
            eng.tensor_tensor(d_[:, :, 0:D], d_[:, :, 0:D], over(wts["C"][:, :], CHUNK), ALU.add).then_inc(dense_sum[q], 1)

        def rows_of(dram, G):
            part = dram[bass.ds(G.g * GE, GE), :] if not isinstance(G.g, int) else dram[G.g * GE:(G.g + 1) * GE, :]
            return part.rearrange("(t p) c -> p t c", p=P)

        def load_keys(eng, G, which, S):
            if G.from_(2):
                eng.wait_ge(S["sel"], G.g - 1)
            k = keys_dram[which]
            part = k[bass.ds(G.g * GE, GE + 1)] if not isinstance(G.g, int) else k[G.g * GE:G.g * GE + GE + 1]
            eng.dma_start(keys_r[G.slot][:, 0:GE + 1], part.partition_broadcast(P)).then_inc(keys_at.of(G), 16)

        @block.sync
        def _(sp):
            sp.wait_ge(consts_ready, 1)
            lane_rows = x[0:P * PER_LANE, :].rearrange("(p r) c -> p r c", r=PER_LANE)
            lane_out = table[0:P * PER_LANE, :].rearrange("(p r) c -> p r c", r=PER_LANE)
            sp.dma_start(nv1, node_vec1[0:P * PER_LANE, 0].rearrange("(p r) -> p r", r=PER_LANE)).then_inc(dvec_in, 16)
            sp.dma_start(nv2, node_vec1_n2[0:P * PER_LANE, 0].rearrange("(p r) -> p r", r=PER_LANE)).then_inc(dvec_in, 16)
            sp.dma_start(hw_last, hw[M - 1:M].partition_broadcast(P)).then_inc(dvec_in, 16)
            for to, of in SMALL_LOADS:
                sp.dma_start(to, of).then_inc(weights_in, 16)
            n = len(SMALL_LOADS)
            with nc.allow_non_contiguous_dma(reason="small weights"):
                for h in range(H):
                    sp.dma_start(att[C * h:C * h + C, h:h + 1], att_src[0, h, :].unsqueeze(1)).then_inc(weights_in, 16)
                    sp.dma_start(att[C * h:C * h + C, 4 + h:5 + h], att_dst[0, h, :].unsqueeze(1)).then_inc(weights_in, 16)
                    n += 2
                sp.dma_start(wts["B1"][0:32, 0:32], w1_s).then_inc(weights_in, 16)
                n += 1
                for a in range(3):
                    sp.dma_start(wts["B1"][32 + a:P:3, 32 + 32 * a:64 + 32 * a], w1_v).then_inc(weights_in, 16)
                    n += 1
                for k, b in enumerate(("B2a", "B2b")):
                    sp.dma_start(wts[b][0:32, 0:32], w2_s[k]).then_inc(weights_in, 16)
                    n += 1
                    for a in range(3):
                        sp.dma_start(wv_st[32 + 32 * a:64 + 32 * a, 32 * k:32 * k + 32], w2_v[k]).then_inc(weights_in, 16)
                        n += 1
            assert n == N_WEIGHTS

            full, rest = M // PER_LANE, M % PER_LANE
            sp.wait_ge(dense_ready, 1)
            sp.dma_start(nvh[0:full, :], hw[0:full * PER_LANE].rearrange("(p r) -> p r", r=PER_LANE)).then_inc(dvec_in, 16)
            sp.dma_start(nvh[full:full + 1, 0:rest], hw[full * PER_LANE:M].unsqueeze(0)).then_inc(dvec_in, 16)

            def load_chunk(i, q):
                if not isinstance(i, int) or i > 0:
                    sp.wait_ge(dense_out[q], 16 * i)
                    plain(sp)
                sp.dma_start(dense[q][:, :, 0:D], rows_at(lane_rows, i, q)).then_inc(dense_in[q], 16)

            def store_chunk(i, q):
                sp.wait_ge(dense_sum[q], i + 1)
                plain(sp)
                sp.dma_start(rows_at(lane_out, i, q), dense[q]).then_inc(dense_out[q], 16)

            def step(i):
                for q in range(DBUF):
                    load_chunk(i, q)
                    if q >= AHEAD:
                        store_chunk(i, q - AHEAD)
                    elif not isinstance(i, int) or i > 0:
                        store_chunk(i - 1, q - AHEAD + DBUF)
            step(0)
            with sp.Fori(1, STEPS) as i:
                step(i)
            load_chunk(STEPS, 0)
            for q in range(DBUF - AHEAD, DBUF):
                store_chunk(STEPS - 1, q)
            store_chunk(STEPS, 0)
            sp.dma_start(left_rows[:, 0:D], x[P * PER_LANE:N, :]).then_inc(left_in, 16)
            sp.dma_start(left_rows[:, COL_A:COL_A + 1], node_vec1[P * PER_LANE:N, :]).then_inc(left_in, 16)
            sp.dma_start(left_rows[:, COL_B:COL_B + 1], node_vec1_n2[P * PER_LANE:N, :]).then_inc(left_in, 16)
            sp.wait_ge(left_sum, 1)
            sp.dma_start(table[P * PER_LANE:N, :], left_rows).then_inc(left_out, 16)
            sp.dma_start(table[N:N + 1, :], zeros[0:1, 0:ROW]).then_inc(left_out, 16)
            sp.dma_start(table[N + 1:TABLE, :].rearrange("(p r) c -> p (r c)", p=P), zeros[:, 0:SPARE // P * ROW]
                         ).then_inc(left_out, 16)
            sp.wait_ge(left_out, 48)
            for k in range(DBUF):
                sp.wait_ge(dense_out[k], 16 * len(range(k, NCHUNK, DBUF)))

            stage_end(sp, 1)

            def load_indices(G, name, of):
                if G.from_(UNROLL):
                    rows_in.wait(sp, name, G.before(UNROLL))
                    plain(sp)
                for k, f in enumerate(of):
                    sp.dma_start(idx_r[G.place][:, 4 * k:4 * k + 4], cols4(f, G)).then_inc(idx_in.of(G), 16)

            def move_rows(name, S, columns, of_gather, of_add):
                def into(G):
                    rows_in.wait(sp, name, G)
                    sp.dma_start(cols4(big, G, GROUP * ROW).rearrange("p (t c) -> p t c", c=ROW)[:, :, 0:columns],
                                 rows_r[G.place].rearrange("p (t c) -> p t c", c=ROW)[:, :, 0:columns]
                                 ).then_inc(big_in.of(G), 16)

                def body(G):
                    load_indices(G, name, [of_gather])
                    if G.from_(3):
                        into(G.before(3))
                for_groups(sp, body)
                for g in (NG - 3, NG - 2, NG - 1):
                    into(group(g))
                big_in.wait_all(sp, name)

                def out(G):
                    if G.from_(UNROLL):
                        added.wait(sp, name, G.before(UNROLL))
                        plain(sp)
                    sp.dma_start(idxa_r[G.place][:, 0:4], cols4(of_add, G)).then_inc(idxa_in.of(G), 16)
                    sp.wait_ge(S["kept"], G.g + 1)
                    plain(sp)
                    sp.dma_start(rows_r[G.place], cols4(big, G, GROUP * ROW)).then_inc(fed.of(G), 16)
                for_groups(sp, out)

            move_rows("GCN", GCN, ROW, idx["dst_s"], idx["add_s"])
            stage_end(sp, 2)

            for_groups(sp, lambda G: load_indices(G, "GAT", [idx["src_d"], idx["dst_d"]]))
            stage_end(sp, 3)
            stage_end(sp, 4)

            for_groups(sp, lambda G: load_keys(sp, G, "dst", GATSUM))
            stage_end(sp, 5)

            def store(G):
                sp.wait_ge(HYP["hes"], G.g + 1)
                sp.dma_start(rows_of(he_dram, G), t4(dl_r[G.slot][:, 0:512])).then_inc(hes_stored.of(G), 16)

            def body(G):
                load_keys(sp, G, "clip", HYP)
                if G.from_(3):
                    store(G.before(3))
            for_groups(sp, body)
            for g in (NG - 3, NG - 2, NG - 1):
                store(group(g))
            hes_stored.wait_all(sp, "HYP")
            stage_end(sp, 6)

            def store(G):
                sp.wait_ge(HYPSUM["wide"], G.g + 1)
                sp.dma_start(at(w_dram, G, 1024), wide_r[G.slot]).then_inc(w_stored.of(G), 16)

            def body(G):
                load_keys(sp, G, "src", HYPSUM)
                if G.from_(2):
                    store(G.before(2))
            for_groups(sp, body)
            store(group(NG - 2))
            store(group(NG - 1))
            w_stored.wait_all(sp, "HYPSUM")
            stage_end(sp, 7)

            move_rows("TP", TP, D, idx["src_d"], idx["add_d"])
            stage_end(sp, 8)

        @block.gpsimd
        def _(pool):
            g_ = nc.gpsimd
            for b in ("B1", "B2a", "B2b"):
                g_.memset(wts[b][:, :], 0.0)
            g_.memset(att[:, :], 0.0)
            g_.memset(wv_st[:, :], 0.0)
            g_.memset(ident[:, :], 0.0).then_inc(consts_ready, 1)
            g_.iota(pos[:, :], pattern=[[1, F]], base=0, channel_multiplier=F)
            g_.memset(one[:, :], 1.0)
            g_.memset(zero_col[:, :], 0.0)
            g_.memset(eps_col[:, :], EPS)
            g_.memset(edge_mark[:, :], -1.0)
            pool.wait_ge(consts_ready, 1)
            g_.affine_select(out=ident[:, :], in_=ident[:, :], compare_op=ALU.not_equal, fill=1.0, base=0,
                             pattern=[[-1, P]], channel_multiplier=1).then_inc(consts_ready, 1)

            taken = {"gather": 0, "add": 0}

            def take_indices(G, kind, of, name):
                ring_, done_ = (idx_r, of_rows(name)) if kind == "gather" else (idxa_r, added)
                if G.from_(UNROLL):
                    done_.wait(pool, name, G.before(UNROLL))
                for k, f in enumerate(of):
                    ins = g_.tensor_copy(ring_[G.place][:, 4 * k:4 * k + 4], cols4(f, G))
                ins.then_inc(idx_taken if kind == "gather" else idxa_taken, 1)

            def with_indices(kind, of, name, move):
                loaded = idx_in if kind == "gather" else idxa_in
                if name in loaded.loops:
                    def body(G):
                        loaded.wait(pool, name, G)
                        move(G)
                    return body
                base = taken[kind]
                taken[kind] += NG
                counter = idx_taken if kind == "gather" else idxa_taken
                take_indices(group(0), kind, of, name)

                def body(G):
                    if not (isinstance(G.g, int) and G.g == NG - 1):
                        take_indices(G.after(), kind, of, name)
                    pool.wait_ge(counter, G.g + (1 + base))
                    move(G)
                return body

            def gathers(name, table_ap, of, free=None, columns=ROW, ring_=rows_r, done_before=0):
                def move(G):
                    if G.from_(UNROLL):
                        if free is None:
                            big_in.wait(pool, name, G.before(UNROLL))
                        else:
                            pool.wait_ge(free, G.g + (done_before - UNROLL + 1))
                    plain(pool)
                    for k in range(4 * len(of)):
                        g_.indirect_dma_start(ring_[G.place][:, k * columns:(k + 1) * columns], None, table_ap,
                                              bass.IndirectOffsetOnAxis(ap=idx_r[G.place][:, k:k + 1], axis=0)
                                              ).then_inc(of_rows(name).of(G), 16)
                return with_indices("gather", of, name, move)

            def adds(name, of, ready=None, ring_=dl4_r):
                def move(G):
                    if ready is None:
                        fed.wait(pool, name, G)
                    else:
                        pool.wait_ge(ready, G.g + 1)
                    plain(pool)
                    for k in range(GROUP):
                        g_.indirect_dma_start(table[:, :], bass.IndirectOffsetOnAxis(ap=idxa_r[G.place][:, k:k + 1], axis=0),
                                              ring_[G.place][:, k * ROW:(k + 1) * ROW], None, compute_op=ALU.add
                                              ).then_inc(added.of(G), 16)
                return with_indices("add", of, name, move)

            pool.wait_ge(raw_stored, 16)
            unsorted = load_unsorted(pool)
            with pool.If(unsorted > 0):
                pool.wait_ge(e_ready, 1)
                for_groups(pool, gathers("BY_DST", rec_raw, [idx["e_d"]], R["taken"], REC))
            with pool.If(unsorted < 1):
                pool.sem_inc(idx_taken, NG)

            for k in range(DBUF):
                g_.memset(dense[k][:, :, COL_DV], 0.0)
            pool.wait_ge(biases_ready, 1)
            pool.wait_ge(dvec_in, 80)
            with pool.Fori(0, POOL_STEPS) as i:
                for q in range(DBUF):
                    dense_chunk(g_, pool, i, q)

            pool.wait_ge(recs_stored, 16)
            pool.wait_ge(e_ready, 2)
            for_groups(pool, gathers("BY_SRC", rec_d, [idx["e_s"]], R["taken"], REC, done_before=NG))
            stage_end(pool, 1)
            for_groups(pool, gathers("GCN", table, [idx["dst_s"]]))
            rows_in.wait_all(pool, "GCN")
            for_groups(pool, adds("GCN", [idx["add_s"]], ring_=rows_r))
            added.wait_all(pool, "GCN")
            stage_end(pool, 2)
            for_groups(pool, gathers("GAT", table, [idx["src_d"], idx["dst_d"]], GAT["taken"], ring_=rows8_r))
            stage_end(pool, 3)
            stage_end(pool, 4)
            for_groups(pool, adds("GATSUM", [idx["add_d"]], GATSUM["kept"]))
            added.wait_all(pool, "GATSUM")
            stage_end(pool, 5)
            for_groups(pool, gathers("HYP", table, [idx["src_d"]], HYP["taken"]))
            stage_end(pool, 6)

            take = gathers("HYPSUM", he_dram, [idx["last_s"]], HYPSUM["sums"], D)
            add = adds("HYPSUM", [idx["add_s"]], HYPSUM["kept"], dl4h_r)

            def body(G):
                take(G)
                if G.from_(3):
                    add(G.before(3))
            for_groups(pool, body)
            for g in (NG - 3, NG - 2, NG - 1):
                add(group(g))
            added.wait_all(pool, "HYPSUM")
            stage_end(pool, 7)
            for_groups(pool, gathers("TP", table, [idx["src_d"]]))
            rows_in.wait_all(pool, "TP")
            for_groups(pool, adds("TP", [idx["add_d"]], ring_=rows_r))
            added.wait_all(pool, "TP")
            stage_end(pool, 8)

        @block.tensor
        def _(pe):
            T = nc.tensor
            count = [0]

            def asked_next():
                count[0] += 1
                pe.wait_ge(asked, count[0])

            def flip_blocks(of, cols_of, n_in, width):
                for b in range(2):
                    last = T.transpose(bank[0][0:width, b * n_in:(b + 1) * n_in], cols_of(of, b), ident[0:n_in, 0:n_in])
                last.then_inc(answered, 1)

            lane_blocks = lambda ap, b: ap[:, b * P:(b + 1) * P]
            col_blocks = lambda ap, b: ap[:, b::2]

            def carries(n, row):
                asked_next()
                T.transpose(bank[1][0:n, 0:LANES], ends[:, 0:n], ident[0:LANES, 0:LANES])
                T.transpose(bank[1][0:n, LANES:2 * LANES], endz[:, 0:n], ident[0:LANES, 0:LANES]).then_inc(answered, 1)
                asked_next()
                T.transpose(bank[1][0:LANES, 256:256 + n], row[0:n, :], ident[0:n, 0:n]).then_inc(answered, 1)

            fwd_row, bwd_row = run[:, 0:LANES], run[:, 1:LANES + 1]

            pe.wait_ge(consts_ready, 2)
            asked_next()
            T.matmul(bank[1][0:1, 0:P], worst, ident[:, :], start=True, stop=True).then_inc(answered, 1)

            def sort_transposes(between=lambda k: None):
                for k in range(9, LOG + 1):
                    asked_next()
                    flip_blocks(sort_b[0], lane_blocks, P, P)
                    asked_next()
                    flip_blocks(sort_a[(k - 8) % 2], col_blocks, P, P)
                    between(k)
                asked_next()
                flip_blocks(sort_b[0], lane_blocks, P, P)

            def to_cols(ap):
                asked_next()
                for b in range(2):
                    last = T.transpose(bank[0][:, b * LANES:(b + 1) * LANES], ap[:, b * P:(b + 1) * P], ident[0:LANES, 0:LANES])
                last.then_inc(answered, 1)

            unsorted = load_unsorted(pe)
            before = count[0]
            with pe.If(unsorted > 0):
                sort_transposes()
                asked_next()
                for b in range(2):
                    last = T.transpose(bank[0][0:LANES, b * P:(b + 1) * P],
                                       rec[:, :].rearrange("p (t c) -> p t c", c=REC)[:, b::2, R_SRC], ident[:, :])
                last.then_inc(answered, 1)
            with pe.If(unsorted < 1):
                pe.wait_ge(asked, count[0])
                pe.sem_inc(answered, count[0] - before)
            to_cols(keyl)

            pe.wait_ge(weights_in, 16 * N_WEIGHTS)
            asked_next()
            for k, w in enumerate(("W1", "Wg", "W2", "L2")):
                T.transpose(bank[0][:, k * P:(k + 1) * P], wts[w][:, :], ident[:, :])
            T.matmul(bank[1][:, 0:8], wts["Wg"][:, :], att[:, :], start=True, stop=True).then_inc(answered, 1)
            asked_next()
            T.matmul(bank[1][:, 128:256], wts["lbgB"][:, :], wts["W2T"][:, :], start=True, stop=True).then_inc(answered, 1)

            def runs_by_dst(k):
                if k == RUNS_AT:
                    to_cols(fa)
                    to_cols(clipl)
                    carries(1, bwd_row)
                    to_cols(fb)
                    carries(1, fwd_row)
                    to_cols(fa)
            sort_transposes(runs_by_dst)
            to_cols(keyl)
            to_cols(fa)
            stage_end(pe, 1)

            def sum_tiles(G, S, rhs, lhs, out, ready):
                pe.wait_ge(S["sel"], G.g + 1)
                if ready:
                    pe.wait_ge(S[ready], G.g + 1)
                if G.from_(2):
                    pe.wait_ge(S["chained"], G.g - 1)
                for t in range(GROUP):
                    last = T.matmul(out[:, t * P:(t + 1) * P], lhs[:, t * P:(t + 1) * P], rhs[:, t * P:(t + 1) * P],
                                    start=True, stop=True)
                return last

            def sums(G):
                pe.wait_ge(GCN["selw"], G.g + 1)
                sum_tiles(G, GCN, selw_r[G.slot], h_r[G.slot], bank[G.slot], "h")
                for t in range(GROUP):
                    last = T.matmul(bank[2 + G.slot][0:1, t * P:(t + 1) * P], small[G.slot][:, 64 + t:65 + t],
                                    sel_r[G.slot][:, t * P:(t + 1) * P], start=True, stop=True)
                last.then_inc(GCN["sums"], 1)

            def delta(G):
                pe.wait_ge(GCN["chained"], G.g + 1)
                if G.from_(2):
                    pe.wait_ge(GCN["kept"], G.g - 1)
                for t in range(GROUP):
                    T.matmul(bank[4 + G.slot][:, t * P:(t + 1) * P], uT_r[G.slot][:, t * P:(t + 1) * P],
                             wts["W0"][:, :], start=True, stop=True)
                for t in range(GROUP):
                    last = T.matmul(bank[6 + G.slot][:, t:t + 1], row_r[G.slot][0:1, t * P:(t + 1) * P], one[0:1, 0:1],
                                    start=True, stop=True)
                last.then_inc(GCN["delta"], 1)

            def body(G):
                sums(G)
                if G.from_(1):
                    delta(G.before())
            for_groups(pe, body)
            delta(group(NG - 1))
            stage_end(pe, 2)

            def turn(G):
                pe.wait_ge(GAT["h"], G.g + 1)
                if G.from_(1):
                    pe.wait_ge(GAT["hTs"], G.g)
                for t in range(W8):
                    last = T.transpose(bank[t // 4][:, t % 4 * P:(t % 4 + 1) * P], h8[G.slot][:, t * P:(t + 1) * P], ident[:, :])
                last.then_inc(GAT["hT"], 1)

            def first(G):
                pe.wait_ge(GAT["hTs"], G.g + 1)
                if G.from_(1):
                    pe.wait_ge(GAT["xxs"], G.g)
                for k in range(2):
                    last = T.matmul(bank[2 + k][:, :], wts["W1T"][:, :], hT8[:, k * 512:(k + 1) * 512], start=True, stop=True)
                last.then_inc(GAT["xx"], 1)

            def second(G):
                pe.wait_ge(GAT["xxs"], G.g + 1)
                if G.from_(1):
                    pe.wait_ge(GAT["kept"], G.g)
                    pe.wait_ge(GAT["logits"], G.g)
                for t in range(GROUP):
                    T.matmul(bank[4][:, t * P:(t + 1) * P], xxT8[:, t * P:(t + 1) * P], wts["WgT"][:, :], start=True, stop=True)
                for t in range(GROUP):
                    o = bank[5][:, t * H:(t + 1) * H]
                    T.matmul(o, xxT8[:, t * P:(t + 1) * P], attw[:, 0:4], start=True, stop=False)
                    last = T.matmul(o, xxT8[:, 512 + t * P:512 + (t + 1) * P], attw[:, 4:8], start=False, stop=True)
                last.then_inc(GAT["hh"], 1)

            def body(G):
                turn(G)
                if G.from_(1):
                    second(G.before())
                first(G)
            for_groups(pe, body)
            second(group(NG - 1))
            stage_end(pe, 3)

            asked_next()
            alc = al[:, :].rearrange("p (t h) -> p t h", h=H)
            for h in range(H):
                for b in range(2):
                    c0 = (h % 2) * F + b * P
                    last = T.transpose(bank[2 + h // 2][0:LANES, c0:c0 + P], alc[:, b::2, h], ident[:, :])
            last.then_inc(answered, 1)
            carries(H, fwd_row)
            carries(H, bwd_row)
            carries(H, fwd_row)
            carries(H, bwd_row)
            asked_next()
            for h in range(H):
                for b in range(2):
                    c0 = (h % 2) * TILES + b * LANES
                    last = T.transpose(bank[2 + h // 2][:, c0:c0 + LANES], tt4[:, h * F + b * P:h * F + (b + 1) * P],
                                       ident[0:LANES, 0:LANES])
            last.then_inc(answered, 1)
            stage_end(pe, 4)

            def sums(G):
                sum_tiles(G, GATSUM, sel_r[G.slot], h_r[G.slot], bank[G.slot], None).then_inc(GATSUM["sums"], 1)

            def delta(G):
                pe.wait_ge(GATSUM["z"], G.g + 1)
                if G.from_(2):
                    pe.wait_ge(GATSUM["kept"], G.g - 1)
                for t in range(GROUP):
                    o = bank[4 + G.slot][:, t * P:(t + 1) * P]
                    T.matmul(o, one[0:1, :], negc1[0:1, :], start=True, stop=False)
                    last = T.matmul(o, z_r[G.slot][:, t * P:(t + 1) * P], wts["W2T"][:, :], start=False, stop=True)
                last.then_inc(GATSUM["delta"], 1)

            def body(G):
                sums(G)
                if G.from_(2):
                    delta(G.before(2))
            for_groups(pe, body)
            delta(group(NG - 2))
            delta(group(NG - 1))
            stage_end(pe, 5)

            def sums(G):
                sum_tiles(G, HYP, sel_r[G.slot], h_r[G.slot], bank[G.slot], "h").then_inc(HYP["sums"], 1)

            def turn(G):
                pe.wait_ge(HYP["chained"], G.g + 1)
                if G.from_(2):
                    pe.wait_ge(HYP["hes"], G.g - 1)
                for t in range(GROUP):
                    last = T.transpose(bank[4 + G.slot][:, t * P:(t + 1) * P], uT_r[G.slot][:, t * P:(t + 1) * P], ident[:, :])
                last.then_inc(HYP["he"], 1)

            def body(G):
                sums(G)
                if G.from_(1):
                    turn(G.before())
            for_groups(pe, body)
            turn(group(NG - 1))
            stage_end(pe, 6)

            def sums(G):
                rows_in.wait(pe, "HYPSUM", G)
                sum_tiles(G, HYPSUM, sel_r[G.slot], rows_r[G.place], bank[G.slot], None).then_inc(HYPSUM["sums"], 1)

            def delta(G):
                pe.wait_ge(HYPSUM["chained"], G.g + 1)
                if G.from_(1):
                    pe.wait_ge(HYPSUM["kept"], G.g)
                for t in range(GROUP):
                    last = T.matmul(bank[2][:, t * P:(t + 1) * P], uT_r[G.slot][:, t * P:(t + 1) * P],
                                    wts["L2T"][:, :], start=True, stop=True)
                last.then_inc(HYPSUM["delta"], 1)

            def net_in(G):
                pe.wait_ge(HYPSUM["at"], G.g + 1)
                for t in range(GROUP):
                    last = T.transpose(bank[3][0:NSC, t * P:(t + 1) * P], small[G.slot][:, t * NSC:(t + 1) * NSC], ident[:, :])
                last.then_inc(HYPSUM["atT"], 1)

            def net_mid(G):
                pe.wait_ge(HYPSUM["atTs"], G.g + 1)
                T.matmul(bank[5][0:HID, :], fc1[:, :], row_r[0][0:NSC, :], start=True, stop=True).then_inc(HYPSUM["fc"], 1)

            def net_out(G):
                pe.wait_ge(HYPSUM["fcs"], G.g + 1)
                if G.from_(1):
                    pe.wait_ge(HYPSUM["ws"], G.g)
                for t in range(GROUP):
                    last = T.matmul(bank[6][:, t * P:(t + 1) * P], z_r[0][0:HID, t * P:(t + 1) * P], fc2[:, :],
                                    start=True, stop=True)
                last.then_inc(HYPSUM["w"], 1)

            def body(G):
                net_in(G)
                sums(G)
                net_mid(G)
                if G.from_(1):
                    delta(G.before())
                net_out(G)
            for_groups(pe, body)
            delta(group(NG - 1))
            stage_end(pe, 7)

            def turn(G):
                pe.wait_ge(TP["h"], G.g + 1)
                if G.from_(1):
                    pe.wait_ge(TP["hTs"], G.g)
                for t in range(GROUP):
                    last = T.transpose(bank[0][:, t * P:(t + 1) * P], h_r[G.slot][:, t * P:(t + 1) * P], ident[:, :])
                last.then_inc(TP["hT"], 1)

            def linear(G):
                pe.wait_ge(TP["hTs"], G.g + 1)
                if G.from_(2):
                    pe.wait_ge(TP["feat"], G.g - 1)
                for t in range(GROUP):
                    last = T.matmul(bank[1 + G.slot][:, t * P:(t + 1) * P], hT_s[:, t * P:(t + 1) * P], wts["B1"][:, :],
                                    start=True, stop=True)
                last.then_inc(TP["e"], 1)

            def sums(G):
                pe.wait_ge(TP["feat"], G.g + 1)
                pe.wait_ge(TP["sel"], G.g + 1)
                if G.from_(2):
                    pe.wait_ge(TP["chained"], G.g - 1)
                f = feat_r[G.slot].rearrange("p (t k c) -> p t k c", t=GROUP, k=2)
                for k in range(2):
                    for t in range(GROUP):
                        last = T.matmul(bank[3 + 2 * G.slot + k][:, t * P:(t + 1) * P], f[:, t, k, :],
                                        sel_r[G.slot][:, t * P:(t + 1) * P], start=True, stop=True)
                last.then_inc(TP["sums"], 1)

            def delta(G):
                pe.wait_ge(TP["chained"], G.g + 1)
                if G.from_(1):
                    pe.wait_ge(TP["kept"], G.g)
                for t in range(GROUP):
                    o = bank[7][:, t * P:(t + 1) * P]
                    T.matmul(o, uT2_r[G.slot][:, t * P:(t + 1) * P], wts["B2a"][:, :], start=True, stop=False)
                    last = T.matmul(o, uT2_r[G.slot][:, 512 + t * P:512 + (t + 1) * P], wts["B2b"][:, :], start=False, stop=True)
                last.then_inc(TP["delta"], 1)

            def body(G):
                turn(G)
                linear(G)
                if G.from_(1):
                    sums(G.before())
                if G.from_(2):
                    delta(G.before(2))
            for_groups(pe, body)
            sums(group(NG - 1))
            delta(group(NG - 2))
            delta(group(NG - 1))
            stage_end(pe, 8)

        @block.scalar
        def _(act):
            S_ = nc.scalar

            act.wait_ge(pads_ready, 1)
            full, rest = E // F, E % F
            for to, of in ((src_i, src), (dst_i, dst)):
                act.dma_start(to[0:full, :], of[0:full * F].rearrange("(q f) -> q f", f=F)).then_inc(ids_in, 16)
                act.dma_start(to[full:full + 1, 0:rest], of[full * F:E].unsqueeze(0)).then_inc(ids_in, 16)
            full, rest = (E - 1) // F, (E - 1) % F
            act.dma_start(next_i[0:full, :], dst[1:full * F + 1].rearrange("(q f) -> q f", f=F)).then_inc(ids_in, 16)
            act.dma_start(next_i[full:full + 1, 0:rest], dst[full * F + 1:E].unsqueeze(0)).then_inc(ids_in, 16)
            full, rest = E // F, E % F
            act.wait_ge(pads_ready, 2)
            act.dma_start(wt_in[0:full, :], edge_weight[0:full * F].rearrange("(q f) -> q f", f=F)).then_inc(raw_in, 16)
            act.dma_start(wt_in[full:full + 1, 0:rest], edge_weight[full * F:E].unsqueeze(0)).then_inc(raw_in, 16)
            for to, of, c in ((at4_in, edge_attr_4, 4), (at8_in, edge_attr_8, 8)):
                act.dma_start(to[0:full, :], of[0:full * F, :].rearrange("(q f) c -> q (f c)", f=F)).then_inc(raw_in, 16)
                act.dma_start(to[full:full + 1, 0:rest * c], of[full * F:E, :].rearrange("(q f) c -> q (f c)", q=1)
                              ).then_inc(raw_in, 16)
            act.wait_ge(rec_ready, 1)
            act.dma_start(rec_raw.rearrange("(q f) c -> q (f c)", f=F), rec_st[0:LANES, :]).then_inc(raw_stored, 16)
            act.wait_ge(raw_stored, 16)

            def keep_records(name, to, n):
                def body(G):
                    of_rows(name).wait(act, name, G)
                    S_.copy(cols4(to, G, 4 * n).rearrange("p (t c) -> p t c", c=n),
                           rows_r[G.place][:, 0:4 * REC].rearrange("p (t c) -> p t c", c=REC)[:, :, 0:n]
                           ).then_inc(R["taken"], 1)
                for_groups(act, body)

            unsorted = load_unsorted(act)
            with act.If(unsorted > 0):
                keep_records("BY_DST", rec, REC)
            with act.If(unsorted < 1):
                act.dma_start(rec[:, :].rearrange("p (t c) -> p t c", c=REC),
                              rec_raw.rearrange("(t p) c -> p t c", p=P)).then_inc(raw_stored, 16)
                act.wait_ge(raw_stored, 32)
                act.sem_inc(R["taken"], NG)

            def exchange_keys(which, n_keys, n_done):
                act.wait_ge(keys_ready, n_keys)
                k = keys_dram[which]
                of = clipl if which == "clip" else keyl
                act.dma_start(k[1:EP + 1].rearrange("(q f) -> q f", f=F), of).then_inc(keys_stored, 16)
                act.dma_start(k[0:1].unsqueeze(0), edge_mark[0:1, 0:1]).then_inc(keys_stored, 16)
                act.dma_start(k[EP + 1:EP + 2].unsqueeze(0), edge_mark[0:1, 1:2]).then_inc(keys_stored, 16)
                act.wait_ge(keys_stored, 48 * n_done)

            def neighbours(which, n):
                k = keys_dram[which]
                act.dma_start(prevl, k[0:EP].rearrange("(q f) -> q f", f=F)).then_inc(keys_in, 16)
                act.dma_start(nextl, k[2:EP + 2].rearrange("(q f) -> q f", f=F)).then_inc(keys_in, 16)
                act.wait_ge(keys_in, 32 * n)

            exchange_keys("dst", 1, 1)
            neighbours("dst", 1)
            exchange_keys("clip", 2, 2)
            act.wait_ge(recs_ready, 1)
            act.dma_start(rec_d.rearrange("(t p) c -> p t c", p=P), rec[:, :].rearrange("p (t c) -> p t c", c=REC)
                          ).then_inc(recs_stored, 16)
            act.wait_ge(recs_stored, 16)
            exchange_keys("src", 3, 3)
            neighbours("src", 2)
            keep_records("BY_SRC", rec_s, 4)
            act.wait_ge(R["taken"], 2 * NG)
            stage_end(act, 1)

            def deviations(G, S, tiles):
                act.wait_ge(S["var"], G.g + 1)
                s = small[G.slot]
                S_.activation(s[:, 104:104 + tiles], s[:, 81:81 + 2 * tiles:2], ACT.Sqrt, bias=eps_col[:, :]
                             ).then_inc(S["dev"], 1)

            def norm(G, S, v, h, tiles, stat):
                act.wait_ge(S["norm"], G.g + 1)
                for t in range(tiles):
                    last = S_.activation(h[:, t * P:(t + 1) * P], v(t), ACT.Relu, bias=stat[:, 8 + t:9 + t],
                                        scale=stat[:, t:t + 1])
                last.then_inc(S["h"], 1)

            def next_keys(G, which, S):
                if not (isinstance(G.g, int) and G.g == NG - 1):
                    load_keys(act, G.after(), which, S)

            def keep(G):
                act.wait_ge(GCN["delta"], G.g + 1)
                to = cols4(big, G, GROUP * ROW).rearrange("p (t c) -> p t c", c=ROW)
                S_.copy(to[:, :, 0:D], t4(bank[4 + G.slot][:, :]))
                S_.copy(to[:, :, COL_DV], bank[6 + G.slot][:, 0:GROUP]).then_inc(GCN["kept"], 1)

            def weigh(G):
                act.wait_ge(GCN["sel"], G.g + 1)
                w4 = cols4(rec_s, G, 16)
                for t in range(GROUP):
                    c = slice(t * P, (t + 1) * P)
                    last = S_.mul(selw_r[G.slot][:, c], sel_r[G.slot][:, c], w4[:, 4 * t + R_W:4 * t + R_W + 1])
                last.then_inc(GCN["selw"], 1)

            def body(G):
                deviations(G, GCN, GROUP)
                if G.from_(2):
                    act.wait_ge(GCN["sums"], G.g - 1)
                weigh(G)
                norm(G, GCN, lambda t: v_r[G.slot][:, t * P:(t + 1) * P], h_r[G.slot], GROUP, small[G.slot])
                if G.from_(2):
                    keep(G.before(2))
                next_keys(G, "src", GCN)
            load_keys(act, group(0), "src", GCN)
            for_groups(act, body)
            keep(group(NG - 2))
            keep(group(NG - 1))
            act.wait_ge(roots, 1)
            S_.activation(dvis_s[:, :], dvis_s[:, :], ACT.Sqrt).then_inc(roots, 1)
            stage_end(act, 2)

            def keep(G):
                act.wait_ge(GAT["hh"], G.g + 1)
                S_.copy(cols4(big, G, 512), bank[4][:, :]).then_inc(GAT["kept"], 1)

            def bias(G):
                act.wait_ge(GAT["xx"], G.g + 1)
                for k in range(2):
                    last = S_.activation(xxT8[:, k * 512:(k + 1) * 512], bank[2 + k][:, :], ACT.Identity, bias=cols[:, 0:1])
                last.then_inc(GAT["xxs"], 1)

            def body(G):
                deviations(G, GAT, W8)
                if G.from_(2):
                    act.wait_ge(GAT["hT"], G.g - 1)
                norm(G, GAT, lambda t: v8[G.slot][:, t * P:(t + 1) * P], h8[G.slot], W8, small[G.slot])
                if G.from_(2):
                    keep(G.before(2))
                if G.from_(1):
                    bias(G.before())
                act.wait_ge(GAT["hT"], G.g + 1)
                for k in range(2):
                    last = S_.copy(hT8[:, k * 512:(k + 1) * 512], bank[k][:, :])
                last.then_inc(GAT["hTs"], 1)
            for_groups(act, body)
            keep(group(NG - 2))
            bias(group(NG - 1))
            keep(group(NG - 1))
            act.wait_ge(GAT["kept"], NG)
            stage_end(act, 3)

            act.dma_start(keyl, keys_dram["dst"][1:EP + 1].rearrange("(q f) -> q f", f=F)).then_inc(keys_in, 16)
            act.dma_start(prevl, keys_dram["dst"][0:EP].rearrange("(q f) -> q f", f=F)).then_inc(keys_in, 16)
            act.dma_start(nextl, keys_dram["dst"][2:EP + 2].rearrange("(q f) -> q f", f=F)).then_inc(keys_in, 16)
            act.wait_ge(keys_in, 32 * 2 + 48)
            S_.activation(exp_warm[:, :], zero_col[:, :], ACT.Exp)
            act.wait_ge(exp_asked, 1)
            S_.activation(alb, alb, ACT.Exp).then_inc(exp_done, 1)
            act.wait_ge(exp_done, 1)
            stage_end(act, 4)

            def biased(G):
                act.wait_ge(GATSUM["chained"], G.g + 1)
                if G.from_(2):
                    act.wait_ge(GATSUM["z"], G.g - 1)
                S_.activation(t1_r[G.slot], uT_r[G.slot], ACT.Identity, bias=cols[:, 1:2]).then_inc(GATSUM["biased"], 1)

            def keep(G):
                act.wait_ge(GATSUM["delta"], G.g + 1)
                if G.from_(UNROLL):
                    added.wait(act, "GATSUM", G.before(UNROLL))
                S_.copy(dl4_r[G.place].rearrange("p (t c) -> p t c", c=ROW)[:, :, 0:D], t4(bank[4 + G.slot][:, :])
                       ).then_inc(GATSUM["kept"], 1)

            def body(G):
                if G.from_(1):
                    biased(G.before())
                if G.from_(2):
                    keep(G.before(2))
            for_groups(act, body)
            biased(group(NG - 1))
            keep(group(NG - 2))
            keep(group(NG - 1))
            act.wait_ge(roots, 3)
            S_.activation(wt_col[:, :], wt_col[:, :], ACT.Sqrt).then_inc(roots, 1)
            stage_end(act, 5)

            def keep(G):
                act.wait_ge(HYP["he"], G.g + 1)
                if G.from_(2):
                    hes_stored.wait(act, "HYP", G.before(2))
                s4 = cols4(hsc_col, G)
                for t in range(GROUP):
                    last = S_.mul(dl_r[G.slot][:, t * P:(t + 1) * P], bank[4 + G.slot][:, t * P:(t + 1) * P], s4[:, t:t + 1])
                last.then_inc(HYP["hes"], 1)

            def body(G):
                deviations(G, HYP, GROUP)
                if G.from_(2):
                    act.wait_ge(HYP["sums"], G.g - 1)
                norm(G, HYP, lambda t: v_r[G.slot][:, t * P:(t + 1) * P], h_r[G.slot], GROUP, small[G.slot])
                if G.from_(2):
                    keep(G.before(2))
            for_groups(act, body)
            keep(group(NG - 2))
            keep(group(NG - 1))
            stage_end(act, 6)

            def keep(G):
                act.wait_ge(HYPSUM["delta"], G.g + 1)
                if G.from_(UNROLL):
                    added.wait(act, "HYPSUM", G.before(UNROLL))
                s4 = cols4(dvis_s, G)
                for t in range(GROUP):
                    last = S_.mul(dl4h_r[G.place][:, t * ROW:t * ROW + D], bank[2][:, t * P:(t + 1) * P], s4[:, t:t + 1])
                last.then_inc(HYPSUM["kept"], 1)

            def attrs(G):
                if G.from_(2):
                    act.wait_ge(HYPSUM["atT"], G.g - 1)
                S_.copy(small[G.slot][:, 0:GROUP * NSC].rearrange("p (t c) -> p t c", c=NSC),
                       cols4(rec, G, GROUP * REC).rearrange("p (t c) -> p t c", c=REC)[:, :, R_A8:R_A8 + NSC]
                       ).then_inc(HYPSUM["at"], 1)

            def body(G):
                attrs(G)
                act.wait_ge(HYPSUM["atT"], G.g + 1)
                if G.from_(1):
                    act.wait_ge(HYPSUM["fc"], G.g)
                S_.copy(row_r[0][0:NSC, :], bank[3][0:NSC, :]).then_inc(HYPSUM["atTs"], 1)
                act.wait_ge(HYPSUM["fc"], G.g + 1)
                if G.from_(1):
                    act.wait_ge(HYPSUM["w"], G.g)
                S_.activation(z_r[0][0:HID, :], bank[5][0:HID, :], ACT.Silu, scale=1.0 / math.sqrt(NSC)
                             ).then_inc(HYPSUM["fcs"], 1)
                if G.from_(1):
                    keep(G.before())
                act.wait_ge(HYPSUM["w"], G.g + 1)
                if G.from_(2):
                    act.wait_ge(HYPSUM["wide"], G.g - 1)
                S_.copy(t1_r[G.slot], bank[6][:, :]).then_inc(HYPSUM["ws"], 1)
            for_groups(act, body)
            keep(group(NG - 1))
            stage_end(act, 7)

            def keep(G):
                act.wait_ge(TP["delta"], G.g + 1)
                b4 = cols4(sc_d, G, 16)
                to = cols4(big, G, GROUP * ROW)
                for t in range(GROUP):
                    last = S_.mul(to[:, t * ROW:t * ROW + D], bank[7][:, t * P:(t + 1) * P], b4[:, 4 * t + 1:4 * t + 2])
                last.then_inc(TP["kept"], 1)

            def body(G):
                deviations(G, TP, GROUP)
                if G.from_(2):
                    act.wait_ge(TP["hT"], G.g - 1)
                norm(G, TP, lambda t: cols4(big, G, GROUP * ROW)[:, t * ROW:t * ROW + D], h_r[G.slot], GROUP, small[G.slot])
                if G.from_(2):
                    act.wait_ge(TP["feat"], G.g - 1)
                act.dma_start(w_r[G.slot], at(w_dram, G, 1024)).then_inc(w_in.of(G), 16)
                act.wait_ge(TP["hT"], G.g + 1)
                if G.from_(1):
                    act.wait_ge(TP["e"], G.g)
                S_.copy(hT_s, bank[0][:, :]).then_inc(TP["hTs"], 1)
                if G.from_(3):
                    keep(G.before(3))
                next_keys(G, "dst", TP)
            load_keys(act, group(0), "dst", TP)
            for_groups(act, body)
            keep(group(NG - 3))
            keep(group(NG - 2))
            keep(group(NG - 1))
            act.wait_ge(TP["kept"], NG)
            stage_end(act, 8)

        @block.vector
        def _(dve):
            V = nc.vector
            order = Order(dve, vec)
            link, done, need = order.link, order.done, order.need
            count = [0]

            def ask(ins):
                count[0] += 1
                ins.then_inc(asked, 1)
                dve.wait_ge(answered, count[0])

            V.memset(src_i, N)
            V.memset(dst_i, N)
            V.memset(next_i, N).then_inc(pads_ready, 1)
            V.memset(wt_in, 0.0)
            V.memset(at4_in, 0.0)
            V.memset(at8_in, 0.0)
            V.memset(zeros, 0.0).then_inc(pads_ready, 1)

            dve.wait_ge(ids_in, 16 * 6)
            dve.wait_ge(consts_ready, 2)
            link(V.tensor_copy(key_f, dst_i))
            link(V.tensor_tensor(tmp_f, key_f, next_i, ALU.is_gt))
            ask(V.tensor_reduce(worst, tmp_f, AX.X, ALU.max))
            V.tensor_reduce(steps_down[:, :], bank[1][0:1, 0:P], AX.X, ALU.max).then_inc(flag_ready, 1)

            dve.wait_ge(dvec_in, 48)
            V.tensor_copy(nvh, hw_last.broadcast_to([P, PER_LANE])).then_inc(dense_ready, 1)

            dve.wait_ge(raw_in, 16 * 6)
            r16 = rec_st.rearrange("p (f c) -> p f c", c=REC)
            link(V.tensor_copy(r16[:, :, R_SRC], src_i))
            link(V.tensor_copy(r16[:, :, R_DST], dst_i))
            link(V.tensor_copy(r16[:, :, R_W], wt_in))
            link(V.memset(r16[:, :, R_LAST], 0.0))
            link(V.tensor_copy(r16[:, :, R_A4:R_A4 + 4], at4_in.rearrange("p (f c) -> p f c", c=4)))
            V.tensor_copy(r16[:, :, R_A8:R_A8 + 8], at8_in.rearrange("p (f c) -> p f c", c=8)).then_inc(rec_ready, 1)

            link(V.tensor_scalar(gray, pos[:, :], 1, None, ALU.logical_shift_right))
            link(V.tensor_tensor(gray, gray, pos[:, :], ALU.bitwise_xor))

            def to_int(ap):
                return ap.bitcast(i32)

            def turn_signs(k):
                of, by = (pos[:, :], 30) if k == 0 else (gray, 31 - k)
                link(V.tensor_scalar(flip, of, by, SIGN, ALU.logical_shift_left, ALU.bitwise_and))
                link(V.tensor_tensor(to_int(sort_b[0]), to_int(sort_b[0]), flip, ALU.bitwise_xor))

            def step(bufs, b, dist, ask_pe=False):
                x_ = bufs[b].rearrange("p (n two d) -> p n two d", two=2, d=dist)
                y_ = bufs[1 - b].rearrange("p (n two d) -> p n two d", two=2, d=dist)
                done(V.tensor_tensor(y_[:, :, 0, :], x_[:, :, 0, :], x_[:, :, 1, :], ALU.min))
                ins = V.tensor_tensor(y_[:, :, 1, :], x_[:, :, 0, :], x_[:, :, 1, :], ALU.max)
                if ask_pe:
                    ask(ins)
                else:
                    link(ins)

            def sort(kf, between=lambda k: None):
                m_i = to_int(tmp_g)
                link(V.tensor_scalar(tmp_f, kf, float(-MID), None, ALU.add))
                link(V.scalar_tensor_tensor(tmp_f, tmp_f, -1.0, tmp_f, ALU.mult, ALU.max))
                link(V.tensor_scalar(m_i, tmp_f, float(LEAST), None, ALU.add))
                link(V.scalar_tensor_tensor(to_int(sort_b[0]), m_i, LOG, pos[:, :], ALU.logical_shift_left, ALU.bitwise_or))
                link(V.tensor_scalar(m_i, kf, float(MID), None, ALU.is_lt))
                link(V.scalar_tensor_tensor(to_int(sort_b[0]), m_i, 31, to_int(sort_b[0]), ALU.logical_shift_left, ALU.bitwise_or))
                turn_signs(0)
                for k in range(1, LOG + 1):
                    b = 0
                    if k <= 8:
                        dists = [1 << j for j in range(k - 1, -1, -1)]
                        for d_ in dists:
                            step(sort_b, b, d_)
                            b = 1 - b
                        if b:
                            link(V.tensor_copy(sort_b[0], sort_b[1]))
                    else:
                        for_ask = V.tensor_copy(sort_a[1][:, 0:1], sort_b[0][:, 0:1])
                        ask(for_ask)
                        link(V.tensor_copy(sort_a[0].rearrange("p (q b) -> p b q", b=2),
                                           bank[0][:, 0:F].rearrange("p (b q) -> p b q", b=2)))
                        a = 0
                        for j in range(k - 1, 7, -1):
                            step(sort_a, a, (1 << j) // P, ask_pe=(j == 8))
                            a = 1 - a
                        link(V.tensor_copy(sort_b[0], bank[0][:, 0:F]))
                        for j in range(7, -1, -1):
                            step(sort_b, b, 1 << j)
                            b = 1 - b
                    if k < LOG:
                        turn_signs(k)
                    between(k)
                ask(V.tensor_copy(sort_a[1][:, 0:1], sort_b[0][:, 0:1]))
                link(V.tensor_copy(sort_a[0].rearrange("p (q b) -> p b q", b=2),
                                   bank[0][:, 0:F].rearrange("p (b q) -> p b q", b=2)))

            def unpack(edge_idx, n):
                link(V.tensor_scalar(to_int(tmp_g)[:, 0:TILES], to_int(sort_a[0])[:, 0:TILES], (1 << LOG) - 1, None,
                                     ALU.bitwise_and))
                V.tensor_scalar(edge_idx[:, :], to_int(tmp_g)[:, 0:TILES], float(EP - 1), None, ALU.min).then_inc(e_ready, 1)
                s_i = to_int(sort_b[0])[0:LANES, :]
                link(V.tensor_scalar(to_int(tmp_f)[0:LANES, :], s_i, LOG, 0xffff, ALU.logical_shift_right, ALU.bitwise_and))
                link(V.tensor_scalar(fa, to_int(tmp_f)[0:LANES, :], float(-LEAST), None, ALU.add))
                link(V.tensor_scalar(to_int(tmp_f)[0:LANES, :], s_i, 31, None, ALU.logical_shift_right))
                link(V.tensor_scalar(fb, to_int(tmp_f)[0:LANES, :], -2.0, 1.0, ALU.mult, ALU.add))
                link(V.tensor_tensor(fa, fa, fb, ALU.mult))
                V.tensor_scalar(keyl, fa, float(MID), None, ALU.add).then_inc(keys_ready, 1)
                dve.wait_ge(keys_ready, n)

            def to_cols(ins, out):
                ask(ins)
                link(V.tensor_copy(out.rearrange("p (q b) -> p b q", b=2),
                                   bank[0][:, 0:TILES].rearrange("p (b q) -> p b q", b=2)))

            def run_flags(k_, p_, n_):
                done(V.tensor_tensor(sprev, k_, p_, ALU.is_equal))
                done(V.tensor_tensor(snext, k_, n_, ALU.is_equal))
                done(V.tensor_scalar(eqp, k_, p_[:, 0:1], None, ALU.is_equal))
                done(V.tensor_scalar(eqn, k_, n_[:, F - 1:F], None, ALU.is_equal))
                link(V.tensor_tensor(isl, k_, n_, ALU.not_equal))

            def carries(n, ends_of, z_of, op1, op0, initial, forward):
                link(V.tensor_copy(ends[:, 0:n], ends_of))
                ask(V.tensor_copy(endz[:, 0:n], z_of.broadcast_to([LANES, n])))
                done(V.memset(run[0:n, :], initial))
                link(V.tensor_copy(rows[0:n, 0:2 * LANES], bank[1][0:n, 0:2 * LANES]))
                if forward:
                    ask(V.tensor_tensor_scan(run[0:n, 1:LANES + 1], rows[0:n, LANES:2 * LANES], rows[0:n, 0:LANES],
                                             initial, op0, op1))
                else:
                    ask(V.tensor_tensor_scan(run[0:n, LANES - 1::-1], rows[0:n, 2 * LANES - 1:LANES - 1:-1],
                                             rows[0:n, LANES - 1::-1], initial, op0, op1))
                link(V.tensor_copy(carry[:, 0:n], bank[1][0:LANES, 256:256 + n]))

            def head(ap, h):
                return ap[:, h * F:(h + 1) * F]

            def ends_of(ap, n, c):
                return ap[:, c:n * F:F]

            def run_sums(v, out, n):
                for h in range(n):
                    last = V.tensor_tensor_scan(head(out, h), sprev, head(v, h), 0.0, ALU.mult, ALU.add)
                    done(last)
                need(order.off)
                carries(n, ends_of(out, n, F - 1), eqp[:, F - 1:F], ALU.add, ALU.mult, 0.0, True)
                for h in range(n):
                    done(V.scalar_tensor_tensor(head(out, h), eqp, carry[:, h:h + 1], head(out, h), ALU.mult, ALU.add))
                need(order.off)

            def spread_last(v, out, n):
                for h in range(n):
                    done(V.tensor_tensor_scan(head(out, h)[:, ::-1], snext[:, ::-1], head(v, h)[:, ::-1], 0.0,
                                              ALU.mult, ALU.add))
                need(order.off)
                carries(n, ends_of(out, n, 0), eqn[:, 0:1], ALU.add, ALU.mult, 0.0, False)
                for h in range(n):
                    done(V.scalar_tensor_tensor(head(out, h), eqn, carry[:, h:h + 1], head(out, h), ALU.mult, ALU.add))
                need(order.off)

            def targets(add_idx):
                link(V.tensor_tensor(fa, keyl, trash, ALU.subtract))
                link(V.tensor_tensor(fa, fa, isl, ALU.mult))
                to_cols(V.tensor_tensor(fa, fa, trash, ALU.add), add_idx[:, :])

            def dense_rest():
                dve.wait_ge(dvec_in, 80)
                with dve.Fori(POOL_STEPS, STEPS) as i:
                    for q in range(DBUF):
                        dense_chunk(V, dve, i, q)
                dense_chunk(V, dve, STEPS, 0)
                dve.wait_ge(left_in, 48)
                done(V.tensor_copy(left_rows[:, COL_HW:COL_HW + 1], hw_last[0:LEFT, :]))
                done(V.memset(left_rows[:, COL_DV:COL_DV + 1], 0.0))
                done(V.tensor_copy(zeros[0:1, COL_HW:COL_HW + 1], hw_last[0:1, :]))
                V.tensor_tensor(left_rows[:, 0:D], left_rows[:, 0:D], wts["C"][0:LEFT, :], ALU.add).then_inc(left_sum, 1)

            unsorted = load_unsorted(dve)
            start, start_asked = order.off, count[0]
            with dve.If(unsorted > 0):
                sort(key_f)
                unpack(idx["e_d"], 1)
                dve.wait_ge(R["taken"], NG)
                done(V.memset(key_f, float(N)))
                ask(V.memset(tmp_g[:, 0:1], 0.0))
                link(V.tensor_copy(key_f[0:LANES, :], bank[0][0:LANES, 0:F]))
            with dve.If(unsorted < 1):
                link_, order.off = order.off, start
                V.tensor_copy(keyl, key_f[0:LANES, :]).then_inc(keys_ready, 1)
                dve.wait_ge(keys_ready, 1)
                done(V.tensor_copy(key_f, src_i))
                dve.sem_inc(e_ready, 1)
                dve.sem_inc(asked, count[0] - start_asked)
                dve.sem_inc(vec, link_ - order.off)
                order.off = link_
            to_cols(V.tensor_copy(fb, keyl), key_col["dst"][:, :])

            rec3 = rec[:, :].rearrange("p (t c) -> p t c", c=REC)
            def prepare_weights():
                dve.wait_ge(weights_in, 16 * N_WEIGHTS)
                bg, lbg = cols[:, 1:2], cols[:, 2:3]
                link(V.scalar_tensor_tensor(lbg, bg, 0.01, bg, ALU.mult, ALU.max))
                ask(V.tensor_copy(wts["lbgB"][:, :], lbg.broadcast_to([P, P])))
                link(V.tensor_copy(attw[:, :], bank[1][:, 0:8]))
                for k, w in enumerate(("W1T", "WgT", "L2T")):
                    b = {"W1T": 0, "WgT": 1, "L2T": 3}[w]
                    link(V.tensor_copy(wts[w][:, :], bank[0][:, b * P:(b + 1) * P]))
                ask(V.tensor_copy(wts["W2T"][:, :], bank[0][:, 2 * P:3 * P]))
                link(V.tensor_scalar(negc1[:, :], bank[1][0:1, 128:256], -1.0, None, ALU.mult))
                link(V.tensor_tensor(wts["K1"][:, :], wts["K1"][:, :], bank[1][:, 128:256], ALU.add))
                link(V.tensor_tensor(wts["K1"][:, :], wts["K1"][:, :], wts["K2"][:, :], ALU.add))
                V.tensor_tensor(wts["C"][:, :], wts["C"][:, :], wts["K1"][:, :], ALU.add).then_inc(biases_ready, 1)
                link(V.tensor_scalar(wts["B1"][:, :], wts["B1"][:, :], 1.0 / math.sqrt(MUL), None, ALU.mult))
                out_scale = 1.0 / math.sqrt(2.0 * MUL) / math.sqrt(16.0)
                for k, b in enumerate(("B2a", "B2b")):
                    link(V.tensor_scalar(wts[b][0:32, 0:32], wts[b][0:32, 0:32],
                                         out_scale if k == 0 else out_scale / math.sqrt(3.0), None, ALU.mult))
                    for a in range(3):
                        r = slice(32 + 32 * a, 64 + 32 * a)
                        link(V.tensor_scalar(wts[b][r, 32 + a:P:3], wv_st[r, 32 * k:32 * k + 32], out_scale, None, ALU.mult))
                link(V.tensor_scalar(fc2[:, :], fc2[:, :], 1.0 / math.sqrt(HID), None, ALU.mult))

            def meanwhile(k):
                if k == WEIGHTS_AT:
                    prepare_weights()
                if k != RUNS_AT:
                    return
                dve.wait_ge(R["taken"], NG)
                dve.wait_ge(keys_in, 32)
                run_flags(keyl, prevl, nextl)
                link(V.tensor_scalar(to_int(posf), pos[0:LANES, :], SPARE - 1, None, ALU.bitwise_and))
                link(V.tensor_scalar(trash, to_int(posf), float(N + 1), None, ALU.add))
                link(V.tensor_copy(posf, pos[0:LANES, :]))
                targets(idx["add_d"])
                link(V.tensor_scalar(clprev, prevl, float(M - 1), None, ALU.min))
                link(V.tensor_scalar(clnext, nextl, float(M - 1), None, ALU.min))
                V.tensor_scalar(clipl, keyl, float(M - 1), None, ALU.min).then_inc(keys_ready, 1)
                dve.wait_ge(keys_ready, 2)
                to_cols(V.tensor_copy(fb, clipl), key_col["clip"][:, :])
                run_flags(clipl, clprev, clnext)
                link(V.tensor_tensor(fa, posf, isl, ALU.mult))
                spread_last(fa, fb, 1)
                ask(V.tensor_copy(fa, fb))
                V.tensor_copy(rec3[:, :, R_LAST].rearrange("p (q b) -> p b q", b=2),
                              bank[0][:, 0:TILES].rearrange("p (b q) -> p b q", b=2)).then_inc(recs_ready, 1)
                dve.wait_ge(recs_ready, 1)
                link(V.tensor_scalar(fb, keyl, float(M), None, ALU.is_lt))
                run_sums(fb, fa, 1)
                to_cols(V.tensor_copy(clnext, fa), cnt_col[:, :])
                link(V.tensor_copy(idx["src_d"][:, :], rec3[:, :, R_SRC]))
                link(V.tensor_copy(idx["dst_d"][:, :], rec3[:, :, R_DST]))

            sort(key_f, meanwhile)
            dve.wait_ge(keys_stored, 96)
            unpack(idx["e_s"], 3)
            dense_rest()
            to_cols(V.tensor_copy(fb, keyl), key_col["src"][:, :])
            dve.wait_ge(keys_in, 64)
            run_flags(keyl, prevl, nextl)
            targets(idx["add_s"])
            dve.wait_ge(R["taken"], 2 * NG)
            rs = rec_s[:, :].rearrange("p (t c) -> p t c", c=4)
            link(V.tensor_copy(idx["dst_s"][:, :], rs[:, :, R_DST]))
            link(V.tensor_copy(idx["last_s"][:, :], rs[:, :, R_LAST]))
            stage_end(dve, 1)

            def variances(G, S, tiles):
                plain(dve)
                s = small[G.slot]
                for t in range(tiles):
                    ins = V.bn_aggr(s[:, 80 + 2 * t:82 + 2 * t], s[:, 16 + 6 * t:22 + 6 * t])
                    if t < tiles - 1:
                        done(ins)
                ins.then_inc(S["var"], 1)

            def statistics(G, S, v, tiles):
                s = small[G.slot]
                for t in range(tiles):
                    done(V.bn_stats(s[:, 16 + 6 * t:22 + 6 * t], v(t)))
                need(order.off)
                variances(G, S, tiles)

            def scales(G, S, tiles):
                s = small[G.slot]
                dve.wait_ge(S["dev"], G.g + 1)
                link(V.reciprocal(s[:, 0:tiles], s[:, 104:104 + tiles]))
                V.scalar_tensor_tensor(s[:, 8:8 + tiles], s[:, 80:80 + 2 * tiles:2], -1.0, s[:, 0:tiles],
                                       ALU.mult, ALU.mult).then_inc(S["norm"], 1)

            def going_on(G, name):
                keys_at.wait(dve, name, G)
                k = keys_r[G.slot]
                here = t4(k[:, 1:GE + 1])
                done(V.tensor_tensor(t4(ind_r[G.slot]), here, wide(k[:, 0:GE:P]), ALU.is_equal))
                return here

            def matrices(G, S, which, name):
                here = going_on(G, name)
                V.tensor_tensor(t4(sel_r[G.slot]), here, wide(cols4(key_col[which], G)), ALU.is_equal).then_inc(S["sel"], 1)

            def carry_on(G, banks, ring_, t, k):
                o = 512 * k
                if t:
                    before = ring_[G.slot][:, o + t * P - 1:o + t * P]
                elif G.from_(1):
                    before = ring_[1 - G.slot][:, o + 511:o + 512]
                else:
                    before = zero_col[:, :]
                return V.scalar_tensor_tensor(ring_[G.slot][:, o + t * P:o + (t + 1) * P],
                                              ind_r[G.slot][:, t * P:(t + 1) * P], before,
                                              banks[k][:, t * P:(t + 1) * P], ALU.mult, ALU.add)

            def chain(G, S, banks, ring_, free):
                dve.wait_ge(S["sums"], G.g + 1)
                if G.from_(2):
                    dve.wait_ge(S[free], G.g - 1)
                for t in range(GROUP):
                    for k in range(len(banks)):
                        ins = carry_on(G, banks, ring_, t, k)
                        if t < GROUP - 1 or k < len(banks) - 1:
                            done(ins)
                    if t < GROUP - 1:
                        need(order.off)
                ins.then_inc(S["chained"], 1)
                dve.wait_ge(S["chained"], G.g + 1)

            def front(G):
                big_in.wait(dve, "GCN", G)
                r = cols4(big, G, GROUP * ROW).rearrange("p (t c) -> p t c", c=ROW)
                if G.from_(2):
                    dve.wait_ge(GCN["sums"], G.g - 1)
                done(V.tensor_tensor(t4(v_r[G.slot]), r[:, :, 0:D], over(wts["C"][:, :], GROUP), ALU.subtract))
                done(V.tensor_copy(small[G.slot][:, 64:68], r[:, :, COL_HW]))
                need(order.off)
                done(V.tensor_copy(r[:, :, D:COL_DV], wide(zero_col[:, :].broadcast_to([P, GROUP]), 3)))
                statistics(G, GCN, lambda t: v_r[G.slot][:, t * P:(t + 1) * P], GROUP)
                matrices(G, GCN, "src", "GCN")
                scales(G, GCN, GROUP)

            def chains(G):
                dve.wait_ge(GCN["sums"], G.g + 1)
                if G.from_(2):
                    dve.wait_ge(GCN["delta"], G.g - 1)
                for t in range(GROUP):
                    c = slice(t * P, (t + 1) * P)
                    if t:
                        u0, d0 = uT_r[G.slot][:, t * P - 1:t * P], row_r[G.slot][0:1, t * P - 1:t * P]
                    elif G.from_(1):
                        u0, d0 = uT_r[1 - G.slot][:, 511:512], row_r[1 - G.slot][0:1, 511:512]
                    else:
                        u0, d0 = zero_col[:, :], zero_col[0:1, :]
                    done(V.scalar_tensor_tensor(row_r[G.slot][0:1, c], ind_r[G.slot][0:1, c], d0,
                                                bank[2 + G.slot][0:1, c], ALU.mult, ALU.add))
                    ins = V.scalar_tensor_tensor(uT_r[G.slot][:, c], ind_r[G.slot][:, c], u0, bank[G.slot][:, c],
                                                 ALU.mult, ALU.add)
                    if t < GROUP - 1:
                        link(ins)
                ins.then_inc(GCN["chained"], 1)
                dve.wait_ge(GCN["chained"], G.g + 1)

            def body(G):
                front(G)
                if G.from_(1):
                    chains(G.before())
            for_groups(dve, body, order)
            chains(group(NG - 1))
            dve.wait_ge(GCN["kept"], NG)
            V.tensor_scalar(dvis_s[:, :], big[:, :].rearrange("p (t c) -> p t c", c=ROW)[:, :, COL_DV],
                            1.0, None, ALU.max).then_inc(roots, 1)
            dve.wait_ge(roots, 2)
            link(V.reciprocal(dvis_s[:, :], dvis_s[:, :]))
            stage_end(dve, 2)

            def logits(G):
                dve.wait_ge(GAT["hh"], G.g + 1)
                done(V.tensor_copy(small[G.slot][:, 112:128], bank[5][:, 0:16]))
                need(order.off)
                V.scalar_tensor_tensor(cols4(al, G, 16), small[G.slot][:, 112:128], 0.2, small[G.slot][:, 112:128],
                                       ALU.mult, ALU.max).then_inc(GAT["logits"], 1)

            def body(G):
                rows_in.wait(dve, "GAT", G)
                if G.from_(2):
                    dve.wait_ge(GAT["h"], G.g - 1)
                r = rows8_r[G.place].rearrange("p (t c) -> p t c", c=ROW)
                done(V.tensor_tensor(t4(v8[G.slot]), r[:, :, 0:D], over(wts["K1"][:, :], W8), ALU.subtract))
                done(V.tensor_copy(cols4(sc_s, G, 16).rearrange("p (t c) -> p t c", c=4), r[:, 0:GROUP, D:ROW]))
                V.tensor_copy(cols4(sc_d, G, 16).rearrange("p (t c) -> p t c", c=4), r[:, GROUP:W8, D:ROW]
                              ).then_inc(GAT["taken"], 1)
                need(order.off)
                statistics(G, GAT, lambda t: v8[G.slot][:, t * P:(t + 1) * P], W8)
                scales(G, GAT, W8)
                if G.from_(2):
                    logits(G.before(2))
            for_groups(dve, body, order)
            logits(group(NG - 2))
            logits(group(NG - 1))
            dve.wait_ge(GAT["logits"], NG)
            s4 = sc_s[:, :].rearrange("p (t c) -> p t c", c=4)
            d4 = sc_d[:, :].rearrange("p (t c) -> p t c", c=4)
            stage_end(dve, 3)

            dve.wait_ge(keys_in, 64 + 48)
            run_flags(keyl, prevl, nextl)
            ask(V.tensor_copy(fb, keyl))
            for k in range(2):
                done(V.tensor_copy(alb[:, 512 * k:512 * (k + 1)], bank[2 + k][0:LANES, :]))
            need(order.off)
            link(V.tensor_scalar(fa, sprev, 1.0, BIG_NUM, ALU.subtract, ALU.mult))
            link(V.tensor_scalar(fb, eqp, 1.0, BIG_NUM, ALU.subtract, ALU.mult))
            for h in range(H):
                done(V.tensor_tensor_scan(head(fw, h), fa, head(alb, h), -BIG_NUM, ALU.add, ALU.max))
            need(order.off)
            carries(H, ends_of(fw, H, F - 1), fb[:, F - 1:F], ALU.max, ALU.add, -BIG_NUM, True)
            for h in range(H):
                done(V.scalar_tensor_tensor(head(fw, h), fb, carry[:, h:h + 1], head(fw, h), ALU.add, ALU.max))
            need(order.off)
            h4 = lambda ap: ap.rearrange("p (h f) -> p h f", h=H)
            link(V.tensor_tensor(h4(fw), h4(fw), over(isl, H), ALU.mult))
            spread_last(fw, bw, H)
            V.tensor_tensor(alb, alb, bw, ALU.subtract).then_inc(exp_asked, 1)
            dve.wait_ge(exp_done, 1)
            run_sums(alb, fw, H)
            link(V.scalar_tensor_tensor(h4(fw), h4(fw), 1e-16, over(isl, H), ALU.add, ALU.mult))
            spread_last(fw, bw, H)
            link(V.reciprocal(bw, bw))
            ask(V.tensor_tensor(tt4, alb, bw, ALU.mult))
            alc = al[:, :].rearrange("p (q b h) -> p h b q", b=2, h=H)
            for h in range(H):
                c0 = (h % 2) * TILES
                link(V.tensor_copy(alc[:, h], bank[2 + h // 2][:, c0:c0 + TILES].rearrange("p (b q) -> p b q", b=2)))
            for s in range(UNROLL):
                link(V.memset(dl4_r[s].rearrange("p (t c) -> p t c", c=ROW)[:, :, D:ROW], 0.0))
            stage_end(dve, 4)

            def front(G):
                if G.from_(2):
                    dve.wait_ge(GATSUM["sums"], G.g - 1)
                c = cols4(al, G, 16)
                done(V.tensor_tensor(h_r[G.slot].rearrange("p (a c) -> p a c", c=C),
                                     cols4(big, G, 512).rearrange("p (a c) -> p a c", c=C), wide(c, C), ALU.mult))
                matrices(G, GATSUM, "dst", "GATSUM")

            def leaky(G):
                dve.wait_ge(GATSUM["biased"], G.g + 1)
                if G.from_(2):
                    dve.wait_ge(GATSUM["delta"], G.g - 1)
                V.scalar_tensor_tensor(z_r[G.slot], t1_r[G.slot], 0.01, t1_r[G.slot], ALU.mult, ALU.max
                                       ).then_inc(GATSUM["z"], 1)

            def body(G):
                front(G)
                if G.from_(2):
                    leaky(G.before(2))
                if G.from_(1):
                    chain(G.before(), GATSUM, [bank[1 - G.slot]], uT_r, "biased")
            for_groups(dve, body, order)
            leaky(group(NG - 2))
            chain(group(NG - 1), GATSUM, [bank[0]], uT_r, "biased")
            leaky(group(NG - 1))
            dve.wait_ge(GATSUM["z"], NG)
            V.tensor_scalar(wt_col[:, :], s4[:, :, 3], 1.0, None, ALU.max).then_inc(roots, 1)
            dve.wait_ge(roots, 4)
            link(V.reciprocal(wt_col[:, :], wt_col[:, :]))
            link(V.tensor_scalar(hsc_col[:, :], key_col["dst"][:, :], float(M), None, ALU.is_lt))
            link(V.tensor_tensor(wt_col[:, :], wt_col[:, :], hsc_col[:, :], ALU.mult))
            link(V.tensor_scalar(hsc_col[:, :], cnt_col[:, :], 1.0, None, ALU.max))
            link(V.reciprocal(hsc_col[:, :], hsc_col[:, :]))
            link(V.tensor_tensor(hsc_col[:, :], hsc_col[:, :], d4[:, :, 2], ALU.mult))
            link(V.tensor_tensor(rec3[:, :, R_A4:R_A4 + 4], rec3[:, :, R_A4:R_A4 + 4], wide(s4[:, :, 0], 4), ALU.mult))
            stage_end(dve, 5)

            def body(G):
                last_one = isinstance(G.g, int) and G.g == NG
                before = G.before()
                if not last_one:
                    rows_in.wait(dve, "HYP", G)
                    if G.from_(2):
                        dve.wait_ge(HYP["sums"], G.g - 1)
                    r = rows_r[G.place].rearrange("p (t c) -> p t c", c=ROW)
                    V.tensor_tensor(t4(v_r[G.slot]), r[:, :, 0:D], over(wts["K2"][:, :], GROUP), ALU.subtract
                                    ).then_inc(HYP["taken"], 1)
                    if G.from_(2):
                        dve.wait_ge(HYP["chained"], G.g - 1)
                    here = going_on(G, "HYP")
                    dve.wait_ge(HYP["taken"], G.g + 1)
                    s = small[G.slot]
                    for t in range(GROUP):
                        done(V.bn_stats(s[:, 16 + 6 * t:22 + 6 * t], v_r[G.slot][:, t * P:(t + 1) * P]))
                    at_ = order.off
                    V.tensor_tensor(t4(sel_r[G.slot]), here, wide(cols4(key_col["clip"], G)), ALU.is_equal
                                    ).then_inc(HYP["sel"], 1)
                    need(at_)
                    variances(G, HYP, GROUP)
                if G.from_(1):
                    dve.wait_ge(HYP["sums"], G.g)
                    if G.from_(3):
                        dve.wait_ge(HYP["he"], G.g - 2)
                    a0 = done(carry_on(before, [bank[before.slot]], uT_r, 0, 0))
                if not last_one:
                    dve.wait_ge(HYP["dev"], G.g + 1)
                    at_ = done(V.reciprocal(s[:, 0:GROUP], s[:, 104:104 + GROUP]))
                if G.from_(1):
                    need(a0)
                    a1 = done(carry_on(before, [bank[before.slot]], uT_r, 1, 0))
                if not last_one:
                    need(at_)
                    at_ = done(V.tensor_tensor(s[:, 0:GROUP], s[:, 0:GROUP], cols4(wt_col, G), ALU.mult))
                if G.from_(1):
                    need(a1)
                    a2 = done(carry_on(before, [bank[before.slot]], uT_r, 2, 0))
                if not last_one:
                    need(at_)
                    V.scalar_tensor_tensor(s[:, 8:8 + GROUP], s[:, 80:80 + 2 * GROUP:2], -1.0, s[:, 0:GROUP],
                                           ALU.mult, ALU.mult).then_inc(HYP["norm"], 1)
                if G.from_(1):
                    need(a2)
                    carry_on(before, [bank[before.slot]], uT_r, 3, 0).then_inc(HYP["chained"], 1)
            for_groups(dve, body, order)
            dve.wait_ge(HYP["chained"], NG - 1)
            body(group(NG))
            stage_end(dve, 6)
            for s in range(UNROLL):
                link(V.memset(dl4h_r[s].rearrange("p (t c) -> p t c", c=ROW)[:, :, D:ROW], 0.0))

            def widen(G):
                dve.wait_ge(HYPSUM["ws"], G.g + 1)
                if G.from_(2):
                    w_stored.wait(dve, "HYPSUM", G.before(2))
                w = t4(t1_r[G.slot]).rearrange("p t (k c) -> p t k c", c=MUL)
                to = wide_r[G.slot].rearrange("p (t k c) -> p t k c", t=GROUP, c=MUL)
                y = cols4(rec, G, GROUP * REC).rearrange("p (t c) -> p t c", c=REC)

                def times(k_to, n, w_, y_):
                    return V.tensor_tensor(to[:, :, k_to:k_to + n, :], w_.broadcast_to([P, GROUP, n, MUL]),
                                           y[:, :, R_A4 + y_:R_A4 + y_ + n].unsqueeze(3).broadcast_to([P, GROUP, n, MUL]),
                                           ALU.mult)
                done(times(0, 1, w[:, :, 0:1, :], 0))
                done(times(1, 3, w[:, :, 1:2, :], 1))
                done(times(4, 1, w[:, :, 2:3, :], 0))
                times(5, 3, w[:, :, 3:4, :], 1).then_inc(HYPSUM["wide"], 1)

            def body(G):
                if G.from_(2):
                    dve.wait_ge(HYPSUM["sums"], G.g - 1)
                matrices(G, HYPSUM, "src", "HYPSUM")
                if G.from_(1):
                    chain(G.before(), HYPSUM, [bank[1 - G.slot]], uT_r, "delta")
                    widen(G.before())
            for_groups(dve, body, order)
            chain(group(NG - 1), HYPSUM, [bank[0]], uT_r, "delta")
            widen(group(NG - 1))
            stage_end(dve, 7)
            link(V.memset(big[:, :].rearrange("p (t c) -> p t c", c=ROW)[:, :, D:ROW], 0.0))

            def front(G):
                big_in.wait(dve, "TP", G)
                if G.from_(2):
                    dve.wait_ge(TP["h"], G.g - 1)
                statistics(G, TP, lambda t: cols4(big, G, GROUP * ROW)[:, t * ROW:t * ROW + D], GROUP)
                scales(G, TP, GROUP)

            def features(G):
                dve.wait_ge(TP["e"], G.g + 1)
                w_in.wait(dve, "TP", G)
                e_ = t4(bank[1 + G.slot][:, :])
                ev = e_[:, :, 32:128].rearrange("p t (i c) -> p t i c", c=MUL)
                w = w_r[G.slot].rearrange("p (t k c) -> p t k c", t=GROUP, c=MUL)
                f = feat_r[G.slot].rearrange("p (t k c) -> p t k c", t=GROUP, c=MUL)
                tv = t_t.rearrange("p (t i c) -> p t i c", t=GROUP, i=3)
                done(V.tensor_tensor(tv, ev, w[:, :, 5:8, :], ALU.mult))
                at_ = order.off
                done(V.tensor_tensor(f[:, :, 5:8, :], ev, w[:, :, 4:5, :].broadcast_to([P, GROUP, 3, MUL]), ALU.mult))
                need(at_)
                done(V.tensor_reduce(f[:, :, 4, :], tv.rearrange("p t i c -> p t c i"), AX.X, ALU.add))
                V.tensor_tensor(f[:, :, 0:4, :], e_[:, :, 0:32].unsqueeze(2).broadcast_to([P, GROUP, 4, MUL]),
                                w[:, :, 0:4, :], ALU.mult).then_inc(TP["feat"], 1)

            def chain2(G):
                chain(G, TP, [bank[3 + 2 * G.slot], bank[4 + 2 * G.slot]], uT2_r, "delta")

            def body(G):
                front(G)
                if G.from_(1):
                    features(G.before())
                if G.from_(2):
                    chain2(G.before(2))
                matrices(G, TP, "dst", "TP")
            for_groups(dve, body, order)
            features(group(NG - 1))
            chain2(group(NG - 2))
            chain2(group(NG - 1))
            stage_end(dve, 8)


N_WEIGHTS = 12 + 2 * H + 1 + 3 + 2 * 4

_INS = ["x", "src", "dst", "edge_attr_4", "edge_attr_8", "edge_weight", "node_vec1", "node_vec1_n2",
        "L0_gnn_weight", "L0_gnn_bias", "L1_gnn_W1", "L1_gnn_b1", "L1_gnn_Wg", "L1_gnn_att_src",
        "L1_gnn_att_dst", "L1_gnn_bias_g", "L1_gnn_W2", "L1_gnn_b2", "L2_gnn_hyperedge_weight",
        "L2_gnn_W", "L2_gnn_b", "L3_gnn_w1_s", "L3_gnn_w1_v", "L3_gnn_Wfc1", "L3_gnn_Wfc2",
        "L3_gnn_w2_s", "L3_gnn_w2_v"]


def kernel(**inputs):
    import numpy as _np
    import concourse.bacc as _bacc
    from concourse import mybir as _mybir
    from concourse.bass_utils import run_bass_kernel_spmd as _run

    nc = _bacc.Bacc("TRN2", target_bir_lowering=False, num_devices=1)
    arrays, args = {}, []
    for name in _INS:
        a = _np.ascontiguousarray(inputs[name])
        arrays[f"in_{name}_dram"] = a
        args.append(nc.dram_tensor(f"in_{name}_dram", a.shape, _mybir.dt.from_np(a.dtype), kind="ExternalInput").ap())
    args.append(nc.dram_tensor("out_0_dram", (TABLE, ROW), _mybir.dt.float32, kind="ExternalOutput").ap())
    build_gnn(nc, *args)
    r = _run(nc, [arrays], core_ids=[0])
    return _np.ascontiguousarray(r.results[0]["out_0_dram"][:N, :D])
```
